# Optimizing a Trainium2 kernel written in Bass

```python
import numpy as np
import jax
import jax.numpy as jnp

def _softmax(x, axis=-1):
    return jax.nn.softmax(x, axis=axis)

def _gelu(x):
    return jax.nn.gelu(x, approximate=True)

def _silu(x):
    return jax.nn.silu(x)

def _sigmoid(x):
    return jax.nn.sigmoid(x)

def _layernorm(x, axis=-1, eps=1e-05):
    m = jnp.mean(x, axis=axis, keepdims=True)
    v = jnp.var(x, axis=axis, keepdims=True)
    return (x - m) / jnp.sqrt(v + eps)

def _scatter_add(tgt, idx, src, axis=0):
    return tgt.at[idx].add(src)

def _segment_sum(src, seg, n):
    return jax.ops.segment_sum(src, seg, n)
kernel_name = 'mk_hybrid_d2_jaxref_r8_38f5f3'

def setup_inputs(seed: int=0):
    np.random.seed(seed)
    _w = jnp.asarray

    def _L0_attn_a_setup():
        import math
        import jax, jax.numpy as jnp
        import numpy as np
        B, C, D = (4, 256, 128)
        DQ = DV = 64
        H = 16
        key = jax.random.key(seed)
        kx, kq, kk, kv, kw = jax.random.split(key, 5)
        x = jax.random.normal(kx, (B, C, D), dtype=jnp.float32)
        Q = jax.random.normal(kq, (DQ, D, H), dtype=jnp.float32) / math.sqrt(D)
        K = jax.random.normal(kk, (DQ, D, H), dtype=jnp.float32) / math.sqrt(D)
        V = jax.random.normal(kv, (DV, D, H), dtype=jnp.float32) / math.sqrt(D)
        W = jax.random.normal(kw, (D, DV, H), dtype=jnp.float32) / math.sqrt(DV)
        return {'x': x, 'Q': Q, 'K': K, 'V': V, 'W': W}
    _L0_attn_a_in = _L0_attn_a_setup()

    def _L0_attn_b_setup():
        import jax, jax.numpy as jnp
        import numpy as np
        EPS = 0.0001

        def mp_normalize(x, axis):
            red = int(np.prod([x.shape[a] for a in axis])) if isinstance(axis, (list, tuple)) else x.shape[axis]
            w = jnp.sqrt(jnp.sum(jnp.square(x.astype(jnp.float32)), axis=axis, keepdims=True))
            w = EPS + w / np.sqrt(red)
            return x / w.astype(x.dtype)

        def mp_linear(x, w, gain):
            fan_in = w.shape[1]
            wn = mp_normalize(w.astype(jnp.float32), axis=(1,)) * (gain / np.sqrt(fan_in))
            return jnp.einsum('bse,oe->bso', x, wn.astype(x.dtype))

        def attention(query, gain, w_q, w_k, w_v, w_o, num_heads=16, attn_balance=0.5):
            B, S, E = query.shape
            hd = E // num_heads
            res = query
            q = mp_linear(query, w_q, gain).reshape(B, S, num_heads, hd).transpose(0, 2, 1, 3)
            k = mp_linear(query, w_k, gain).reshape(B, S, num_heads, hd).transpose(0, 2, 1, 3)
            v = mp_linear(query, w_v, gain).reshape(B, S, num_heads, hd).transpose(0, 2, 1, 3)
            q = mp_normalize(q, axis=(3,))
            k = mp_normalize(k, axis=(3,))
            scores = jnp.einsum('bnsh,bnsk->bnhk', q, k / np.sqrt(S))
            attn = jax.nn.softmax(scores, axis=3)
            o = jnp.einsum('bnhk,bnsk->bnsh', attn, v)
            o = o.transpose(0, 2, 1, 3).reshape(B, S, E)
            out = mp_linear(o, w_o, gain)
            t = attn_balance
            return (res * (1.0 - t) + out * t) / np.sqrt((1 - t) ** 2 + t ** 2)
        key = jax.random.key(seed)
        ks = jax.random.split(key, 5)
        B, S, E = (4, 512, 128)
        return {'query': jax.random.normal(ks[0], (B, S, E), dtype=jnp.float32), 'gain': jnp.float32(1.0), 'w_q': jax.random.normal(ks[1], (E, E), dtype=jnp.float32), 'w_k': jax.random.normal(ks[2], (E, E), dtype=jnp.float32), 'w_v': jax.random.normal(ks[3], (E, E), dtype=jnp.float32), 'w_o': jax.random.normal(ks[4], (E, E), dtype=jnp.float32)}
    _L0_attn_b_in = _L0_attn_b_setup()

    def _L0_ffn_setup():
        import jax, jax.numpy as jnp
        import numpy as np
        DIM = 128
        DEPTH = 6
        HEADS = 16
        DIM_HEAD = 64
        WINDOW = 32
        INNER = HEADS * DIM_HEAD
        DIM_INNER = int(DIM * 4 * 2 / 3)
        QK_SCALE = 8.0

        def shift_tokens(t):
            a, s = jnp.split(t, 2, -1)
            s = jnp.pad(s, ((0, 0), (1, 0), (0, 0)))[:, :-1]
            return jnp.concatenate([a, s], -1)

        def l2norm(t):
            return t / jnp.maximum(jnp.linalg.norm(t, axis=-1, keepdims=True), 1e-12)

        def rotate_half(x):
            x1, x2 = jnp.split(x, 2, -1)
            return jnp.concatenate([-x2, x1], -1)

        def rotary_tables(n):
            half = jnp.arange(0, DIM_HEAD, 2, dtype=jnp.float32)
            inv_freq = 1.0 / 10000.0 ** (half / DIM_HEAD)
            t = jnp.arange(n, dtype=jnp.float32)
            freqs = t[:, None] * inv_freq[None, :]
            freqs = jnp.concatenate([freqs, freqs], -1)
            base_scale = (half + 0.4 * DIM_HEAD) / (1.4 * DIM_HEAD)
            power = (t - n // 2) / (WINDOW // 2)
            scale = base_scale[None, :] ** power[:, None]
            scale = jnp.concatenate([scale, scale], -1)
            return (freqs, scale)

        def local_attention(q, k, v):
            b, h, n, d = q.shape
            w = WINDOW
            nw = n // w
            bq = q.reshape(b, h, nw, w, d)
            bk = k.reshape(b, h, nw, w, d)
            bv = v.reshape(b, h, nw, w, d)

            def look(t):
                p = jnp.pad(t, ((0, 0), (0, 0), (1, 0), (0, 0), (0, 0)))
                return jnp.concatenate([p[:, :, :nw], p[:, :, 1:]], axis=3)
            bk2, bv2 = (look(bk), look(bv))
            seq = jnp.arange(n).reshape(nw, w)
            seq_p = jnp.pad(seq, ((1, 0), (0, 0)), constant_values=-1)
            jt = jnp.concatenate([seq_p[:nw], seq_p[1:]], axis=1)
            it = seq[:, :, None]
            jb = jt[:, None, :]
            mask = (it < jb) | (it > jb + w) | (jb == -1)
            sim = jnp.einsum('bhwie,bhwje->bhwij', bq, bk2) * QK_SCALE
            sim = jnp.where(mask, -jnp.finfo(sim.dtype).max, sim)
            attn = jax.nn.softmax(sim, -1)
            out = jnp.einsum('bhwij,bhwje->bhwie', attn, bv2)
            return out.reshape(b, h, n, d)

        def attn_layer(x, Wqkv, qs, ksc, Wo):
            b, n, _ = x.shape
            qkv = x @ Wqkv
            q, k, v = jnp.split(qkv, 3, -1)
            sh = lambda t: t.reshape(b, n, HEADS, DIM_HEAD).transpose(0, 2, 1, 3)
            q, k, v = (sh(q), sh(k), sh(v))
            q = l2norm(q) * qs
            k = l2norm(k) * ksc
            freqs, scale = rotary_tables(n)
            cos, sin = (jnp.cos(freqs), jnp.sin(freqs))
            q = q * cos * scale + rotate_half(q) * sin * scale
            inv = 1.0 / scale
            k = k * cos * inv + rotate_half(k) * sin * inv
            out = local_attention(q, k, v)
            out = out.transpose(0, 2, 1, 3).reshape(b, n, INNER)
            return out @ Wo

        def ffn_layer(x, g, bln, W1, b1, W2, b2):
            mu = x.mean(-1, keepdims=True)
            var = ((x - mu) ** 2).mean(-1, keepdims=True)
            xn = (x - mu) / jnp.sqrt(var + 1e-05) * g + bln
            hg = xn @ W1 + b1
            a, gate = jnp.split(hg, 2, -1)
            return a * jax.nn.gelu(gate, approximate=False) @ W2 + b2
        key = jax.random.key(seed)
        ks = jax.random.split(key, 8)
        B, N = (2, 256)
        init = lambda k, shape: jax.random.normal(k, shape, jnp.float32) * 0.02
        return {'x': jax.random.normal(ks[0], (B, N, DIM), jnp.float32), 'Wqkv': init(ks[1], (DEPTH, DIM, 3 * INNER)), 'q_scale': jnp.ones((DEPTH, DIM_HEAD), jnp.float32), 'k_scale': jnp.ones((DEPTH, DIM_HEAD), jnp.float32), 'Wo': init(ks[2], (DEPTH, INNER, DIM)), 'ln_g': jnp.ones((DEPTH, DIM), jnp.float32), 'ln_b': jnp.zeros((DEPTH, DIM), jnp.float32), 'W1': init(ks[3], (DEPTH, DIM, 2 * DIM_INNER)), 'b1': jnp.zeros((DEPTH, 2 * DIM_INNER), jnp.float32), 'W2': init(ks[4], (DEPTH, DIM_INNER, DIM)), 'b2': jnp.zeros((DEPTH, DIM), jnp.float32)}
    _L0_ffn_in = _L0_ffn_setup()

    def _L1_attn_a_setup():
        import jax, jax.numpy as jnp
        import numpy as np
        H = 16
        W = 64
        NEG = -1000000000.0

        def _neighborhood(t, nb):
            tp = jnp.pad(t, ((0, 0), (W, W), (0, 0), (0, 0)))
            idx = jnp.arange(nb)[:, None] * W + jnp.arange(3 * W)[None, :]
            return tp[:, idx]
        key = jax.random.key(seed)
        k0, k1, k2 = jax.random.split(key, 3)
        B, N, C = (2, 512, 128)
        x = jax.random.normal(k0, (B, N, C), dtype=jnp.float32)
        w_qkv = jax.random.normal(k1, (C, 3 * C), dtype=jnp.float32) * 0.02
        w_out = jax.random.normal(k2, (C, C), dtype=jnp.float32) * 0.02
        b_out = jnp.zeros((C,), dtype=jnp.float32)
        return {'x': x, 'w_qkv': w_qkv, 'w_out': w_out, 'b_out': b_out}
    _L1_attn_a_in = _L1_attn_a_setup()

    def _L1_attn_b_setup():
        import jax, jax.numpy as jnp
        import numpy as np
        T, B, H = (128, 32, 128)
        key = jax.random.key(seed)
        k1, k2, k3, k4 = jax.random.split(key, 4)
        s = 1.0 / np.sqrt(H)
        return {'inputs': jax.random.normal(k1, (T, B, H), dtype=jnp.float32), 'W': jax.random.normal(k2, (H, H), dtype=jnp.float32) * s, 'proj': jax.random.normal(k3, (H,), dtype=jnp.float32) * s, 'concat_w': jax.random.normal(k4, (H, 2 * H), dtype=jnp.float32) * s, 'concat_b': jnp.zeros((H,), dtype=jnp.float32)}
    _L1_attn_b_in = _L1_attn_b_setup()

    def _L1_ffn_setup():
        import jax, jax.numpy as jnp
        import numpy as np
        B, S, H = (2, 128, 128)
        E, F = (16, 64)
        G, TOPK_G, TOPK = (4, 2, 4)
        N_SHARED = 2
        ROUTE_SCALE = 1.0
        FS = N_SHARED * F

        def _gate(x, w_gate):
            T = x.shape[0]
            scores = jax.nn.sigmoid(x @ w_gate.T)
            sv = scores.reshape(T, G, E // G)
            group_scores = jax.lax.top_k(sv, 2)[0].sum(-1)
            top_groups = jax.lax.top_k(group_scores, TOPK_G)[1]
            allowed = jnp.zeros((T, G), dtype=bool).at[jnp.arange(T)[:, None], top_groups].set(True)
            masked = jnp.where(allowed[:, :, None], sv, -jnp.inf).reshape(T, E)
            _, idx = jax.lax.top_k(masked, TOPK)
            w = jnp.take_along_axis(scores, idx, axis=1)
            w = w / (w.sum(-1, keepdims=True) + 1e-06) * ROUTE_SCALE
            return (w, idx)

        def _swiglu(x, w1, w3, w2):
            return jax.nn.silu(x @ w1.T) * (x @ w3.T) @ w2.T
        key = jax.random.key(seed)
        ks = jax.random.split(key, 8)
        scale = 0.02
        return {'hidden_states': jax.random.normal(ks[0], (B, S, H), dtype=jnp.float32), 'w_gate': jax.random.normal(ks[1], (E, H), dtype=jnp.float32) * scale, 'w1_e': jax.random.normal(ks[2], (E, F, H), dtype=jnp.float32) * scale, 'w3_e': jax.random.normal(ks[3], (E, F, H), dtype=jnp.float32) * scale, 'w2_e': jax.random.normal(ks[4], (E, H, F), dtype=jnp.float32) * scale, 'w1_s': jax.random.normal(ks[5], (FS, H), dtype=jnp.float32) * scale, 'w3_s': jax.random.normal(ks[6], (FS, H), dtype=jnp.float32) * scale, 'w2_s': jax.random.normal(ks[7], (H, FS), dtype=jnp.float32) * scale}
    _L1_ffn_in = _L1_ffn_setup()
    _d = {'L0_attn_a_x': _L0_attn_a_in['x'], 'L0_attn_a_Q': _L0_attn_a_in['Q'], 'L0_attn_a_K': _L0_attn_a_in['K'], 'L0_attn_a_V': _L0_attn_a_in['V'], 'L0_attn_a_W': _L0_attn_a_in['W'], 'L0_attn_b_gain': _L0_attn_b_in['gain'], 'L0_attn_b_w_q': _L0_attn_b_in['w_q'], 'L0_attn_b_w_k': _L0_attn_b_in['w_k'], 'L0_attn_b_w_v': _L0_attn_b_in['w_v'], 'L0_attn_b_w_o': _L0_attn_b_in['w_o'], 'L0_ffn_Wqkv': _L0_ffn_in['Wqkv'], 'L0_ffn_q_scale': _L0_ffn_in['q_scale'], 'L0_ffn_k_scale': _L0_ffn_in['k_scale'], 'L0_ffn_Wo': _L0_ffn_in['Wo'], 'L0_ffn_ln_g': _L0_ffn_in['ln_g'], 'L0_ffn_ln_b': _L0_ffn_in['ln_b'], 'L0_ffn_W1': _L0_ffn_in['W1'], 'L0_ffn_b1': _L0_ffn_in['b1'], 'L0_ffn_W2': _L0_ffn_in['W2'], 'L0_ffn_b2': _L0_ffn_in['b2'], 'L1_attn_a_w_qkv': _L1_attn_a_in['w_qkv'], 'L1_attn_a_w_out': _L1_attn_a_in['w_out'], 'L1_attn_a_b_out': _L1_attn_a_in['b_out'], 'L1_attn_b_W': _L1_attn_b_in['W'], 'L1_attn_b_proj': _L1_attn_b_in['proj'], 'L1_attn_b_concat_w': _L1_attn_b_in['concat_w'], 'L1_attn_b_concat_b': _L1_attn_b_in['concat_b'], 'L1_ffn_w_gate': _L1_ffn_in['w_gate'], 'L1_ffn_w1_e': _L1_ffn_in['w1_e'], 'L1_ffn_w3_e': _L1_ffn_in['w3_e'], 'L1_ffn_w2_e': _L1_ffn_in['w2_e'], 'L1_ffn_w1_s': _L1_ffn_in['w1_s'], 'L1_ffn_w3_s': _L1_ffn_in['w3_s'], 'L1_ffn_w2_s': _L1_ffn_in['w2_s']}
    _x0 = _d['L0_attn_a_x']
    _d['L0_attn_a_x'] = jax.random.normal(jax.random.fold_in(jax.random.key(seed), 1), (4, 512, 128), dtype=_x0.dtype)
    del _x0
    return _d

def reference(L0_attn_a_x, L0_attn_a_Q, L0_attn_a_K, L0_attn_a_V, L0_attn_a_W, L0_attn_b_gain, L0_attn_b_w_q, L0_attn_b_w_k, L0_attn_b_w_v, L0_attn_b_w_o, L0_ffn_Wqkv, L0_ffn_q_scale, L0_ffn_k_scale, L0_ffn_Wo, L0_ffn_ln_g, L0_ffn_ln_b, L0_ffn_W1, L0_ffn_b1, L0_ffn_W2, L0_ffn_b2, L1_attn_a_w_qkv, L1_attn_a_w_out, L1_attn_a_b_out, L1_attn_b_W, L1_attn_b_proj, L1_attn_b_concat_w, L1_attn_b_concat_b, L1_ffn_w_gate, L1_ffn_w1_e, L1_ffn_w3_e, L1_ffn_w2_e, L1_ffn_w1_s, L1_ffn_w3_s, L1_ffn_w2_s):

    def _L0_attn_a_ref(x, Q, K, V, W):
        import math
        import jax, jax.numpy as jnp
        import numpy as np
        B, C, D = (4, 256, 128)
        DQ = DV = 64
        H = 16
        d_query, d_embed, num_heads = Q.shape
        d_value = V.shape[0]
        sq = math.sqrt(d_query / d_embed)
        sv = math.sqrt(d_value / d_embed)
        q = jnp.einsum('qdh,bcd->bhcq', Q, x) * sq
        k = jnp.einsum('qdh,bcd->bhcq', K, x) * sq
        v = jnp.einsum('vdh,bcd->bhcv', V, x) * sv
        att = jnp.einsum('bhcq,bhCq->bhcC', q, k) / d_query
        T = x.shape[1]
        causal = jnp.arange(T)[:, None] >= jnp.arange(T)[None, :]
        att = jnp.where(causal, att, -jnp.inf)
        p = jax.nn.softmax(att, axis=-1)
        y = jnp.einsum('bhcC,bhCv->bhcv', p, v)
        z = jnp.einsum('dvh,bhcv->bcd', W, y) * (math.sqrt(d_embed / d_value) / num_heads)
        return z

    def _L0_attn_b_ref(query, gain, w_q, w_k, w_v, w_o):
        import jax, jax.numpy as jnp
        import numpy as np
        EPS = 0.0001

        def mp_normalize(x, axis):
            red = int(np.prod([x.shape[a] for a in axis])) if isinstance(axis, (list, tuple)) else x.shape[axis]
            w = jnp.sqrt(jnp.sum(jnp.square(x.astype(jnp.float32)), axis=axis, keepdims=True))
            w = EPS + w / np.sqrt(red)
            return x / w.astype(x.dtype)

        def mp_linear(x, w, gain):
            fan_in = w.shape[1]
            wn = mp_normalize(w.astype(jnp.float32), axis=(1,)) * (gain / np.sqrt(fan_in))
            return jnp.einsum('bse,oe->bso', x, wn.astype(x.dtype))

        def attention(query, gain, w_q, w_k, w_v, w_o, num_heads=16, attn_balance=0.5):
            B, S, E = query.shape
            hd = E // num_heads
            res = query
            q = mp_linear(query, w_q, gain).reshape(B, S, num_heads, hd).transpose(0, 2, 1, 3)
            k = mp_linear(query, w_k, gain).reshape(B, S, num_heads, hd).transpose(0, 2, 1, 3)
            v = mp_linear(query, w_v, gain).reshape(B, S, num_heads, hd).transpose(0, 2, 1, 3)
            q = mp_normalize(q, axis=(3,))
            k = mp_normalize(k, axis=(3,))
            scores = jnp.einsum('bnsh,bnsk->bnhk', q, k / np.sqrt(S))
            attn = jax.nn.softmax(scores, axis=3)
            o = jnp.einsum('bnhk,bnsk->bnsh', attn, v)
            o = o.transpose(0, 2, 1, 3).reshape(B, S, E)
            out = mp_linear(o, w_o, gain)
            t = attn_balance
            return (res * (1.0 - t) + out * t) / np.sqrt((1 - t) ** 2 + t ** 2)
        return attention(query, gain, w_q, w_k, w_v, w_o)

    def _L0_ffn_ref(x, Wqkv, q_scale, k_scale, Wo, ln_g, ln_b, W1, b1, W2, b2):
        import jax, jax.numpy as jnp
        import numpy as np
        DIM = 128
        DEPTH = 6
        HEADS = 16
        DIM_HEAD = 64
        WINDOW = 32
        INNER = HEADS * DIM_HEAD
        DIM_INNER = int(DIM * 4 * 2 / 3)
        QK_SCALE = 8.0

        def shift_tokens(t):
            a, s = jnp.split(t, 2, -1)
            s = jnp.pad(s, ((0, 0), (1, 0), (0, 0)))[:, :-1]
            return jnp.concatenate([a, s], -1)

        def l2norm(t):
            return t / jnp.maximum(jnp.linalg.norm(t, axis=-1, keepdims=True), 1e-12)

        def rotate_half(x):
            x1, x2 = jnp.split(x, 2, -1)
            return jnp.concatenate([-x2, x1], -1)

        def rotary_tables(n):
            half = jnp.arange(0, DIM_HEAD, 2, dtype=jnp.float32)
            inv_freq = 1.0 / 10000.0 ** (half / DIM_HEAD)
            t = jnp.arange(n, dtype=jnp.float32)
            freqs = t[:, None] * inv_freq[None, :]
            freqs = jnp.concatenate([freqs, freqs], -1)
            base_scale = (half + 0.4 * DIM_HEAD) / (1.4 * DIM_HEAD)
            power = (t - n // 2) / (WINDOW // 2)
            scale = base_scale[None, :] ** power[:, None]
            scale = jnp.concatenate([scale, scale], -1)
            return (freqs, scale)

        def local_attention(q, k, v):
            b, h, n, d = q.shape
            w = WINDOW
            nw = n // w
            bq = q.reshape(b, h, nw, w, d)
            bk = k.reshape(b, h, nw, w, d)
            bv = v.reshape(b, h, nw, w, d)

            def look(t):
                p = jnp.pad(t, ((0, 0), (0, 0), (1, 0), (0, 0), (0, 0)))
                return jnp.concatenate([p[:, :, :nw], p[:, :, 1:]], axis=3)
            bk2, bv2 = (look(bk), look(bv))
            seq = jnp.arange(n).reshape(nw, w)
            seq_p = jnp.pad(seq, ((1, 0), (0, 0)), constant_values=-1)
            jt = jnp.concatenate([seq_p[:nw], seq_p[1:]], axis=1)
            it = seq[:, :, None]
            jb = jt[:, None, :]
            mask = (it < jb) | (it > jb + w) | (jb == -1)
            sim = jnp.einsum('bhwie,bhwje->bhwij', bq, bk2) * QK_SCALE
            sim = jnp.where(mask, -jnp.finfo(sim.dtype).max, sim)
            attn = jax.nn.softmax(sim, -1)
            out = jnp.einsum('bhwij,bhwje->bhwie', attn, bv2)
            return out.reshape(b, h, n, d)

        def attn_layer(x, Wqkv, qs, ksc, Wo):
            b, n, _ = x.shape
            qkv = x @ Wqkv
            q, k, v = jnp.split(qkv, 3, -1)
            sh = lambda t: t.reshape(b, n, HEADS, DIM_HEAD).transpose(0, 2, 1, 3)
            q, k, v = (sh(q), sh(k), sh(v))
            q = l2norm(q) * qs
            k = l2norm(k) * ksc
            freqs, scale = rotary_tables(n)
            cos, sin = (jnp.cos(freqs), jnp.sin(freqs))
            q = q * cos * scale + rotate_half(q) * sin * scale
            inv = 1.0 / scale
            k = k * cos * inv + rotate_half(k) * sin * inv
            out = local_attention(q, k, v)
            out = out.transpose(0, 2, 1, 3).reshape(b, n, INNER)
            return out @ Wo

        def ffn_layer(x, g, bln, W1, b1, W2, b2):
            mu = x.mean(-1, keepdims=True)
            var = ((x - mu) ** 2).mean(-1, keepdims=True)
            xn = (x - mu) / jnp.sqrt(var + 1e-05) * g + bln
            hg = xn @ W1 + b1
            a, gate = jnp.split(hg, 2, -1)
            return a * jax.nn.gelu(gate, approximate=False) @ W2 + b2
        for i in range(DEPTH):
            x = attn_layer(shift_tokens(x), Wqkv[i], q_scale[i], k_scale[i], Wo[i]) + x
            x = ffn_layer(shift_tokens(x), ln_g[i], ln_b[i], W1[i], b1[i], W2[i], b2[i]) + x
        return x

    def _L1_attn_a_ref(x, w_qkv, w_out, b_out):
        import jax, jax.numpy as jnp
        import numpy as np
        H = 16
        W = 64
        NEG = -1000000000.0

        def _neighborhood(t, nb):
            tp = jnp.pad(t, ((0, 0), (W, W), (0, 0), (0, 0)))
            idx = jnp.arange(nb)[:, None] * W + jnp.arange(3 * W)[None, :]
            return tp[:, idx]
        B, N, C = x.shape
        Dh = C // H
        scale = Dh ** (-0.5)
        pad = W // 2
        nb = N // W
        qkv = (x @ w_qkv).reshape(B, N, 3, H, Dh)
        q, k, v = (qkv[:, :, 0], qkv[:, :, 1], qkv[:, :, 2])
        qb = q.reshape(B, nb, W, H, Dh)
        kn = _neighborhood(k, nb)
        vn = _neighborhood(v, nb)
        logits = jnp.einsum('bnqhd,bnkhd->bhnqk', qb, kn) * scale
        q_idx = jnp.arange(W)[:, None]
        k_idx = jnp.arange(3 * W)[None, :]
        rel = k_idx - W - q_idx
        win = (rel >= -pad) & (rel <= pad - 1)
        j_abs = jnp.arange(nb)[:, None, None] * W + (k_idx[None] - W)
        valid = win[None] & (j_abs >= 0) & (j_abs < N)
        logits = jnp.where(valid[None, None], logits, NEG)
        attn_local = jax.nn.softmax(logits, axis=-1)
        out_local = jnp.einsum('bhnqk,bnkhd->bnqhd', attn_local, vn).reshape(B, N, H, Dh)
        kg = k[:, ::W]
        vg = v[:, ::W]
        lg = jnp.einsum('bnhd,bghd->bhng', q, kg) * scale
        attn_g = jax.nn.softmax(lg, axis=-1)
        out_global = jnp.einsum('bhng,bghd->bnhd', attn_g, vg)
        out = (out_local + out_global).reshape(B, N, C)
        return out @ w_out + b_out

    def _L1_attn_b_ref(inputs, W, proj, concat_w, concat_b):
        import jax, jax.numpy as jnp
        import numpy as np
        T, B, H = (128, 32, 128)
        T_, B_, H_ = inputs.shape
        hp = jnp.tanh(jnp.einsum('sbh,hk->sbk', inputs, W))
        scores = jnp.einsum('sbk,k->sb', hp, proj)
        t_idx = jnp.arange(T_)
        mask = t_idx[None, :] < t_idx[:, None]
        neg = jnp.finfo(scores.dtype).min
        logits = jnp.where(mask[:, :, None], scores[None, :, :], neg)
        attn = jax.nn.softmax(logits, axis=1)
        context = jnp.einsum('tsb,sbh->tbh', attn, inputs)
        cat = jnp.concatenate([inputs, context], axis=-1)
        out = jnp.tanh(jnp.einsum('tbc,hc->tbh', cat, concat_w) + concat_b)
        out = out.at[:2].set(inputs[:2])
        return out

    def _L1_ffn_ref(hidden_states, w_gate, w1_e, w3_e, w2_e, w1_s, w3_s, w2_s):
        import jax, jax.numpy as jnp
        import numpy as np
        B, S, H = (2, 128, 128)
        E, F = (16, 64)
        G, TOPK_G, TOPK = (4, 2, 4)
        N_SHARED = 2
        ROUTE_SCALE = 1.0
        FS = N_SHARED * F

        def _gate(x, w_gate):
            T = x.shape[0]
            scores = jax.nn.sigmoid(x @ w_gate.T)
            sv = scores.reshape(T, G, E // G)
            group_scores = jax.lax.top_k(sv, 2)[0].sum(-1)
            top_groups = jax.lax.top_k(group_scores, TOPK_G)[1]
            allowed = jnp.zeros((T, G), dtype=bool).at[jnp.arange(T)[:, None], top_groups].set(True)
            masked = jnp.where(allowed[:, :, None], sv, -jnp.inf).reshape(T, E)
            _, idx = jax.lax.top_k(masked, TOPK)
            w = jnp.take_along_axis(scores, idx, axis=1)
            w = w / (w.sum(-1, keepdims=True) + 1e-06) * ROUTE_SCALE
            return (w, idx)

        def _swiglu(x, w1, w3, w2):
            return jax.nn.silu(x @ w1.T) * (x @ w3.T) @ w2.T
        shape = hidden_states.shape
        x = hidden_states.reshape(-1, H)
        weights, idx = _gate(x, w_gate)
        combine = (jax.nn.one_hot(idx, E, dtype=x.dtype) * weights[..., None]).sum(1)
        g = jax.nn.silu(jnp.einsum('th,efh->tef', x, w1_e))
        u = jnp.einsum('th,efh->tef', x, w3_e)
        routed = jnp.einsum('tef,ehf,te->th', g * u, w2_e, combine)
        shared = _swiglu(x, w1_s, w3_s, w2_s)
        return (routed + shared).reshape(shape)
    x = L0_attn_a_x
    x = x + _L0_attn_a_ref(_layernorm(x, axis=-1), L0_attn_a_Q, L0_attn_a_K, L0_attn_a_V, L0_attn_a_W)
    x = x + _L0_ffn_ref(_layernorm(x, axis=-1), L0_ffn_Wqkv, L0_ffn_q_scale, L0_ffn_k_scale, L0_ffn_Wo, L0_ffn_ln_g, L0_ffn_ln_b, L0_ffn_W1, L0_ffn_b1, L0_ffn_W2, L0_ffn_b2)
    x = x + _L0_attn_b_ref(_layernorm(x, axis=-1), L0_attn_b_gain, L0_attn_b_w_q, L0_attn_b_w_k, L0_attn_b_w_v, L0_attn_b_w_o)
    x = x + _L0_ffn_ref(_layernorm(x, axis=-1), L0_ffn_Wqkv, L0_ffn_q_scale, L0_ffn_k_scale, L0_ffn_Wo, L0_ffn_ln_g, L0_ffn_ln_b, L0_ffn_W1, L0_ffn_b1, L0_ffn_W2, L0_ffn_b2)
    x = x + _L1_attn_a_ref(_layernorm(x, axis=-1), L1_attn_a_w_qkv, L1_attn_a_w_out, L1_attn_a_b_out)
    x = x + _L1_ffn_ref(_layernorm(x, axis=-1), L1_ffn_w_gate, L1_ffn_w1_e, L1_ffn_w3_e, L1_ffn_w2_e, L1_ffn_w1_s, L1_ffn_w3_s, L1_ffn_w2_s)
    x = x + _L1_attn_b_ref(_layernorm(x, axis=-1), L1_attn_b_W, L1_attn_b_proj, L1_attn_b_concat_w, L1_attn_b_concat_b)
    x = x + _L1_ffn_ref(_layernorm(x, axis=-1), L1_ffn_w_gate, L1_ffn_w1_e, L1_ffn_w3_e, L1_ffn_w2_e, L1_ffn_w1_s, L1_ffn_w3_s, L1_ffn_w2_s)
    return x

_drawn_inputs = setup_inputs


def setup_inputs(seed=0):
    import zlib

    import numpy as np

    out = dict(_drawn_inputs(seed))
    spreads = {'L0_ffn_q_scale': (1.0, 0.6),
     'L0_ffn_k_scale': (1.0, 0.6),
     'L0_ffn_ln_g': (1.0, 0.6),
     'L0_ffn_ln_b': (0.0, 0.8),
     'L0_ffn_b1': (0.0, 0.621),
     'L0_ffn_b2': (0.0, 0.1),
     'L1_attn_a_b_out': (0.0, 0.319),
     'L1_attn_b_concat_b': (0.0, 0.775)}
    factors = {'L0_attn_a_Q': 8.0,
     'L0_attn_a_K': 8.0,
     'L1_attn_a_w_qkv': 7.802,
     'L1_attn_a_w_out': 7.34,
     'L1_ffn_w_gate': 8.0,
     'L1_ffn_w1_e': 8.0,
     'L1_ffn_w3_e': 8.0,
     'L1_ffn_w2_e': 8.0,
     'L1_ffn_w1_s': 8.0,
     'L1_ffn_w3_s': 8.0,
     'L1_ffn_w2_s': 8.0,
     'L1_attn_b_W': 3.276,
     'L1_attn_b_proj': 3.048}
    for name, (base, spread) in spreads.items():
        noise = np.random.default_rng([zlib.crc32(name.encode()), seed]).standard_normal(out[name].shape)
        drawn = base * np.exp(spread * noise) if base else spread * noise
        out[name] = jnp.asarray(drawn.astype(out[name].dtype))
    for name, factor in factors.items():
        out[name] = (out[name] * factor).astype(out[name].dtype)
    return out
```

```python
from contextlib import ExitStack

import numpy as np
import concourse.bass as bass
from concourse import mybir

F32 = mybir.dt.float32
BF16 = mybir.dt.bfloat16
ALU = mybir.AluOpType
ACT = mybir.ActivationFunctionType
AX = mybir.AxisListType

P = 128
D = 128
B, S = 4, 512
TPB = S // P
NT = B * TPB
NEG = -1.0e30
LN_EPS = 1e-5


def wait(eng, sem, value):
    if isinstance(value, int) and value <= 0:
        return
    eng.wait_ge(sem, value)


def slot(t):
    return (t // TPB) * (TPB + 1) + t % TPB + 1


class Pool_:

    def __init__(self, nc, ctx, tag):
        self.nc, self.ctx, self.tag = nc, ctx, tag

    def sb(self, name, shape, dt=F32):
        return self.ctx.enter_context(self.nc.sbuf_tensor(f"{self.tag}_{name}", shape, dt))

    def ps(self, name, shape, dt=F32):
        return self.ctx.enter_context(self.nc.psum_tensor(f"{self.tag}_{name}", shape, dt))

    def sem(self, name):
        return self.ctx.enter_context(self.nc.semaphore(f"{self.tag}_{name}"))


def layernorm(nc, tag, src, dst):
    with ExitStack() as ctx:
        new = Pool_(nc, ctx, tag)
        stats = new.sb("stats", [P, NT, 6])
        mean_var = new.sb("mean_var", [P, NT, 2])
        log_var = new.sb("log_var", [P, NT])
        rstd = new.sb("rstd", [P, NT])
        stats_ready, moments_ready, eps_added, rstd_ready, centred, dve_chain = (
            new.sem(n) for n in ("stats", "moments", "eps_added", "rstd_ready", "centred", "chain"))
        block = ctx.enter_context(nc.Block())

        @block.vector
        def _(dve):
            for t in range(NT):
                dve.bn_stats(stats[:, t, :], src[:, slot(t), :]).then_inc(stats_ready, 1)
            for t in range(NT):
                dve.wait_ge(stats_ready, t + 1)
                dve.bn_aggr(mean_var[:, t, :], stats[:, t, :]).then_inc(moments_ready, 1)
            dve.wait_ge(moments_ready, NT)
            dve.tensor_scalar(log_var[:, :], mean_var[:, :, 1], LN_EPS, None, ALU.add).then_inc(eps_added, 1)
            dve.wait_ge(rstd_ready, 2)
            for t in range(NT):
                dve.tensor_scalar(dst[:, slot(t), :], src[:, slot(t), :], mean_var[:, t, 0:1],
                                  rstd[:, t:t + 1], ALU.subtract, ALU.mult).then_inc(centred, 1)

        @block.scalar
        def _(act):
            act.wait_ge(eps_added, 1)
            act.activation(rstd[:, :], log_var[:, :], ACT.Ln).then_inc(rstd_ready, 1)
            act.wait_ge(rstd_ready, 1)
            act.activation(rstd[:, :], rstd[:, :], ACT.Exp, scale=-0.5).then_inc(rstd_ready, 1)


def add_stream(nc, tag, X, Y):
    with ExitStack() as ctx:
        new = Pool_(nc, ctx, tag)
        added = new.sem("added")
        block = ctx.enter_context(nc.Block())

        @block.vector
        def _(dve):
            dve.tensor_tensor(X[:, :, :], X[:, :, :], Y[:, :, :], ALU.add).then_inc(added, 1)


DEPTH, HEADS, DH, WINDOW = 6, 16, 64, 32
INNER = HEADS * DH
FF = int(D * 4 * 2 / 3)
KEYS = WINDOW + P
PAIRS = HEADS // 2
FF_CHUNKS = [(0, 128), (128, 128), (256, FF - 256)]


def rotary_base():
    half = np.arange(0, DH, 2, dtype=np.float32)
    inv_freq = (1.0 / np.float32(10000.0) ** (half / np.float32(DH))).astype(np.float32)
    t = np.arange(S, dtype=np.float32)
    freqs = t[:, None] * inv_freq[None, :]
    freqs = np.concatenate([freqs, freqs], -1).astype(np.float32)
    base = ((half + np.float32(0.4 * DH)) / np.float32(1.4 * DH)).astype(np.float32)
    scale = (base[None, :] ** ((t - S // 2) / (WINDOW // 2))[:, None]).astype(np.float32)
    scale = np.concatenate([scale, scale], -1)
    cos, sin = np.cos(freqs), np.sin(freqs)
    sin = np.concatenate([-sin[:, :DH // 2], sin[:, DH // 2:]], -1)
    tab = np.stack([cos * scale * 8.0, sin * scale * 8.0, cos / scale, sin / scale], 1)
    return np.ascontiguousarray(tab.reshape(TPB, P, 4, DH).transpose(1, 0, 2, 3)).astype(np.float32)


def rotary_tables(nc, tag, table, dram):
    with ExitStack() as ctx:
        new = Pool_(nc, ctx, tag + "_rot")
        base = new.sb("base", [P, TPB, 4, DH])
        scales = new.sb("scales", [P, DEPTH, 4, DH])
        loaded, built = new.sem("loaded"), new.sem("built")
        block = ctx.enter_context(nc.Block())

        @block.sync
        def _(sp):
            sp.dma_start(base[:, :, :, :], dram["rotary"]).then_inc(loaded, 16)
            sp.dma_start(scales[:, :, :, :].rearrange("p l a e -> p (l a e)"),
                         dram["qk_scales"].partition_broadcast(P)).then_inc(loaded, 16)

        @block.vector
        def _(dve):
            dve.wait_ge(loaded, 32)
            for l in range(DEPTH):
                for j in range(TPB):
                    dve.tensor_tensor(table[:, l, j, :, :], base[:, j, :, :], scales[:, l, :, :],
                                      ALU.mult).then_inc(built, 1)


def ffn_stack(nc, tag, X1, Y, ident, identb, dram):
    STEPS = DEPTH * NT
    with ExitStack() as ctx:
        new = Pool_(nc, ctx, tag)
        w_qkv = new.sb("w_qkv", [P, 2, 3 * INNER])
        w_o = new.sb("w_o", [P, 2, PAIRS, D])
        w_1 = new.sb("w_1", [P, 2, 2 * FF])
        w_2 = new.sb("w_2", [P, 2, 3, D])
        b_1 = new.sb("b_1", [P, 2, 2 * FF])
        b_2 = new.sb("b_2", [P, 2, D])
        ln_gb = new.sb("ln_gb", [P, DEPTH, 2])
        table = new.sb("table", [P, DEPTH, TPB, 4, DH])
        mask = new.sb("mask", [P, 2, KEYS], BF16)
        shift = new.sb("shift", [P, P])
        carry = new.sb("carry", [P, P])

        xs = new.sb("xs", [P, 2, D])
        xsT = new.sb("xsT", [P, 2, P])
        squares = new.sb("squares", [P, 2, 512])
        cos_part = new.sb("cos_part", [P, 2, 512])
        sin_part = new.sb("sin_part", [P, 2, 512])
        qk = new.sb("qk", [P, 4, 512])
        sum_sq = new.sb("sum_sq", [P, 2 * HEADS])
        norms = new.sb("norms", [P, 2 * HEADS])
        qT = new.sb("qT", [P, 2, 2, PAIRS, P])
        kT = new.sb("kT", [P, 2, PAIRS, KEYS])
        v = new.sb("v", [P, 2, INNER])
        v_before = new.sb("v_before", [WINDOW, 2, INNER])

        neg_max = new.sb("neg_max", [P, 2, 2])
        row_sum = new.sb("row_sum", [P, 2, 2])
        inv_sum = new.sb("inv_sum", [P, 2, 2])
        probs = new.sb("probs", [P, 2, 2, KEYS])
        probsT = new.sb("probsT", [P, 2, 2 * P + 2 * WINDOW])
        oT = new.sb("oT", [P, PAIRS, P])

        xm = new.sb("xm", [P, D])
        ln_stats = new.sb("ln_stats", [P, 6])
        ln_mv = new.sb("ln_mv", [P, 2])
        ln_var = new.sb("ln_var", [P, 1])
        ln_rstd = new.sb("ln_rstd", [P, 1])
        zeros = new.sb("zeros", [P, 1])
        held = new.sb("held", [1, 1])
        xhat = new.sb("xhat", [P, D])
        xnT = new.sb("xnT", [P, P])
        up = new.sb("up", [P, 2, FF])
        gate = new.sb("gate", [P, FF])
        hT = new.sb("hT", [P, 3, P])
        x1b = new.sb("x1b", [P, D])

        rotary_tables(nc, tag, table, dram)

        ps_front = [new.ps(f"ps_front{n}", [P, 512]) for n in range(2)]
        ps_s = [new.ps(f"ps_s{n}", [P, 512]) for n in range(2)]
        ps_pT = new.ps("ps_pT", [P, 512])
        ps_o = new.ps("ps_o", [P, 4, P])
        ps_up = new.ps("ps_up", [P, 512])
        ps_gate = new.ps("ps_gate", [P, 512])
        ps_small = ps_up[:, 384:512]
        ps_y = ps_gate[:, 384:512]

        base_loaded, weights0, weights1 = (new.sem(n) for n in ("base_loaded", "weights0", "weights1"))
        const_ready, psum_zeroed, q_zeroed = (new.sem(n) for n in ("const_ready", "psum_zeroed", "q_zeroed"))
        (shifted_f, xs_ready, xsT_full, xsT_ready, proj_full, squared, sumsq_ready, rotated, summed, clamped,
         logged, rn_ready, qk_ready, qkT_full, qkT_ready, v_ready, k_before_ready, v_before_ready) = (new.sem(n) for n in (
             "shifted_f", "xs_ready", "xsT_full", "xsT_ready", "proj_full", "squared", "sumsq_ready", "rotated",
             "summed", "clamped", "logged", "rn_ready", "qk_ready", "qkT_full", "qkT_ready", "v_ready",
             "k_before_ready", "v_before_ready"))
        (s_full, max_ready, exp_ready, inv_ready, p_ready, pT_full, pT_ready, pv_done, o_ready, y_full,
         x1_ready) = (new.sem(n) for n in ("s_full", "max_ready", "exp_ready", "inv_ready", "p_ready", "pT_full",
                                           "pT_ready", "pv_done", "o_ready", "y_full", "x1_ready"))
        (shifted_m, xm_ready, stats_ready, mv_ready, var_ready, mlog_ready, mrstd_ready, xhat_ready, xhT_full,
         xnT_ready, up_full, biased, gelu_ready, hid_ready, hT_full, hT_ready, down_full, x1b_ready,
         y_ready) = (new.sem(n) for n in (
             "shifted_m", "xm_ready", "stats_ready", "mv_ready", "var_ready", "mlog_ready", "mrstd_ready",
             "xhat_ready", "xhT_full", "xnT_ready", "up_full", "biased", "gelu_ready", "hid_ready", "hT_full",
             "hT_ready", "down_full", "x1b_ready", "y_ready"))
        block = ctx.enter_context(nc.Block())

        def par(i):
            return (i // NT) % 2

        def u(i):
            t = i % NT
            return (t // TPB) * (TPB + 1) + t % TPB + 1

        def run(step, eng):
            step(0, 0, True, False, False)
            step(1, 1, True, True, False)
            with eng.Fori(1, STEPS // 2) as two_steps:
                i = 2 * two_steps
                step(i, 0, True, True, True)
                step(i + 1, 1, True, True, True)
            step(STEPS, 0, False, True, True)
            step(STEPS + 1, 1, False, False, True)

        WEIGHT_DMAS = 7

        def wait_weights(eng, i):
            l = i // NT
            wait(eng, weights0, 16 * WEIGHT_DMAS * ((l + 2) // 2))
            wait(eng, weights1, 16 * WEIGHT_DMAS * ((l + 1) // 2))

        def pool_copy(dst, src):
            shape, zero = list(src.shape), zeros[:, :]
            while len(zero.shape) < len(shape):
                zero = zero.unsqueeze(1)
            return nc.gpsimd.tensor_tensor(dst, src, zero.to_broadcast(shape), ALU.add)

        @block.sync
        def _(sp):
            def load(l, q):
                done = (weights0, weights1)[q]
                sp.dma_start(w_qkv[:, q, :], dram["Wqkv"][l]).then_inc(done, 16)
                sp.dma_start(w_o[:, q, :, :], dram["Wo"][l].rearrange("(c p) d -> p c d", p=P)).then_inc(done, 16)
                sp.dma_start(w_1[:, q, :], dram["W1"][l]).then_inc(done, 16)
                sp.dma_start(w_2[:, q, 0:2, :],
                             dram["W2"][l, 0:256, :].rearrange("(c p) d -> p c d", p=P)).then_inc(done, 16)
                sp.dma_start(w_2[0:FF - 256, q, 2, :], dram["W2"][l, 256:FF, :]).then_inc(done, 16)
                sp.dma_start(b_1[:, q, :], dram["b1"][l].partition_broadcast(P)).then_inc(done, 16)
                sp.dma_start(b_2[:, q, :], dram["b2"][l].partition_broadcast(P)).then_inc(done, 16)

            load(0, 0)
            sp.dma_start(ln_gb[:, :, :], dram["ln_gb"]).then_inc(base_loaded, 16)
            load(1, 1)
            with sp.Fori(1, DEPTH // 2) as two_layers:
                l = 2 * two_layers
                sp.wait_ge(y_ready, NT * l)
                load(l, 0)
                sp.wait_ge(y_ready, NT * (l + 1))
                load(l + 1, 1)

        @block.gpsimd
        def _(pool):
            pool.memset(shift[:, :], 0.0).then_inc(const_ready, 1)
            pool.memset(carry[:, :], 0.0).then_inc(const_ready, 1)
            pool.memset(mask[:, :, :], 0.0).then_inc(const_ready, 1)
            pool.memset(kT[:, 1, :, :], 0.0).then_inc(const_ready, 1)
            pool.memset(v[:, 1, :], 0.0).then_inc(const_ready, 1)
            pool.memset(zeros[:, :], 0.0).then_inc(const_ready, 1)
            pool.wait_ge(const_ready, 6)
            pool.affine_select(out=shift[:, :], in_=shift[:, :], compare_op=ALU.not_equal, fill=1.0, base=1,
                               pattern=[[-1, P]], channel_multiplier=1).then_inc(const_ready, 1)
            pool.affine_select(out=carry[:, :], in_=carry[:, :], compare_op=ALU.not_equal, fill=1.0,
                               base=-(P - 1), pattern=[[P, P]], channel_multiplier=1).then_inc(const_ready, 1)
            pool.affine_select(out=mask[:, :, :], in_=mask[:, :, :], compare_op=ALU.is_ge, fill=NEG, base=0,
                               pattern=[[0, 2], [1, KEYS]], channel_multiplier=-1).then_inc(const_ready, 1)
            pool.wait_ge(const_ready, 9)
            pool.affine_select(out=mask[:, :, :], in_=mask[:, :, :], compare_op=ALU.is_ge, fill=NEG, base=WINDOW,
                               pattern=[[0, 2], [-1, KEYS]], channel_multiplier=1).then_inc(const_ready, 1)
            pool.wait_ge(const_ready, 10)
            pool.memset(mask[:, 0, 0:WINDOW], NEG).then_inc(const_ready, 1)
            pool.wait_ge(const_ready, 11)

            def norm_probs(a, c):
                n = PAIRS * a + c
                wait(pool, inv_ready, n + 1)
                inv = inv_sum[:, c % 2, :].unsqueeze(2).to_broadcast([P, 2, KEYS])
                pool.tensor_tensor(probs[:, c % 2, :, :], probs[:, c % 2, :, :], inv, ALU.mult).then_inc(p_ready, 1)

            def add_parts(i, c):
                wait(pool, rotated, 4 * i + c + 1)
                wait(pool, qkT_full, 4 * (i - 1) + c + 1)
                pool.tensor_tensor(qk[:, c, :], cos_part[:, c % 2, :], sin_part[:, c % 2, :],
                                   ALU.add).then_inc(summed, 1)

            def norm_qk(i, c):
                wait(pool, summed, 4 * i + c + 1)
                view = qk[:, c, :].rearrange("p (h e) -> p h e", e=DH)
                rn = norms[:, 8 * c:8 * c + 8].unsqueeze(2).to_broadcast([P, 8, DH])
                pool.tensor_tensor(view, view, rn, ALU.mult).then_inc(qk_ready, 1)

            def step(i, p, front, attend, mlp):
                a, m = i - 1, i - 2
                if front:
                    wait(pool, y_ready, i + 1)
                    wait(pool, xsT_full, i - 1)
                    pool_copy(xs[:, p, 0:DH], Y[:, u(i), 0:DH]).then_inc(xs_ready, 1)
                if mlp:
                    wait(pool, x1_ready, m + 1)
                    wait(pool, xhat_ready, m)
                    pool_copy(xm[:, 0:DH], X1[:, u(m), 0:DH]).then_inc(xm_ready, 1)
                for c in range(PAIRS):
                    if attend:
                        norm_probs(a, c)
                    if front and c in (2, 3):
                        add_parts(i, c - 2)
                    if front and c == 4:
                        wait(pool, rn_ready, 2 * i + 1)
                        norm_qk(i, 0)
                        norm_qk(i, 1)
                        add_parts(i, 2)
                    if front and c == 5:
                        add_parts(i, 3)
                        wait(pool, rn_ready, 2 * i + 2)
                        norm_qk(i, 2)
                        norm_qk(i, 3)
                if mlp:
                    wait_weights(pool, m)
                    wait(pool, y_ready, NT + m)
                    pool.tensor_tensor(x1b[:, :], X1[:, u(m), :], b_2[:, par(m), :],
                                       ALU.add).then_inc(x1b_ready, 1)
                    wait(pool, gelu_ready, m + 1)
                    pool.tensor_tensor(gate[:, :], up[:, 0, :], gate[:, :], ALU.mult).then_inc(hid_ready, 1)
                if front:
                    wait(pool, qkT_ready, 4 * i)
                    wait(pool, s_full, PAIRS * (i - 1))
                    pool_copy(kT[:, p, :, 0:WINDOW], kT[:, 1 - p, :, P:KEYS]).then_inc(k_before_ready, 1)

            run(step, pool)

        @block.vector
        def _(dve):
            dve.memset(ps_pT[:, :], 0.0).then_inc(psum_zeroed, 1)
            dve.wait_ge(const_ready, 11)
            dve.memset(qT[DH:P, :, 0, :, :], 0.0).then_inc(q_zeroed, 1)
            dve.memset(qT[0:DH, :, 1, :, :], 0.0).then_inc(q_zeroed, 1)
            dve.memset(ln_var[:, :], 0.0).then_inc(y_ready, NT)

            def row_max(a, c):
                n = PAIRS * a + c
                wait(dve, s_full, n + 1)
                wait(dve, exp_ready, 2 * n - 2)
                dve.tensor_reduce(neg_max[:, c % 2, :], ps_s[c % 2][:, 0:2 * KEYS].rearrange(
                    "p (h k) -> p h k", k=KEYS), AX.X, ALU.max, negate=True).then_inc(max_ready, 1)

            def inverse(a, c):
                n = PAIRS * a + c
                wait(dve, exp_ready, 2 * n + 2)
                wait(dve, p_ready, n - 1)
                dve.reciprocal(inv_sum[:, c % 2, :], row_sum[:, c % 2, :]).then_inc(inv_ready, 1)

            def rotate(i, c):
                n = 4 * i + c
                src = ps_front[c % 2][:, :].rearrange("p (h a e) -> p h a e", a=2, e=DH // 2)
                j, l, which = i % TPB, i // NT, 2 * (c // 2)
                cos = table[:, l, j, which, :].unsqueeze(1).to_broadcast([P, 8, DH])
                wait(dve, squared, n + 1)
                wait(dve, summed, n - 1)
                dve.tensor_tensor(cos_part[:, c % 2, :].rearrange("p (h e) -> p h e", e=DH),
                                  ps_front[c % 2][:, :].rearrange("p (h e) -> p h e", e=DH), cos, ALU.mult)
                out = sin_part[:, c % 2, :].rearrange("p (h a e) -> p h a e", a=2, e=DH // 2)
                for half in range(2):
                    sin = table[:, l, j, which + 1, half * 32:half * 32 + 32].unsqueeze(1).to_broadcast([P, 8, 32])
                    last = dve.tensor_tensor(out[:, :, half, :], src[:, :, 1 - half, :], sin, ALU.mult)
                last.then_inc(rotated, 1)
                wait(dve, clamped, 2 * i + c // 2 - 1)
                dve.tensor_reduce(sum_sq[:, 8 * c:8 * c + 8], squares[:, c % 2, :].rearrange(
                    "p (h e) -> p h e", e=DH), AX.X, ALU.add).then_inc(sumsq_ready, 1)

            def clamp(i, q):
                wait(dve, sumsq_ready, 4 * i + 2 * q + 2)
                wait(dve, qk_ready, 4 * i + 2 * q - 2)
                dve.tensor_scalar(norms[:, 16 * q:16 * q + 16], sum_sq[:, 16 * q:16 * q + 16], 1e-19, None,
                                  ALU.max).then_inc(clamped, 1)

            def step(i, p, front, attend, mlp):
                a, m = i - 1, i - 2
                if attend:
                    row_max(a, 0)
                if front:
                    wait(dve, shifted_f, i + 1)
                    wait(dve, xsT_full, i - 1)
                    dve.tensor_copy(xs[:, p, DH:D], ps_front[0][:, 0:DH]).then_inc(xs_ready, 1)
                if mlp:
                    wait(dve, shifted_m, m + 1)
                    wait(dve, xhat_ready, m)
                    dve.tensor_copy(xm[:, DH:D], ps_small[:, 0:DH]).then_inc(xm_ready, 1)
                if attend:
                    inverse(a, 0)
                    row_max(a, 1)
                if mlp:
                    wait(dve, xm_ready, 2 * m + 2)
                    dve.bn_stats(ln_stats[:, :], xm[:, :]).then_inc(stats_ready, 1)
                    wait(dve, stats_ready, m + 1)
                    dve.memset(held[:, :], 0.0)
                    dve.bn_aggr(ln_mv[:, :], ln_stats[:, :]).then_inc(mv_ready, 1)
                    wait(dve, mv_ready, m + 1)
                    dve.tensor_scalar(ln_var[:, :], ln_mv[:, 1:2], LN_EPS, None, ALU.add).then_inc(var_ready, 1)
                if attend:
                    inverse(a, 1)
                    row_max(a, 2)
                if front:
                    rotate(i, 0)
                if mlp:
                    wait(dve, mrstd_ready, m + 1)
                    wait(dve, xhT_full, m)
                    dve.tensor_scalar(xhat[:, :], xm[:, :], ln_mv[:, 0:1], ln_rstd[:, 0:1], ALU.subtract,
                                      ALU.mult).then_inc(xhat_ready, 1)
                if attend:
                    inverse(a, 2)
                    row_max(a, 3)
                if front:
                    rotate(i, 1)
                    clamp(i, 0)
                if attend:
                    inverse(a, 3)
                    row_max(a, 4)
                if front:
                    rotate(i, 2)
                if attend:
                    inverse(a, 4)
                    row_max(a, 5)
                if front:
                    rotate(i, 3)
                    clamp(i, 1)
                if attend:
                    inverse(a, 5)
                    row_max(a, 6)
                if mlp:
                    wait_weights(dve, m)
                    wait(dve, up_full, m + 1)
                    wait(dve, hid_ready, m)
                    dve.tensor_tensor(up[:, 0, :], ps_up[:, 0:FF], b_1[:, par(m), 0:FF], ALU.add)
                    dve.tensor_tensor(up[:, 1, :], ps_gate[:, 0:FF], b_1[:, par(m), FF:2 * FF],
                                      ALU.add).then_inc(biased, 1)
                if attend:
                    inverse(a, 6)
                    row_max(a, 7)
                if attend:
                    inverse(a, 7)
                if front:
                    wait(dve, v_ready, 2 * i)
                    wait(dve, pv_done, PAIRS * (i - 1))
                    dve.tensor_copy(v_before[:, p, :], v[P - WINDOW:P, 1 - p, :]).then_inc(v_before_ready, 1)
                if mlp:
                    wait(dve, hT_full, m + 1)
                    wait(dve, down_full, m)
                    dve.tensor_copy(hT[:, 0:2, :].rearrange("p c t -> p (c t)"), ps_up[:, 0:256])
                    dve.tensor_copy(hT[0:FF - 256, 2, :], ps_up[0:FF - 256, 256:384]).then_inc(hT_ready, 1)
                if attend:
                    wait(dve, y_full, a + 1)
                    dve.tensor_tensor(X1[:, u(a), :], ps_y[:, :], Y[:, u(a), :], ALU.add).then_inc(x1_ready, 1)
                if mlp:
                    wait(dve, down_full, m + 1)
                    wait(dve, x1b_ready, m + 1)
                    dve.tensor_tensor(Y[:, u(m), :], ps_small[:, :], x1b[:, :], ALU.add).then_inc(y_ready, 1)

            run(step, dve)

        @block.scalar
        def _(act):
            def exps(a, c):
                n = PAIRS * a + c
                wait(act, max_ready, n + 1)
                wait(act, pT_full, n - 1)
                wait(act, inv_ready, n - 1)
                for h in range(2):
                    act.activation(probs[:, c % 2, h, :], ps_s[c % 2][:, h * KEYS:(h + 1) * KEYS], ACT.Exp,
                                   bias=neg_max[:, c % 2, h:h + 1],
                                   accum_out=row_sum[:, c % 2, h:h + 1]).then_inc(exp_ready, 1)

            def copy_pT(a, c):
                n = PAIRS * a + c
                wait(act, pT_full, n + 1)
                wait(act, pv_done, n - 1)
                act.activation(probsT[:, c % 2, :], ps_pT[:, 0:2 * P + 2 * WINDOW], ACT.Copy).then_inc(pT_ready, 1)

            def square(i, c):
                wait(act, proj_full, 6 * i + c + 1)
                wait(act, sumsq_ready, 4 * i + c - 1)
                act.activation(squares[:, c % 2, :], ps_front[c % 2][:, :], ACT.Square).then_inc(squared, 1)

            def rnorm(i, q):
                wait(act, clamped, 2 * i + q + 1)
                act.activation(norms[:, 16 * q:16 * q + 16], norms[:, 16 * q:16 * q + 16], ACT.Ln).then_inc(logged, 1)
                wait(act, logged, 2 * i + q + 1)
                act.activation(norms[:, 16 * q:16 * q + 16], norms[:, 16 * q:16 * q + 16], ACT.Exp,
                               scale=-0.5).then_inc(rn_ready, 1)

            def copy_v(i, p, c):
                wait(act, proj_full, 6 * i + 5 + c)
                wait(act, pv_done, PAIRS * (i - 1))
                wait(act, v_before_ready, i)
                act.activation(v[:, p, 512 * c:512 * c + 512], ps_front[c][:, :], ACT.Copy).then_inc(v_ready, 1)

            def copy_qkT(i, p, c):
                wait(act, qkT_full, 4 * i + c + 1)
                wait(act, s_full, PAIRS * (i - 1))
                wait(act, k_before_ready, i)
                g = 4 * (c % 2)
                src = ps_front[c % 2][:, :].rearrange("p (c t) -> p c t", t=P)
                if c < 2:
                    act.activation(qT[0:DH, p, 0, g:g + 4, :], src[0:DH], ACT.Copy)
                    act.activation(qT[DH:P, p, 1, g:g + 4, :], src[DH:P], ACT.Copy).then_inc(qkT_ready, 1)
                else:
                    act.activation(kT[:, p, g:g + 4, WINDOW:KEYS], src, ACT.Copy).then_inc(qkT_ready, 1)

            def copy_o(a, g):
                wait(act, pv_done, PAIRS * a + 4 * g + 4)
                wait(act, y_full, a)
                act.activation(oT[:, 4 * g:4 * g + 4, :], ps_o[:, :, :], ACT.Copy).then_inc(o_ready, 1)

            def step(i, p, front, attend, mlp):
                a, m = i - 1, i - 2
                if attend:
                    exps(a, 0)
                if attend:
                    exps(a, 1)
                if front:
                    wait(act, xsT_full, i + 1)
                    wait(act, proj_full, 6 * (i - 1))
                    act.activation(xsT[:, p, :], ps_front[1][:, 0:P], ACT.Copy).then_inc(xsT_ready, 1)
                if mlp:
                    wait(act, var_ready, m + 1)
                    wait(act, xhat_ready, m)
                    act.activation(ln_rstd[:, :], ln_var[:, :], ACT.Ln).then_inc(mlog_ready, 1)
                    wait(act, mlog_ready, m + 1)
                    act.activation(ln_rstd[:, :], ln_rstd[:, :], ACT.Exp, scale=-0.5).then_inc(mrstd_ready, 1)
                if attend:
                    copy_pT(a, 0)
                if attend:
                    exps(a, 2)
                if front:
                    square(i, 0)
                    square(i, 1)
                if mlp:
                    wait(act, xhT_full, m + 1)
                    wait(act, up_full, m)
                    act.activation(xnT[:, :], ps_small[:, :], ACT.Identity, bias=ln_gb[:, m // NT, 1:2],
                                   scale=ln_gb[:, m // NT, 0:1]).then_inc(xnT_ready, 1)
                if attend:
                    copy_pT(a, 1)
                if attend:
                    exps(a, 3)
                if front:
                    square(i, 2)
                if attend:
                    copy_pT(a, 2)
                if attend:
                    exps(a, 4)
                if front:
                    rnorm(i, 0)
                    square(i, 3)
                if attend:
                    copy_pT(a, 3)
                if attend:
                    exps(a, 5)
                if front:
                    copy_v(i, p, 0)
                if attend:
                    copy_pT(a, 4)
                    copy_o(a, 0)
                if attend:
                    exps(a, 6)
                if front:
                    rnorm(i, 1)
                    copy_v(i, p, 1)
                if attend:
                    copy_pT(a, 5)
                if attend:
                    exps(a, 7)
                if front:
                    copy_qkT(i, p, 0)
                    copy_qkT(i, p, 1)
                if attend:
                    copy_pT(a, 6)
                if mlp:
                    wait(act, biased, m + 1)
                    wait(act, hT_full, m)
                    act.activation(gate[:, :], up[:, 1, :], ACT.Gelu).then_inc(gelu_ready, 1)
                    act.preload_act_table_set("natural_log_exp_and_others")
                if attend:
                    copy_pT(a, 7)
                if front:
                    copy_qkT(i, p, 2)
                if front:
                    copy_qkT(i, p, 3)
                if attend:
                    copy_o(a, 1)

            act.preload_act_table_set("natural_log_exp_and_others")
            act.wait_ge(base_loaded, 16)
            run(step, act)

        @block.tensor
        def _(pe):
            def scores(a, p, c):
                n = PAIRS * a + c
                wait(pe, exp_ready, 2 * (n - 1))
                k = 1 if p == 1 else ((a % TPB) + 1) // 2
                dst = ps_s[c % 2][:, 0:2 * KEYS]
                pe.matmul(dst, identb[:, :], mask[:, k, :].unsqueeze(1).to_broadcast([P, 2, KEYS]),
                          start=True, stop=False)
                for h in range(2):
                    last = pe.matmul(dst[:, h * KEYS:(h + 1) * KEYS], qT[:, p, h, c, :], kT[:, p, c, :],
                                     start=False, stop=(h == 1))
                last.then_inc(s_full, 1)

            def turn_probs(a, c):
                n = PAIRS * a + c
                wait(pe, p_ready, n + 1)
                wait(pe, pT_ready, n)
                for h in range(2):
                    pe.transpose(ps_pT[:, h * P:(h + 1) * P], probs[:, c % 2, h, WINDOW:KEYS], ident[:, :])
                for h in range(2):
                    o = 2 * P + h * WINDOW
                    last = pe.transpose(ps_pT[0:WINDOW, o:o + WINDOW], probs[0:WINDOW, c % 2, h, 0:WINDOW],
                                        ident[0:WINDOW, 0:WINDOW])
                last.then_inc(pT_full, 1)

            def weigh_values(a, p, c):
                n = PAIRS * a + c
                wait(pe, pT_ready, n + 1)
                if c % 4 == 0:
                    wait(pe, o_ready, 2 * a + c // 4)
                for h in range(2):
                    head = slice((2 * c + h) * DH, (2 * c + h + 1) * DH)
                    out = ps_o[DH * h:DH * h + DH, c % 4, :]
                    pe.matmul(out, v[:, p, head], probsT[:, c % 2, h * P:(h + 1) * P], start=True, stop=False)
                    o = 2 * P + h * WINDOW
                    last = pe.matmul(out[:, 0:WINDOW], v_before[:, p, head],
                                     probsT[0:WINDOW, c % 2, o:o + WINDOW], start=False, stop=True)
                last.then_inc(pv_done, 1)

            def project(i, p, c):
                if c == 0:
                    wait_weights(pe, i)
                    wait(pe, xsT_ready, i + 1)
                elif c >= 2:
                    n = 4 * i + c - 2
                    wait(pe, rotated, n + 1)
                pe.matmul(ps_front[c % 2][:, :], xsT[:, p, :], w_qkv[:, par(i), 512 * c:512 * c + 512],
                          start=True, stop=True).then_inc(proj_full, 1)

            def turn_qk(i, c):
                wait(pe, qk_ready, 4 * i + c + 1)
                if c < 2:
                    wait(pe, v_ready, 2 * i + c + 1)
                else:
                    wait(pe, qkT_ready, 4 * i + c - 1)
                for n in range(4):
                    last = pe.transpose(ps_front[c % 2][:, n * P:(n + 1) * P], qk[:, c, n * P:(n + 1) * P],
                                        ident[:, :])
                last.then_inc(qkT_full, 1)

            def step(i, p, front, attend, mlp):
                a, m = i - 1, i - 2
                pa = 1 - p
                if attend:
                    wait(pe, qkT_ready, 4 * a + 4)
                    wait(pe, k_before_ready, a + 1)
                    wait(pe, v_before_ready, a + 1)
                    wait(pe, v_ready, 2 * a + 2)
                    scores(a, pa, 0)
                if front:
                    wait(pe, y_ready, i + 1)
                    wait(pe, qkT_ready, 4 * i - 1)
                    pe.matmul(ps_front[0][:, 0:DH], shift[:, :], Y[:, u(i), DH:D], start=True, stop=False)
                    pe.matmul(ps_front[0][:, 0:DH], carry[:, :], Y[:, u(i) - 1, DH:D], start=False,
                              stop=True).then_inc(shifted_f, 1)
                if mlp:
                    wait(pe, x1_ready, m + 1)
                    wait(pe, y_ready, NT + m)
                    pe.matmul(ps_small[:, 0:DH], shift[:, :], X1[:, u(m), DH:D], start=True, stop=False)
                    pe.matmul(ps_small[:, 0:DH], carry[:, :], X1[:, u(m) - 1, DH:D], start=False,
                              stop=True).then_inc(shifted_m, 1)
                if attend:
                    scores(a, pa, 1)
                if front:
                    wait(pe, xs_ready, 2 * i + 2)
                    wait(pe, qkT_ready, 4 * i)
                    pe.transpose(ps_front[1][:, 0:P], xs[:, p, :], ident[:, :]).then_inc(xsT_full, 1)
                if attend:
                    turn_probs(a, 0)
                if attend:
                    scores(a, pa, 2)
                if front:
                    project(i, p, 0)
                    project(i, p, 1)
                if mlp:
                    wait(pe, xhat_ready, m + 1)
                    pe.transpose(ps_small[:, :], xhat[:, :], ident[:, :]).then_inc(xhT_full, 1)
                if attend:
                    turn_probs(a, 1)
                    weigh_values(a, pa, 0)
                if attend:
                    scores(a, pa, 3)
                if front:
                    project(i, p, 2)
                if attend:
                    turn_probs(a, 2)
                    weigh_values(a, pa, 1)
                if attend:
                    scores(a, pa, 4)
                if front:
                    project(i, p, 3)
                if mlp:
                    wait(pe, xnT_ready, m + 1)
                    wait_weights(pe, m)
                    wait(pe, hT_ready, m)
                    pe.matmul(ps_up[:, 0:FF], xnT[:, :], w_1[:, par(m), 0:FF], start=True, stop=True)
                    pe.matmul(ps_gate[:, 0:FF], xnT[:, :], w_1[:, par(m), FF:2 * FF], start=True,
                              stop=True).then_inc(up_full, 1)
                if attend:
                    turn_probs(a, 3)
                    weigh_values(a, pa, 2)
                if attend:
                    scores(a, pa, 5)
                if front:
                    project(i, p, 4)
                if attend:
                    turn_probs(a, 4)
                    weigh_values(a, pa, 3)
                if attend:
                    scores(a, pa, 6)
                if front:
                    project(i, p, 5)
                if attend:
                    turn_probs(a, 5)
                    weigh_values(a, pa, 4)
                if attend:
                    scores(a, pa, 7)
                if front:
                    turn_qk(i, 0)
                    turn_qk(i, 1)
                if attend:
                    turn_probs(a, 6)
                    weigh_values(a, pa, 5)
                if attend:
                    turn_probs(a, 7)
                    weigh_values(a, pa, 6)
                if front:
                    turn_qk(i, 2)
                if mlp:
                    wait(pe, hid_ready, m + 1)
                    for c, (lo, n) in enumerate(FF_CHUNKS):
                        last = pe.transpose(ps_up[0:n, c * P:(c + 1) * P], gate[:, lo:lo + n], ident[:, :])
                    last.then_inc(hT_full, 1)
                if attend:
                    weigh_values(a, pa, 7)
                if front:
                    turn_qk(i, 3)
                if attend:
                    wait_weights(pe, a)
                    wait(pe, o_ready, 2 * a + 2)
                    wait(pe, x1_ready, a)
                    for c in range(PAIRS):
                        last = pe.matmul(ps_y[:, :], oT[:, c, :], w_o[:, par(a), c, :], start=(c == 0),
                                         stop=(c == PAIRS - 1))
                    last.then_inc(y_full, 1)
                if mlp:
                    wait(pe, hT_ready, m + 1)
                    for c, (lo, n) in enumerate(FF_CHUNKS):
                        last = pe.matmul(ps_small[:, :], hT[0:n, c, :], w_2[0:n, par(m), c, :], start=(c == 0),
                                         stop=(c == 2))
                    last.then_inc(down_full, 1)

            pe.wait_ge(const_ready, 11)
            pe.wait_ge(psum_zeroed, 1)
            pe.wait_ge(q_zeroed, 2)
            run(step, pe)


def transpose_stream(nc, tag, Y, YT, ident):
    with ExitStack() as ctx:
        new = Pool_(nc, ctx, tag)
        banks = [new.ps(f"bank{b}", [P, TPB, P]) for b in range(B)]
        turned, copied = new.sem("turned"), new.sem("copied")
        block = ctx.enter_context(nc.Block())

        @block.tensor
        def _(pe):
            for b in range(B):
                for j in range(TPB):
                    last = pe.transpose(banks[b][:, j, :], Y[:, slot(TPB * b + j), :], ident[:, :])
                last.then_inc(turned, 1)

        @block.vector
        def _(dve):
            for b in range(B):
                dve.wait_ge(turned, b + 1)
                dve.tensor_copy(YT[:, TPB * b:TPB * b + TPB, :], banks[b][:, :, :]).then_inc(copied, 1)


def causal_attention(nc, tag, X, Y, ident, identb, dram):
    STEPS = B * PAIRS
    UNITS = 2 * TPB
    with ExitStack() as ctx:
        new = Pool_(nc, ctx, tag)
        YT = new.sb("YT", [P, NT, P])
        transpose_stream(nc, tag + "_turn", Y, YT, ident)
        w_pair = new.sb("w_pair", [P, 2, 4, P])
        causal = new.sb("causal", [P, P], BF16)
        qT = new.sb("qT", [P, 2, 2, S])
        kT = new.sb("kT", [P, 2, S])
        vT = new.sb("vT", [P, S])
        v = new.sb("v", [P, 2, TPB, P])
        neg_max = new.sb("neg_max", [P, 2])
        row_sum = new.sb("row_sum", [P, 2])
        inv_sum = new.sb("inv_sum", [P, 2])
        probs = new.sb("probs", [P, 2, S])
        probsT = new.sb("probsT", [P, 2, S])
        oT = new.sb("oT", [P, S])
        ps_proj = [new.ps(f"ps_proj{n}", [P, 512]) for n in range(2)]
        ps_s = [new.ps(f"ps_s{n}", [P, 512]) for n in range(2)]
        ps_pT = [new.ps(f"ps_pT{n}", [P, 512]) for n in range(2)]
        ps_o = new.ps("ps_o", [P, 512])
        ps_z = new.ps("ps_z", [P, TPB, D])
        w_loaded0, w_loaded1, made, q_zeroed = (new.sem(n) for n in ("w_loaded0", "w_loaded1", "made", "q_zeroed"))
        (q_full, k_full, vT_full, v_full, q_ready, k_ready, vT_ready, v_ready) = (new.sem(n) for n in (
            "q_full", "k_full", "vT_full", "v_full", "q_ready", "k_ready", "vT_ready", "v_ready"))
        (s_full, max_ready, exp_ready, inv_ready, p_ready, pT_full, pT_ready, pv_done, o_ready, z_full,
         x_added) = (new.sem(n) for n in ("s_full", "max_ready", "exp_ready", "inv_ready", "p_ready", "pT_full",
                                          "pT_ready", "pv_done", "o_ready", "z_full", "x_added"))
        block = ctx.enter_context(nc.Block())

        def run(step, eng):
            step(0, 0, True, False)
            step(1, 1, True, True)
            with eng.Fori(1, STEPS // 2) as two_steps:
                i = 2 * two_steps
                step(i, 0, True, True)
                step(i + 1, 1, True, True)
            step(STEPS, 0, False, True)

        def unit(n):
            return n // 2, n % 2

        @block.sync
        def _(sp):
            def load(i, p):
                done = (w_loaded0, w_loaded1)[p]
                sp.dma_start(w_pair[:, p, 0:3, :], dram["a_qkv"][i % PAIRS]).then_inc(done, 16)
                sp.dma_start(w_pair[:, p, 3, :], dram["a_out"][i % PAIRS]).then_inc(done, 16)

            load(0, 0)
            load(1, 1)
            with sp.Fori(1, STEPS // 2) as two_steps:
                i = 2 * two_steps
                sp.wait_ge(z_full, i - 1)
                load(i, 0)
                sp.wait_ge(z_full, i)
                load(i + 1, 1)

        @block.gpsimd
        def _(pool):
            pool.memset(causal[:, :], 0.0).then_inc(made, 1)
            pool.wait_ge(made, 1)
            pool.affine_select(out=causal[:, :], in_=causal[:, :], compare_op=ALU.is_ge, fill=NEG, base=0,
                               pattern=[[-1, P]], channel_multiplier=1).then_inc(made, 1)

        @block.vector
        def _(dve):
            dve.memset(qT[DH:P, :, 0, :], 0.0).then_inc(q_zeroed, 1)
            dve.memset(qT[0:DH, :, 1, :], 0.0).then_inc(q_zeroed, 1)

            def row_max(a, n):
                g, keys = UNITS * a + n, P * (unit(n)[0] + 1)
                wait(dve, s_full, g + 1)
                wait(dve, exp_ready, g - 1)
                dve.tensor_reduce(neg_max[:, n % 2:n % 2 + 1], ps_s[n % 2][:, 0:keys], AX.X, ALU.max,
                                  negate=True).then_inc(max_ready, 1)

            def normalize(a, n):
                g, keys = UNITS * a + n, P * (unit(n)[0] + 1)
                wait(dve, exp_ready, g + 1)
                dve.reciprocal(inv_sum[:, n % 2:n % 2 + 1], row_sum[:, n % 2:n % 2 + 1]).then_inc(inv_ready, 1)
                wait(dve, inv_ready, g + 1)
                dve.tensor_scalar(probs[:, n % 2, 0:keys], probs[:, n % 2, 0:keys], inv_sum[:, n % 2:n % 2 + 1],
                                  None, ALU.mult).then_inc(p_ready, 1)

            def step(i, p, front, attend):
                a = i - 1
                for n in range(UNITS + 1):
                    if attend and n >= 1:
                        normalize(a, n - 1)
                    if attend and n < UNITS:
                        row_max(a, n)
                    if front and n == 2:
                        wait(dve, k_full, i + 1)
                        wait(dve, s_full, UNITS * (i - 1))
                        dve.tensor_copy(kT[:, p, :], ps_proj[1][:, :]).then_inc(k_ready, 1)
                    if front and n == 4:
                        wait(dve, vT_full, i + 1)
                        wait(dve, v_full, i)
                        dve.tensor_copy(vT[:, :], ps_proj[0][:, :]).then_inc(vT_ready, 1)
                if attend:
                    wait(dve, z_full, a + 1)
                    tiles = X[:, 5 * (a // PAIRS) + 1:5 * (a // PAIRS) + 5, :] if isinstance(a, int) else \
                        X[:, bass.ds(5 * (a // PAIRS) + 1, TPB), :]
                    dve.scalar_tensor_tensor(out=tiles, in0=ps_z[:, :, :], scalar=1.0 / HEADS, in1=tiles,
                                             op0=ALU.mult, op1=ALU.add).then_inc(x_added, 1)

            run(step, dve)

        @block.scalar
        def _(act):
            def exp(a, n):
                g, keys = UNITS * a + n, P * (unit(n)[0] + 1)
                wait(act, max_ready, g + 1)
                wait(act, pT_full, g - 1)
                wait(act, inv_ready, g - 1)
                act.activation(probs[:, n % 2, 0:keys], ps_s[n % 2][:, 0:keys], ACT.Exp,
                               bias=neg_max[:, n % 2:n % 2 + 1],
                               accum_out=row_sum[:, n % 2:n % 2 + 1]).then_inc(exp_ready, 1)

            def copy_pT(a, n):
                g, keys = UNITS * a + n, P * (unit(n)[0] + 1)
                wait(act, pT_full, g + 1)
                wait(act, pv_done, g - 1)
                act.activation(probsT[:, n % 2, 0:keys], ps_pT[n % 2][:, 0:keys], ACT.Copy).then_inc(pT_ready, 1)

            def step(i, p, front, attend):
                a = i - 1
                for n in range(UNITS + 1):
                    if attend and n < UNITS:
                        exp(a, n)
                    if front and n == 1:
                        wait(act, q_full, i + 1)
                        wait(act, s_full, UNITS * (i - 1))
                        act.activation(qT[0:DH, p, 0, :], ps_proj[0][0:DH, :], ACT.Copy, scale=1.0 / P)
                        act.activation(qT[DH:P, p, 1, :], ps_proj[0][DH:P, :], ACT.Copy,
                                       scale=1.0 / P).then_inc(q_ready, 1)
                    if front and n == 6:
                        wait(act, v_full, i + 1)
                        wait(act, pv_done, UNITS * (i - 1))
                        act.activation(v[:, p, :, :], ps_proj[1][:, :].rearrange("p (j e) -> p j e", e=P),
                                       ACT.Copy).then_inc(v_ready, 1)
                    if attend and n >= 1:
                        copy_pT(a, n - 1)
                if attend:
                    wait(act, pv_done, UNITS * a + UNITS)
                    wait(act, z_full, a)
                    act.activation(oT[:, :], ps_o[:, :], ACT.Copy).then_inc(o_ready, 1)

            act.wait_ge(q_zeroed, 2)
            run(step, act)

        @block.tensor
        def _(pe):
            def scores(a, p, n):
                g = UNITS * a + n
                t, h = unit(n)
                wait(pe, exp_ready, g - 1)
                pe.matmul(ps_s[n % 2][:, 0:P * (t + 1)], qT[:, p, h, P * t:P * t + P], kT[:, p, 0:P * (t + 1)],
                          start=True, stop=False)
                pe.matmul(ps_s[n % 2][:, P * t:P * t + P], identb[:, :], causal[:, :], start=False,
                          stop=True).then_inc(s_full, 1)

            def turn(a, n):
                g = UNITS * a + n
                wait(pe, p_ready, g + 1)
                wait(pe, pT_ready, g - 1)
                for c in range(unit(n)[0] + 1):
                    last = pe.transpose(ps_pT[n % 2][:, P * c:P * c + P], probs[:, n % 2, P * c:P * c + P],
                                        ident[:, :])
                last.then_inc(pT_full, 1)

            def weigh_values(a, p, n):
                t, h = unit(n)
                wait(pe, pT_ready, UNITS * a + n + 1)
                if n == 0:
                    wait(pe, o_ready, a)
                for c in range(t + 1):
                    last = pe.matmul(ps_o[DH * h:DH * h + DH, P * t:P * t + P], v[:, p, c, DH * h:DH * h + DH],
                                     probsT[:, n % 2, P * c:P * c + P], start=(c == 0), stop=(c == t))
                last.then_inc(pv_done, 1)

            def wait_w(i, p):
                wait(pe, (w_loaded0, w_loaded1)[p], 32 * (i // 2 + 1))

            def step(i, p, front, attend):
                a = i - 1
                tokens = YT[:, TPB * (i // PAIRS):TPB * (i // PAIRS) + TPB, :] if isinstance(i, int) and front \
                    else YT[:, bass.ds(TPB * (i // PAIRS), TPB), :] if front else None
                for n in range(UNITS + 2):
                    if attend and n < UNITS:
                        if n == 0:
                            wait(pe, q_ready, a + 1)
                            wait(pe, k_ready, a + 1)
                            wait(pe, v_ready, a + 1)
                        scores(a, 1 - p, n)
                    if front and n == 0:
                        wait_w(i, p)
                        wait(pe, vT_ready, i)
                        pe.matmul(ps_proj[0][:, :], w_pair[:, p, 0, :], tokens, start=True,
                                  stop=True).then_inc(q_full, 1)
                    if front and n == 1:
                        wait(pe, v_ready, i)
                        pe.matmul(ps_proj[1][:, :], w_pair[:, p, 1, :], tokens, start=True,
                                  stop=True).then_inc(k_full, 1)
                    if front and n == 3:
                        wait(pe, q_ready, i + 1)
                        pe.matmul(ps_proj[0][:, :], w_pair[:, p, 2, :], tokens, start=True,
                                  stop=True).then_inc(vT_full, 1)
                    if front and n == 5:
                        wait(pe, vT_ready, i + 1)
                        wait(pe, k_ready, i + 1)
                        for j in range(TPB):
                            last = pe.transpose(ps_proj[1][:, P * j:P * j + P], vT[:, P * j:P * j + P], ident[:, :])
                        last.then_inc(v_full, 1)
                    if attend and 1 <= n <= UNITS:
                        turn(a, n - 1)
                    if attend and n >= 2:
                        weigh_values(a, 1 - p, n - 2)
                if attend:
                    wait(pe, o_ready, a + 1)
                    wait(pe, x_added, a)
                    for t in range(TPB):
                        last = pe.matmul(ps_z[:, t, :], oT[:, P * t:P * t + P], w_pair[:, 1 - p, 3, :],
                                         start=True, stop=True)
                    last.then_inc(z_full, 1)

            pe.wait_ge(made, 2)
            pe.wait_ge(q_zeroed, 2)
            run(step, pe)


HD_B = D // HEADS
MP_EPS = 1e-4


def block_diagonal(pool, tile_, size, done, inside, outside):
    n, k = tile_.shape[1], tile_.shape[2]
    pool.memset(tile_, inside).then_inc(done, 1)
    pool.wait_ge(done, 1)
    pool.affine_select(out=tile_, in_=tile_, compare_op=ALU.is_ge, fill=outside, base=0,
                       pattern=[[-size, n], [0, k]], channel_multiplier=1).then_inc(done, 1)
    pool.wait_ge(done, 2)
    pool.affine_select(out=tile_, in_=tile_, compare_op=ALU.is_ge, fill=outside, base=size - 1,
                       pattern=[[size, n], [0, k]], channel_multiplier=-1).then_inc(done, 1)


def channel_attention(nc, tag, X, Y, ident, dram):
    GROUPS = TPB * 2 * HEADS
    MIX = 0.5 / np.sqrt(0.5)
    with ExitStack() as ctx:
        new = Pool_(nc, ctx, tag)
        YT = new.sb("YT", [P, NT, P])
        wT = new.sb("wT", [P, 4, D])
        transpose_stream(nc, tag + "_turn", Y, YT, ident)
        normalized_weights(nc, tag + "_w", wT, ident, dram)
        block_mask = new.sb("block_mask", [P, HEADS, HD_B])
        yT = new.sb("yT", [P, S])
        sq = new.sb("sq", [P, GROUPS * HD_B])
        ss = new.sb("ss", [P, GROUPS])
        qk = new.sb("qk", [P, TPB, 2, D])
        vT = new.sb("vT", [P, S])
        logits = new.sb("logits", [P, D])
        neg_max = new.sb("neg_max", [P, 1])
        row_sum = new.sb("row_sum", [P, 1])
        probs = new.sb("probs", [P, D])
        probsT = new.sb("probsT", [P, D])
        oT = new.sb("oT", [P, S])
        ps_qk = new.ps("ps_qk", [P, TPB, 2, D])
        ps_v = new.ps("ps_v", [P, S])
        ps_g = new.ps("ps_g", [P, 512])
        ps_o = new.ps("ps_o", [P, S])
        ps_out = new.ps("ps_out", [P, TPB, D])
        made = new.sem("made")
        (y_copied, qkv_full, squared, summed, rooted, offset, inverted, qk_ready, v_ready, g_full, masked,
         max_ready, exp_ready, sum_inverted, p_ready, pT_full, pT_ready, o_full, o_ready, out_full, kept,
         x_added) = (new.sem(n) for n in (
             "y_copied", "qkv_full", "squared", "summed", "rooted", "offset", "inverted", "qk_ready", "v_ready",
             "g_full", "masked", "max_ready", "exp_ready", "sum_inverted", "p_ready", "pT_full", "pT_ready",
             "o_full", "o_ready", "out_full", "kept", "x_added"))
        block = ctx.enter_context(nc.Block())
        SCALE = float(1.0 / np.sqrt(np.float32(S)))

        @block.gpsimd
        def _(pool):
            block_diagonal(pool, block_mask[:, :, :], HD_B, made, 0.0, NEG)

        @block.vector
        def _(dve):
            dve.wait_ge(made, 3)
            with dve.Fori(0, B) as b:
                dve.tensor_copy(yT[:, :].rearrange("p (j t) -> p j t", t=P),
                                YT[:, bass.ds(TPB * b, TPB), :]).then_inc(y_copied, 1)
                dve.wait_ge(squared, b + 1)
                dve.tensor_reduce(ss[:, :], sq[:, :].rearrange("p (g e) -> p g e", e=HD_B), AX.X,
                                  ALU.add).then_inc(summed, 1)
                dve.wait_ge(rooted, b + 1)
                dve.tensor_scalar(ss[:, :], ss[:, :], float(1.0 / np.sqrt(HD_B)), MP_EPS, ALU.mult,
                                  ALU.add).then_inc(offset, 1)
                dve.wait_ge(offset, b + 1)
                dve.reciprocal(ss[:, :], ss[:, :]).then_inc(inverted, 1)
                dve.wait_ge(inverted, b + 1)
                for bank in range(2):
                    g = GROUPS // 2
                    dve.tensor_tensor(qk[:, 2 * bank:2 * bank + 2, :, :].rearrange("p j w (h e) -> p (j w h) e", e=HD_B),
                                      ps_qk[:, 2 * bank:2 * bank + 2, :, :].rearrange("p j w (h e) -> p (j w h) e", e=HD_B),
                                      ss[:, g * bank:g * bank + g].unsqueeze(2).to_broadcast([P, g, HD_B]),
                                      ALU.mult).then_inc(qk_ready, 1)
                dve.wait_ge(g_full, b + 1)
                dve.scalar_tensor_tensor(out=logits[:, :], in0=ps_g[:, 0:D], scalar=SCALE,
                                         in1=block_mask[:, :, :].rearrange("p n k -> p (n k)"), op0=ALU.mult,
                                         op1=ALU.add).then_inc(masked, 1)
                dve.wait_ge(masked, b + 1)
                dve.tensor_reduce(neg_max[:, :], logits[:, :], AX.X, ALU.max, negate=True).then_inc(max_ready, 1)
                dve.wait_ge(exp_ready, b + 1)
                dve.reciprocal(row_sum[:, :], row_sum[:, :]).then_inc(sum_inverted, 1)
                dve.wait_ge(sum_inverted, b + 1)
                dve.tensor_scalar(probs[:, :], probs[:, :], row_sum[:, 0:1], None, ALU.mult).then_inc(p_ready, 1)
                dve.wait_ge(pT_full, b + 1)
                dve.tensor_copy(probsT[:, :], ps_g[:, 0:D]).then_inc(pT_ready, 1)
                xs, ys = X[:, bass.ds(5 * b + 1, TPB), :], Y[:, bass.ds(5 * b + 1, TPB), :]
                dve.scalar_tensor_tensor(out=xs, in0=ys, scalar=MIX, in1=xs, op0=ALU.mult,
                                         op1=ALU.add).then_inc(kept, 1)
                dve.wait_ge(out_full, b + 1)
                dve.wait_ge(kept, b + 1)
                dve.scalar_tensor_tensor(out=xs, in0=ps_out[:, :, :], scalar=MIX, in1=xs, op0=ALU.mult,
                                         op1=ALU.add).then_inc(x_added, 1)

        @block.scalar
        def _(act):
            with act.Fori(0, B) as b:
                act.wait_ge(qkv_full, b + 1)
                for bank in range(2):
                    last = act.activation(sq[:, 512 * bank:512 * bank + 512],
                                          ps_qk[:, 2 * bank:2 * bank + 2, :, :].rearrange("p j w d -> p (j w d)"),
                                          ACT.Square)
                last.then_inc(squared, 1)
                act.wait_ge(summed, b + 1)
                act.activation(ss[:, :], ss[:, :], ACT.Sqrt).then_inc(rooted, 1)
                act.activation(vT[:, :], ps_v[:, :], ACT.Copy).then_inc(v_ready, 1)
                act.wait_ge(max_ready, b + 1)
                act.activation(probs[:, :], logits[:, :], ACT.Exp, bias=neg_max[:, 0:1],
                               accum_out=row_sum[:, 0:1]).then_inc(exp_ready, 1)
                act.wait_ge(o_full, b + 1)
                act.activation(oT[:, :], ps_o[:, :], ACT.Copy).then_inc(o_ready, 1)

        @block.tensor
        def _(pe):
            with pe.Fori(0, B) as b:
                pe.wait_ge(y_copied, b + 1)
                for j in range(TPB):
                    pe.matmul(ps_qk[:, j, :, :].rearrange("p w d -> p (w d)"), yT[:, P * j:P * j + P],
                              wT[:, 0:2, :].rearrange("p w d -> p (w d)"), start=True, stop=True)
                pe.matmul(ps_v[:, :], wT[:, 2, :], yT[:, :], start=True, stop=True).then_inc(qkv_full, 1)
                pe.wait_ge(qk_ready, 2 * b + 2)
                for j in range(TPB):
                    last = pe.matmul(ps_g[:, 0:D], qk[:, j, 0, :], qk[:, j, 1, :], start=(j == 0),
                                     stop=(j == TPB - 1))
                last.then_inc(g_full, 1)
                pe.wait_ge(p_ready, b + 1)
                pe.transpose(ps_g[:, 0:D], probs[:, :], ident[:, :]).then_inc(pT_full, 1)
                pe.wait_ge(pT_ready, b + 1)
                pe.wait_ge(v_ready, b + 1)
                pe.matmul(ps_o[:, :], probsT[:, :], vT[:, :], start=True, stop=True).then_inc(o_full, 1)
                pe.wait_ge(o_ready, b + 1)
                for j in range(TPB):
                    last = pe.matmul(ps_out[:, j, :], oT[:, P * j:P * j + P], wT[:, 3, :], start=True, stop=True)
                last.then_inc(out_full, 1)
                pe.wait_ge(x_added, b + 1)


def normalized_weights(nc, tag, wT, ident, dram):
    with ExitStack() as ctx:
        new = Pool_(nc, ctx, tag)
        w = new.sb("w", [P, 4, D])
        gain = new.sb("gain", [P, 1])
        sq = new.sb("sq", [P, 4, D])
        norm = new.sb("norm", [P, 4])
        ps_w = new.ps("ps_w", [P, 4, P])
        (loaded, squared, summed, rooted, chain, scaled, turned) = (new.sem(n) for n in (
            "loaded", "squared", "summed", "rooted", "chain", "scaled", "turned"))
        block = ctx.enter_context(nc.Block())

        @block.sync
        def _(sp):
            sp.dma_start(w[:, :, :], dram["b_w"].rearrange("n o e -> o n e")).then_inc(loaded, 16)
            sp.dma_start(gain[:, :], dram["b_gain"].partition_broadcast(P)).then_inc(loaded, 16)

        @block.scalar
        def _(act):
            act.wait_ge(summed, 1)
            act.activation(norm[:, :], norm[:, :], ACT.Sqrt).then_inc(rooted, 1)

        @block.vector
        def _(dve):
            dve.wait_ge(loaded, 32)
            dve.tensor_tensor(sq[:, :, :], w[:, :, :], w[:, :, :], ALU.mult).then_inc(squared, 1)
            dve.wait_ge(squared, 1)
            dve.tensor_reduce(norm[:, :], sq[:, :, :], AX.X, ALU.add).then_inc(summed, 1)
            dve.wait_ge(rooted, 1)
            dve.tensor_scalar(norm[:, :], norm[:, :], float(1.0 / np.sqrt(D)), MP_EPS, ALU.mult,
                              ALU.add).then_inc(chain, 1)
            dve.wait_ge(chain, 1)
            dve.reciprocal(norm[:, :], norm[:, :]).then_inc(chain, 1)
            dve.wait_ge(chain, 2)
            dve.tensor_scalar(norm[:, :], norm[:, :], gain[:, 0:1], float(1.0 / np.sqrt(D)), ALU.mult,
                              ALU.mult).then_inc(chain, 1)
            dve.wait_ge(chain, 3)
            for n in range(4):
                dve.tensor_scalar(w[:, n, :], w[:, n, :], norm[:, n:n + 1], None, ALU.mult).then_inc(scaled, 1)
            dve.wait_ge(turned, 1)
            dve.tensor_copy(wT[:, :, :], ps_w[:, :, :])

        @block.tensor
        def _(pe):
            pe.wait_ge(scaled, 4)
            for n in range(4):
                last = pe.transpose(ps_w[:, n, :], w[:, n, :], ident[:, :])
            last.then_inc(turned, 1)


HALF_WIN, WIN = 32, 64
BAND = P + 2 * HALF_WIN
GLOBALS = S // WIN
DH_W = D // HEADS


def window_attention(nc, tag, X, Y, ident, identb, dram):
    SPAN = S + 2 * HALF_WIN
    SCALE = float(DH_W) ** -0.5
    with ExitStack() as ctx:
        new = Pool_(nc, ctx, tag)
        YT = new.sb("YT", [P, NT, P])
        transpose_stream(nc, tag + "_turn", Y, YT, ident)
        padded = new.sb("padded", [P, B, SPAN])
        w_qkv = new.sb("w_qkv", [P, 3, D])
        w_out = new.sb("w_out", [P, D])
        bias = new.sb("bias", [P, D])
        head_mask = new.sb("head_mask", [P, HEADS, GLOBALS])
        mask = new.sb("mask", [P, 3, BAND], BF16)
        band = new.sb("band", [P, BAND])
        global_rep = new.sb("global_rep", [P, HEADS, GLOBALS])
        qT = new.sb("qT", [P, P])
        q_heads = new.sb("q_heads", [P, HEADS, P])
        kT = new.sb("kT", [P, BAND])
        vA = new.sb("vA", [P, D])
        vB = new.sb("vB", [WIN, D])
        kg = new.sb("kg", [P, HEADS, GLOBALS])
        vg = new.sb("vg", [P, HEADS, DH_W])
        neg_max = new.sb("neg_max", [P, 2, 2])
        row_sum = new.sb("row_sum", [P, HEADS])
        probs = new.sb("probs", [P, 2, 2, BAND])
        probsT = new.sb("probsT", [P, 2, 512])
        g_max = new.sb("g_max", [P, HEADS])
        g_sum = new.sb("g_sum", [P, HEADS])
        g_probs = new.sb("g_probs", [P, HEADS, GLOBALS])
        g_probsT = new.sb("g_probsT", [P, P])
        o_local = new.sb("o_local", [P, HEADS, DH_W])
        o_global = new.sb("o_global", [P, HEADS, DH_W])
        oT = new.sb("oT", [P, P])
        ps_s = [new.ps(f"ps_s{n}", [P, 512]) for n in range(2)]
        ps_pT = [new.ps(f"ps_pT{n}", [P, 512]) for n in range(2)]
        ps_o = new.ps("ps_o", [P, 512])
        ps_a = new.ps("ps_a", [P, 512])
        ps_b = new.ps("ps_b", [P, 512])
        ps_c = new.ps("ps_c", [P, 512])
        (loaded, made, padding, filled, zeroed) = (new.sem(n) for n in (
            "loaded", "made", "padding", "filled", "zeroed"))
        (band_ready, q_full, kv_full, vg_full, kv_ready, q_ready, heads_ready, vg_ready, kg_ready, lg_full, g_chain, g_max_ready,
         g_shifted, g_exp_ready, gT_full, gT_ready, og_full) = (new.sem(n) for n in (
             "band_ready", "q_full", "kv_full", "vg_full", "kv_ready", "q_ready", "heads_ready", "vg_ready", "kg_ready",
             "lg_full", "g_chain", "g_max_ready", "g_shifted", "g_exp_ready", "gT_full", "gT_ready", "og_full"))
        (s_full, max_ready, exp_ready, pT_full, pT_ready, pv_done, inverted, local_ready, global_ready, summed, oT_full,
         oT_ready, out_full, x_added) = (new.sem(n) for n in (
             "s_full", "max_ready", "exp_ready", "pT_full", "pT_ready", "pv_done", "inverted", "local_ready",
             "global_ready", "summed", "oT_full", "oT_ready", "out_full", "x_added"))
        block = ctx.enter_context(nc.Block())

        @block.sync
        def _(sp):
            sp.dma_start(w_qkv[:, :, :].rearrange("p a d -> p (a d)"), dram["w_qkv"]).then_inc(loaded, 16)
            sp.dma_start(w_out[:, :], dram["w_out"]).then_inc(loaded, 16)
            sp.dma_start(bias[:, :], dram["w_bias"].partition_broadcast(P)).then_inc(loaded, 16)

        @block.gpsimd
        def _(pool):
            block_diagonal(pool, head_mask[:, :, :], DH_W, made, 1.0, 0.0)
            pool.memset(mask[:, :, :], 0.0).then_inc(filled, 1)
            pool.wait_ge(filled, 1)
            pool.affine_select(out=mask[:, :, :], in_=mask[:, :, :], compare_op=ALU.is_ge, fill=NEG, base=0,
                               pattern=[[0, 3], [1, BAND]], channel_multiplier=-1).then_inc(filled, 1)
            pool.wait_ge(filled, 2)
            pool.affine_select(out=mask[:, :, :], in_=mask[:, :, :], compare_op=ALU.is_ge, fill=NEG, base=WIN - 1,
                               pattern=[[0, 3], [-1, BAND]], channel_multiplier=1).then_inc(filled, 1)
            pool.wait_ge(filled, 3)
            pool.memset(mask[:, 0, 0:HALF_WIN], NEG).then_inc(filled, 1)
            pool.memset(mask[:, 2, BAND - HALF_WIN:BAND], NEG).then_inc(filled, 1)
            pool.wait_ge(made, 3)
            with pool.Fori(0, NT) as i:
                pool.wait_ge(q_ready, i + 1)
                pool.tensor_tensor(q_heads[:, :, :], qT[:, :].unsqueeze(1).to_broadcast([P, HEADS, P]),
                                   head_mask[:, :, 0:1].to_broadcast([P, HEADS, P]), ALU.mult).then_inc(heads_ready, 1)

        @block.vector
        def _(dve):
            dve.memset(padded[:, :, 0:HALF_WIN], 0.0).then_inc(padding, 1)
            dve.memset(padded[:, :, S + HALF_WIN:SPAN], 0.0).then_inc(padding, 1)
            for n in range(2):
                dve.memset(ps_pT[n][:, :], 0.0).then_inc(zeroed, 1)
            dve.tensor_copy(padded[:, :, HALF_WIN:S + HALF_WIN].rearrange("p b (j t) -> p b j t", t=P),
                            YT[:, :, :].rearrange("p (b j) t -> p b j t", b=B)).then_inc(padding, 1)
            dve.wait_ge(loaded, 48)
            dve.wait_ge(made, 3)
            dve.wait_ge(padding, 3)

            def pair(i, c):
                n = PAIRS * i + c
                dve.wait_ge(s_full, n + 1)
                dve.tensor_reduce(neg_max[:, c % 2, :], ps_s[c % 2][:, 0:2 * BAND].rearrange(
                    "p (h k) -> p h k", k=BAND), AX.X, ALU.max, negate=True).then_inc(max_ready, 1)

            def copy_pT(i, c):
                n = PAIRS * i + c
                dve.wait_ge(pT_full, n + 1)
                dve.tensor_copy(probsT[:, c % 2, :], ps_pT[c % 2][:, :]).then_inc(pT_ready, 1)

            with dve.Fori(0, NT) as i:
                b, j = i // TPB, i % TPB
                tile_ = (i // TPB) * (TPB + 1) + i % TPB + 1
                dve.tensor_copy(band[:, :], padded[:, b, bass.ds(P * j, BAND)])
                dve.tensor_copy(global_rep[:, :, :], padded[:, b, bass.ds(HALF_WIN, GLOBALS, WIN)].unsqueeze(1)
                                .to_broadcast([P, HEADS, GLOBALS])).then_inc(band_ready, 1)
                dve.wait_ge(kv_full, i + 1)
                dve.tensor_copy(kT[:, :], ps_b[:, 0:BAND])
                dve.tensor_copy(vA[:, :], ps_b[:, 192:320])
                dve.tensor_copy(vB[:, :], ps_b[0:WIN, 320:448]).then_inc(kv_ready, 1)
                dve.wait_ge(vg_full, i + 1)
                dve.tensor_tensor(vg[:, :, :], ps_c[:, 0:D].rearrange("p (n e) -> p n e", e=DH_W),
                                  head_mask[:, :, :], ALU.mult)
                dve.tensor_tensor(kg[:, :, :], ps_c[:, 128:136].unsqueeze(1).to_broadcast([P, HEADS, GLOBALS]),
                                  head_mask[:, :, :], ALU.mult).then_inc(kg_ready, 1)
                pair(i, 0)
                pair(i, 1)
                dve.wait_ge(lg_full, i + 1)
                lg = ps_a[:, 0:P].rearrange("p (n g) -> p n g", g=GLOBALS)
                dve.tensor_reduce(g_max[:, :], lg, AX.X, ALU.max, negate=True).then_inc(g_max_ready, 1)
                dve.wait_ge(g_max_ready, i + 1)
                dve.tensor_tensor(g_probs[:, :, :], lg, g_max[:, :].unsqueeze(2).to_broadcast(
                    [P, HEADS, GLOBALS]), ALU.add).then_inc(g_shifted, 1)
                copy_pT(i, 0)
                pair(i, 2)
                dve.wait_ge(g_exp_ready, i + 1)
                dve.tensor_reduce(g_sum[:, :], g_probs[:, :, :], AX.X, ALU.add).then_inc(g_chain, 1)
                for c in range(3, PAIRS):
                    copy_pT(i, c - 2)
                    pair(i, c)
                copy_pT(i, PAIRS - 2)
                copy_pT(i, PAIRS - 1)
                dve.wait_ge(gT_full, i + 1)
                dve.tensor_copy(g_probsT[:, :], ps_a[:, 128:256]).then_inc(gT_ready, 1)
                dve.reciprocal(row_sum[:, :], row_sum[:, :])
                dve.wait_ge(g_chain, 2 * i + 1)
                dve.reciprocal(g_sum[:, :], g_sum[:, :]).then_inc(g_chain, 1)
                dve.wait_ge(g_chain, 2 * i + 2)
                dve.wait_ge(pv_done, PAIRS * i + PAIRS)
                dve.tensor_tensor(o_local[:, :, :], ps_o[:, 0:D].rearrange("p (n e) -> p n e", e=DH_W),
                                  row_sum[:, :].unsqueeze(2).to_broadcast([P, HEADS, DH_W]),
                                  ALU.mult).then_inc(local_ready, 1)
                dve.wait_ge(og_full, i + 1)
                dve.tensor_tensor(o_global[:, :, :], ps_a[:, 256:384].rearrange("p (n e) -> p n e", e=DH_W),
                                  g_sum[:, :].unsqueeze(2).to_broadcast([P, HEADS, DH_W]),
                                  ALU.mult).then_inc(global_ready, 1)
                dve.wait_ge(global_ready, i + 1)
                dve.tensor_tensor(o_local[:, :, :], o_local[:, :, :], o_global[:, :, :],
                                  ALU.add).then_inc(summed, 1)
                dve.wait_ge(oT_full, i + 1)
                dve.tensor_copy(oT[:, :], ps_a[:, 384:512]).then_inc(oT_ready, 1)
                dve.tensor_tensor(X[:, tile_, :], X[:, tile_, :], bias[:, :], ALU.add).then_inc(inverted, 1)
                dve.wait_ge(out_full, i + 1)
                dve.wait_ge(inverted, i + 1)
                dve.tensor_tensor(X[:, tile_, :], X[:, tile_, :], ps_c[:, 256:384], ALU.add).then_inc(x_added, 1)

        @block.scalar
        def _(act):
            def exps(i, c):
                n = PAIRS * i + c
                act.wait_ge(max_ready, n + 1)
                if c >= 2:
                    act.wait_ge(pT_full, n - 1)
                for h in range(2):
                    act.activation(probs[:, c % 2, h, :], ps_s[c % 2][:, h * BAND:(h + 1) * BAND], ACT.Exp,
                                   bias=neg_max[:, c % 2, h:h + 1],
                                   accum_out=row_sum[:, 2 * c + h:2 * c + h + 1]).then_inc(exp_ready, 1)

            with act.Fori(0, NT) as i:
                act.wait_ge(q_full, i + 1)
                act.activation(qT[:, :], ps_a[:, 0:P], ACT.Copy, scale=SCALE).then_inc(q_ready, 1)
                exps(i, 0)
                exps(i, 1)
                act.wait_ge(g_shifted, i + 1)
                act.activation(g_probs[:, :, :], g_probs[:, :, :], ACT.Exp).then_inc(g_exp_ready, 1)
                for c in range(2, PAIRS):
                    exps(i, c)

        @block.tensor
        def _(pe):
            pe.wait_ge(loaded, 48)
            pe.wait_ge(filled, 5)
            pe.wait_ge(zeroed, 2)

            def scores(i, c):
                n = PAIRS * i + c
                if c >= 2:
                    pe.wait_ge(exp_ready, 2 * n - 2)
                dst = ps_s[c % 2][:, 0:2 * BAND]
                variant = (i % TPB + 1) // 2
                pe.matmul(dst, identb[:, :], mask[:, variant, :].unsqueeze(1).to_broadcast([P, 2, BAND]),
                          start=True, stop=False)
                for h in range(2):
                    last = pe.matmul(dst[:, h * BAND:(h + 1) * BAND], q_heads[:, 2 * c + h, :], kT[:, :],
                                     start=False, stop=(h == 1))
                last.then_inc(s_full, 1)

            def turn(i, c):
                n = PAIRS * i + c
                pe.wait_ge(exp_ready, 2 * n + 2)
                if c >= 2:
                    pe.wait_ge(pT_ready, n - 1)
                for h in range(2):
                    pe.transpose(ps_pT[c % 2][:, h * P:(h + 1) * P], probs[:, c % 2, h, 0:P], ident[:, :])
                for h in range(2):
                    last = pe.transpose(ps_pT[c % 2][0:WIN, (2 + h) * P:(3 + h) * P], probs[:, c % 2, h, P:BAND],
                                        ident[:, :])
                last.then_inc(pT_full, 1)

            def weigh_values(i, c):
                pe.wait_ge(pT_ready, PAIRS * i + c + 1)
                for h in range(2):
                    o = DH_W * (2 * c + h)
                    pe.matmul(ps_o[:, o:o + DH_W], probsT[:, c % 2, h * P:(h + 1) * P], vA[:, o:o + DH_W],
                              start=True, stop=False)
                    last = pe.matmul(ps_o[:, o:o + DH_W], probsT[0:WIN, c % 2, (2 + h) * P:(3 + h) * P],
                                     vB[:, o:o + DH_W], start=False, stop=True)
                last.then_inc(pv_done, 1)

            with pe.Fori(0, NT) as i:
                pe.wait_ge(band_ready, i + 1)
                pe.matmul(ps_a[:, 0:P], w_qkv[:, 0, :], band[:, HALF_WIN:HALF_WIN + P], start=True,
                          stop=True).then_inc(q_full, 1)
                pe.matmul(ps_b[:, 0:BAND], w_qkv[:, 1, :], band[:, :], start=True, stop=True)
                pe.matmul(ps_b[:, 192:320], band[:, 0:P], w_qkv[:, 2, :], start=True, stop=True)
                pe.matmul(ps_b[0:WIN, 320:448], band[:, P:BAND], w_qkv[:, 2, :], start=True,
                          stop=True).then_inc(kv_full, 1)
                pe.matmul(ps_c[:, 0:D], global_rep[:, :, :].rearrange("p n g -> p (n g)"), w_qkv[:, 2, :],
                          start=True, stop=True)
                pe.matmul(ps_c[:, 128:136], w_qkv[:, 1, :], global_rep[:, 0, :], start=True,
                          stop=True).then_inc(vg_full, 1)
                pe.wait_ge(heads_ready, i + 1)
                pe.wait_ge(kv_ready, i + 1)
                scores(i, 0)
                scores(i, 1)
                pe.wait_ge(q_ready, i + 1)
                pe.wait_ge(kg_ready, i + 1)
                pe.matmul(ps_a[:, 0:P], qT[:, :], kg[:, :, :].rearrange("p n g -> p (n g)"), start=True,
                          stop=True).then_inc(lg_full, 1)
                turn(i, 0)
                scores(i, 2)
                for c in range(3, PAIRS):
                    turn(i, c - 2)
                    scores(i, c)
                    weigh_values(i, c - 3)
                turn(i, PAIRS - 2)
                weigh_values(i, PAIRS - 3)
                turn(i, PAIRS - 1)
                weigh_values(i, PAIRS - 2)
                pe.wait_ge(g_exp_ready, i + 1)
                pe.transpose(ps_a[:, 128:256], g_probs[:, :, :].rearrange("p n g -> p (n g)"),
                             ident[:, :]).then_inc(gT_full, 1)
                weigh_values(i, PAIRS - 1)
                pe.wait_ge(gT_ready, i + 1)
                pe.matmul(ps_a[:, 256:384], g_probsT[:, :], vg[:, :, :].rearrange("p n e -> p (n e)"),
                          start=True, stop=True).then_inc(og_full, 1)
                pe.wait_ge(summed, i + 1)
                pe.transpose(ps_a[:, 384:512], o_local[:, :, :].rearrange("p n e -> p (n e)"),
                             ident[:, :]).then_inc(oT_full, 1)
                pe.wait_ge(oT_ready, i + 1)
                pe.matmul(ps_c[:, 256:384], oT[:, :], w_out[:, :], start=True, stop=True).then_inc(out_full, 1)
                pe.wait_ge(x_added, i + 1)


EXPERTS, EXPERT_FF, GROUPS, TOP_GROUPS, TOP_K = 16, 64, 4, 2, 4
PER_GROUP = EXPERTS // GROUPS
BLOCKS = EXPERTS + 2
WIDE = BLOCKS * EXPERT_FF
CHUNKS = 3
CHUNK = WIDE // CHUNKS
TURNS = CHUNK // P


def experts(nc, tag, X, Y, ident, dram):
    LAST = NT * CHUNKS
    with ExitStack() as ctx:
        new = Pool_(nc, ctx, tag)
        YT = new.sb("YT", [P, NT, P])
        transpose_stream(nc, tag + "_turn", Y, YT, ident)
        w_gate = new.sb("w_gate", [P, EXPERTS])
        w_g = new.sb("w_g", [P, WIDE])
        w_u = new.sb("w_u", [P, WIDE])
        w_d = new.sb("w_d", [P, CHUNKS * TURNS, D])
        scores = new.sb("scores", [P, NT, EXPERTS])
        pairs4 = new.sb("pairs4", [P, 6, NT * GROUPS])
        lower = new.sb("lower", [P, EXPERTS, EXPERTS])
        beats = new.sb("beats", [P, NT, EXPERTS, EXPERTS])
        ties = new.sb("ties", [P, NT, EXPERTS, EXPERTS])
        rank = new.sb("rank", [P, NT, EXPERTS])
        open_ = new.sb("open", [P, NT * GROUPS])
        allowed = new.sb("allowed", [P, NT, EXPERTS])
        total = new.sb("total", [P, NT])
        combine = new.sb("combine", [P, NT, BLOCKS])
        yT = new.sb("yT", [P, 2, P])
        silu = new.sb("silu", [P, 2, CHUNK])
        act_ = new.sb("act", [P, 2, CHUNK])
        actT = new.sb("actT", [P, 2, CHUNK])
        ps_g = [new.ps(f"ps_g{n}", [P, 512]) for n in range(2)]
        ps_u = [new.ps(f"ps_u{n}", [P, 512]) for n in range(2)]
        ps_t = [new.ps(f"ps_t{n}", [P, 512]) for n in range(2)]
        ps_out = new.ps("ps_out", [P, 512])
        ps_gate = new.ps("ps_gate", [P, NT * EXPERTS])
        (loaded, made, gate_full, scored, chain, combined, ones) = (new.sem(n) for n in (
            "loaded", "made", "gate_full", "scored", "chain", "combined", "ones"))
        (yT_ready, g_full, u_full, silu_ready, act_ready, weighted, t_full, t_ready, down_done,
         x_added) = (new.sem(n) for n in ("yT_ready", "g_full", "u_full", "silu_ready", "act_ready", "weighted",
                                          "t_full", "t_ready", "down_done", "x_added"))
        block = ctx.enter_context(nc.Block())

        def run(step, eng):
            step(0, True)
            with eng.Fori(1, NT // 2) as s:
                step(s, False)

        @block.sync
        def _(sp):
            sp.dma_start(w_gate[:, :], dram["m_gate"]).then_inc(loaded, 16)
            sp.dma_start(w_g[:, :], dram["m_g"]).then_inc(loaded, 16)
            sp.dma_start(w_u[:, :], dram["m_u"]).then_inc(loaded, 16)
            sp.dma_start(w_d[:, :, :], dram["m_d"].rearrange("(c p) d -> p c d", p=P)).then_inc(loaded, 16)

        @block.gpsimd
        def _(pool):
            pool.memset(lower[:, :, :], 1.0).then_inc(made, 1)
            pool.wait_ge(made, 1)
            pool.affine_select(out=lower[:, :, :], in_=lower[:, :, :], compare_op=ALU.is_gt, fill=0.0, base=0,
                               pattern=[[1, EXPERTS], [-1, EXPERTS]], channel_multiplier=0).then_inc(made, 1)
            pool.memset(combine[:, :, EXPERTS:BLOCKS], 1.0).then_inc(made, 1)
            pool.wait_ge(made, 3)
            pool.wait_ge(combined, 1)

            def step(s, first):
                for k in range(2 * CHUNKS):
                    n = 2 * CHUNKS * s + k
                    i, c, b = 2 * s + k // CHUNKS, k % CHUNKS, k % 2
                    wait(pool, act_ready, n + 1)
                    view = act_[:, b, :].rearrange("p (e f) -> p e f", f=EXPERT_FF)
                    e = CHUNK // EXPERT_FF
                    pool.tensor_tensor(view, view, combine[:, i, e * c:e * c + e].unsqueeze(2).to_broadcast(
                        [P, e, EXPERT_FF]), ALU.mult).then_inc(weighted, 1)

            run(step, pool)

        @block.vector
        def _(dve):
            links = [0]

            def link(ins):
                links[0] += 1
                ins.then_inc(chain, 1)
                dve.wait_ge(chain, links[0])

            dve.wait_ge(scored, 1)
            dve.wait_ge(made, 3)
            a, b_, c_, d_ = (scores[:, :, :].rearrange("p t (g k) -> p (t g) k", k=PER_GROUP)[:, :, k]
                             for k in range(PER_GROUP))
            dve.tensor_tensor(pairs4[:, 0, :], a, b_, ALU.max)
            dve.tensor_tensor(pairs4[:, 1, :], a, b_, ALU.min)
            dve.tensor_tensor(pairs4[:, 2, :], c_, d_, ALU.max)
            link(dve.tensor_tensor(pairs4[:, 3, :], c_, d_, ALU.min))
            dve.tensor_tensor(pairs4[:, 4, :], pairs4[:, 0, :], pairs4[:, 2, :], ALU.max)
            link(dve.tensor_tensor(pairs4[:, 5, :], pairs4[:, 0, :], pairs4[:, 2, :], ALU.min))
            link(dve.tensor_tensor(pairs4[:, 1, :], pairs4[:, 1, :], pairs4[:, 3, :], ALU.max))
            link(dve.tensor_tensor(pairs4[:, 5, :], pairs4[:, 5, :], pairs4[:, 1, :], ALU.max))
            link(dve.tensor_tensor(pairs4[:, 4, :], pairs4[:, 4, :], pairs4[:, 5, :], ALU.add))

            def ranks(values, n, out):
                own = values.unsqueeze(3).to_broadcast([P, NT, n, n])
                rival = values.unsqueeze(2).to_broadcast([P, NT, n, n])
                dve.tensor_tensor(beats[:, :, 0:n, 0:n], rival, own, ALU.is_gt)
                link(dve.tensor_tensor(ties[:, :, 0:n, 0:n], rival, own, ALU.is_equal))
                link(dve.tensor_tensor(ties[:, :, 0:n, 0:n], ties[:, :, 0:n, 0:n],
                                       lower[:, 0:n, 0:n].unsqueeze(1).to_broadcast([P, NT, n, n]), ALU.mult))
                link(dve.tensor_tensor(beats[:, :, 0:n, 0:n], beats[:, :, 0:n, 0:n], ties[:, :, 0:n, 0:n], ALU.add))
                link(dve.tensor_reduce(out, beats[:, :, 0:n, 0:n], AX.X, ALU.add))

            ranks(pairs4[:, 4, :].rearrange("p (t g) -> p t g", g=GROUPS), GROUPS,
                  open_[:, :].rearrange("p (t g) -> p t g", g=GROUPS))
            link(dve.tensor_scalar(open_[:, :], open_[:, :], float(TOP_GROUPS), None, ALU.is_lt))
            flat = "p t (g k) -> p (t g) k"
            wide = open_[:, :].unsqueeze(2).to_broadcast([P, NT * GROUPS, PER_GROUP])
            link(dve.tensor_tensor(allowed[:, :, :].rearrange(flat, k=PER_GROUP),
                                   scores[:, :, :].rearrange(flat, k=PER_GROUP), wide, ALU.mult))
            link(dve.tensor_tensor(allowed[:, :, :].rearrange(flat, k=PER_GROUP),
                                   allowed[:, :, :].rearrange(flat, k=PER_GROUP), wide, ALU.add))
            ranks(allowed[:, :, :], EXPERTS, rank[:, :, :])
            link(dve.tensor_scalar(rank[:, :, :], rank[:, :, :], float(TOP_K), None, ALU.is_lt))
            link(dve.tensor_tensor(rank[:, :, :], rank[:, :, :], scores[:, :, :], ALU.mult))
            link(dve.tensor_reduce(total[:, :], rank[:, :, :], AX.X, ALU.add))
            link(dve.tensor_scalar(total[:, :], total[:, :], 1e-6, None, ALU.add))
            link(dve.reciprocal(total[:, :], total[:, :]))
            dve.tensor_tensor(combine[:, :, 0:EXPERTS], rank[:, :, :],
                              total[:, :].unsqueeze(2).to_broadcast([P, NT, EXPERTS]), ALU.mult).then_inc(combined, 1)

            def turned(n, b):
                wait(dve, t_full, n + 1)
                wait(dve, down_done, n - 1)
                dve.tensor_copy(actT[:, b, :], ps_t[b][:, 0:CHUNK]).then_inc(t_ready, 1)

            def add(i, tile_):
                wait(dve, down_done, CHUNKS * i + CHUNKS)
                dve.tensor_tensor(X[:, tile_, :], X[:, tile_, :], ps_out[:, 0:D], ALU.add).then_inc(x_added, 1)

            def tile_of(i):
                return (i // TPB) * (TPB + 1) + i % TPB + 1

            def step(s, first):
                for k in range(2 * CHUNKS):
                    n, b = 2 * CHUNKS * s + k, k % 2
                    wait(dve, u_full, n + 1)
                    wait(dve, silu_ready, n + 1)
                    wait(dve, t_full, n - 1)
                    dve.tensor_tensor(act_[:, b, :], silu[:, b, :], ps_u[b][:, 0:CHUNK], ALU.mult).then_inc(act_ready, 1)
                    if not (first and k == 0):
                        turned(n - 1, 1 - b)
                    if k == 2 and not first:
                        add(2 * s - 1, tile_of(2 * s - 1))
                    if k == 5:
                        add(2 * s, tile_of(2 * s))

            run(step, dve)
            turned(LAST - 1, 1)
            add(NT - 1, tile_of(NT - 1))

        @block.scalar
        def _(act):
            act.wait_ge(gate_full, 1)
            act.activation(scores[:, :, :].rearrange("p t e -> p (t e)"), ps_gate[:, :], ACT.Sigmoid).then_inc(scored, 1)

            def step(s, first):
                for k in range(2 * CHUNKS):
                    n, b = 2 * CHUNKS * s + k, k % 2
                    if k % CHUNKS == 0:
                        i, p = 2 * s + k // CHUNKS, k // CHUNKS
                        wait(act, u_full, CHUNKS * (i - 1))
                        act.activation(yT[:, p, :], YT[:, i, :], ACT.Copy).then_inc(yT_ready, 1)
                    wait(act, g_full, n + 1)
                    wait(act, act_ready, n - 1)
                    act.activation(silu[:, b, :], ps_g[b][:, 0:CHUNK], ACT.Silu).then_inc(silu_ready, 1)

            run(step, act)

        @block.tensor
        def _(pe):
            pe.wait_ge(loaded, 64)
            for i in range(NT):
                last = pe.matmul(ps_gate[:, EXPERTS * i:EXPERTS * i + EXPERTS], YT[:, i, :], w_gate[:, :],
                                 start=True, stop=True)
            last.then_inc(gate_full, 1)

            def turn(n, b):
                wait(pe, weighted, n + 1)
                wait(pe, t_ready, n - 1)
                for k in range(TURNS):
                    last = pe.transpose(ps_t[b][:, P * k:P * k + P], act_[:, b, P * k:P * k + P], ident[:, :])
                last.then_inc(t_full, 1)

            def down(n, c, i, b):
                wait(pe, t_ready, n + 1)
                if c == 0:
                    wait(pe, x_added, i)
                for k in range(TURNS):
                    last = pe.matmul(ps_out[:, 0:D], actT[:, b, P * k:P * k + P], w_d[:, TURNS * c + k, :],
                                     start=(c == 0 and k == 0), stop=(c == CHUNKS - 1 and k == TURNS - 1))
                last.then_inc(down_done, 1)

            def step(s, first):
                for k in range(2 * CHUNKS):
                    n, b = 2 * CHUNKS * s + k, k % 2
                    i, p, c = 2 * s + k // CHUNKS, k // CHUNKS, k % CHUNKS
                    wait(pe, yT_ready, i + 1)
                    wait(pe, silu_ready, n - 1)
                    pe.matmul(ps_g[b][:, 0:CHUNK], yT[:, p, :], w_g[:, CHUNK * c:CHUNK * c + CHUNK],
                              start=True, stop=True).then_inc(g_full, 1)
                    wait(pe, act_ready, n - 1)
                    pe.matmul(ps_u[b][:, 0:CHUNK], yT[:, p, :], w_u[:, CHUNK * c:CHUNK * c + CHUNK],
                              start=True, stop=True).then_inc(u_full, 1)
                    if not (first and k == 0):
                        turn(n - 1, 1 - b)
                    if not (first and k <= 1):
                        m = k - 2
                        down(n - 2, m % CHUNKS, 2 * s + m // CHUNKS, b)

            run(step, pe)
            turn(LAST - 1, 1)
            down(LAST - 2, 1, NT - 1, 0)
            down(LAST - 1, 2, NT - 1, 1)


def time_attention(nc, tag, X, Y, ident, dram):
    T = B
    with ExitStack() as ctx:
        new = Pool_(nc, ctx, tag)
        YT = new.sb("YT", [P, NT, P])
        transpose_stream(nc, tag + "_turn", Y, YT, ident)
        w = new.sb("w", [P, D])
        proj = new.sb("proj", [P, D])
        w_cat = new.sb("w_cat", [P, 2, D])
        bias = new.sb("bias", [P, D])
        yT = new.sb("yT", [P, T, P])
        hp = new.sb("hp", [P, T - 1, D])
        score = new.sb("score", [P, T - 1])
        neg_max = new.sb("neg_max", [P, 2])
        prob = new.sb("prob", [P, 2, T - 1])
        total = new.sb("total", [P, 2])
        context = new.sb("context", [P, 2, D])
        contextT = new.sb("contextT", [P, 2, P])
        res = new.sb("res", [P, 2, D])
        ps_h = new.ps("ps_h", [P, T - 1, D])
        ps_c = new.ps("ps_c", [P, 2, P])
        ps_out = new.ps("ps_out", [P, 2, D])
        (loaded, y_copied, h_full, tanh_ready, chain, max_ready, exp_ready, c_ready, cT_full, cT_ready, out_full,
         biased, out_ready, done) = (new.sem(n) for n in (
             "loaded", "y_copied", "h_full", "tanh_ready", "chain", "max_ready", "exp_ready", "c_ready", "cT_full",
             "cT_ready", "out_full", "biased", "out_ready", "done"))
        block = ctx.enter_context(nc.Block())
        CHAIN = 11

        @block.sync
        def _(sp):
            sp.dma_start(w[:, :], dram["t_w"]).then_inc(loaded, 16)
            sp.dma_start(proj[:, :], dram["t_proj"].partition_broadcast(P)).then_inc(loaded, 16)
            sp.dma_start(w_cat[:, :, :], dram["t_cat"].rearrange("(a p) h -> p a h", p=P)).then_inc(loaded, 16)
            sp.dma_start(bias[:, :], dram["t_bias"].partition_broadcast(P)).then_inc(loaded, 16)

        @block.vector
        def _(dve):
            dve.wait_ge(loaded, 64)
            with dve.Fori(0, TPB) as j:
                links = [0]

                def link(ins):
                    links[0] += 1
                    ins.then_inc(chain, 1)
                    dve.wait_ge(chain, CHAIN * j + links[0])

                dve.tensor_copy(yT[:, :, :], YT[:, bass.ds(j, T, TPB), :]).then_inc(y_copied, 1)
                dve.wait_ge(tanh_ready, j + 1)
                link(dve.tensor_tensor(hp[:, :, :], hp[:, :, :],
                                       proj[:, :].unsqueeze(1).to_broadcast([P, T - 1, D]), ALU.mult))
                link(dve.tensor_reduce(score[:, :], hp[:, :, :], AX.X, ALU.add))
                dve.tensor_reduce(neg_max[:, 0:1], score[:, 0:2], AX.X, ALU.max, negate=True)
                dve.tensor_reduce(neg_max[:, 1:2], score[:, 0:3], AX.X, ALU.max, negate=True).then_inc(max_ready, 1)
                dve.wait_ge(exp_ready, j + 1)
                link(dve.reciprocal(total[:, :], total[:, :]))
                link(dve.tensor_tensor(prob[:, :, :], prob[:, :, :],
                                       total[:, :].unsqueeze(2).to_broadcast([P, 2, T - 1]), ALU.mult))
                link(dve.tensor_scalar(context[:, 0, :], Y[:, 1 + j, :], prob[:, 0, 0:1], None, ALU.mult))
                link(dve.tensor_scalar(context[:, 1, :], Y[:, 1 + j, :], prob[:, 1, 0:1], None, ALU.mult))
                link(dve.scalar_tensor_tensor(out=context[:, 0, :], in0=Y[:, 6 + j, :], scalar=prob[:, 0, 1:2],
                                              in1=context[:, 0, :], op0=ALU.mult, op1=ALU.add))
                link(dve.scalar_tensor_tensor(out=context[:, 1, :], in0=Y[:, 6 + j, :], scalar=prob[:, 1, 1:2],
                                              in1=context[:, 1, :], op0=ALU.mult, op1=ALU.add))
                link(dve.scalar_tensor_tensor(out=context[:, 1, :], in0=Y[:, 11 + j, :], scalar=prob[:, 1, 2:3],
                                              in1=context[:, 1, :], op0=ALU.mult, op1=ALU.add))
                dve.tensor_tensor(X[:, 1 + j, :], X[:, 1 + j, :], Y[:, 1 + j, :], ALU.add)
                link(dve.tensor_tensor(X[:, 6 + j, :], X[:, 6 + j, :], Y[:, 6 + j, :], ALU.add))
                dve.wait_ge(cT_full, j + 1)
                dve.tensor_copy(contextT[:, :, :], ps_c[:, :, :]).then_inc(cT_ready, 1)
                dve.wait_ge(out_full, j + 1)
                dve.tensor_tensor(res[:, :, :], ps_out[:, :, :], bias[:, :].unsqueeze(1).to_broadcast([P, 2, D]),
                                  ALU.add).then_inc(biased, 1)
                dve.wait_ge(out_ready, j + 1)
                dve.tensor_tensor(X[:, 11 + j, :], X[:, 11 + j, :], res[:, 0, :], ALU.add)
                link(dve.tensor_tensor(X[:, 16 + j, :], X[:, 16 + j, :], res[:, 1, :], ALU.add))
                assert links[0] == CHAIN

        @block.scalar
        def _(act):
            with act.Fori(0, TPB) as j:
                act.wait_ge(h_full, j + 1)
                act.activation(hp[:, :, :], ps_h[:, :, :], ACT.Tanh).then_inc(tanh_ready, 1)
                act.wait_ge(max_ready, j + 1)
                act.activation(prob[:, 0, 0:2], score[:, 0:2], ACT.Exp, bias=neg_max[:, 0:1],
                               accum_out=total[:, 0:1])
                act.activation(prob[:, 0, 2:3], score[:, 2:3], ACT.Copy, scale=0.0)
                act.activation(prob[:, 1, :], score[:, :], ACT.Exp, bias=neg_max[:, 1:2],
                               accum_out=total[:, 1:2]).then_inc(exp_ready, 1)
                act.wait_ge(biased, j + 1)
                act.activation(res[:, :, :], res[:, :, :], ACT.Tanh).then_inc(out_ready, 1)

        @block.tensor
        def _(pe):
            pe.wait_ge(loaded, 64)
            with pe.Fori(0, TPB) as j:
                pe.wait_ge(y_copied, j + 1)
                for t in range(T - 1):
                    last = pe.matmul(ps_h[:, t, :], yT[:, t, :], w[:, :], start=True, stop=True)
                last.then_inc(h_full, 1)
                pe.wait_ge(chain, CHAIN * j + 9)
                for n in range(2):
                    last = pe.transpose(ps_c[:, n, :], context[:, n, :], ident[:, :])
                last.then_inc(cT_full, 1)
                pe.wait_ge(cT_ready, j + 1)
                for n in range(2):
                    pe.matmul(ps_out[:, n, :], yT[:, 2 + n, :], w_cat[:, 0, :], start=True, stop=False)
                    last = pe.matmul(ps_out[:, n, :], contextT[:, n, :], w_cat[:, 1, :], start=False, stop=True)
                last.then_inc(out_full, 1)


def load_stream(nc, x, X, ident, identb):
    with ExitStack() as ctx:
        new = Pool_(nc, ctx, "load")
        loaded, made = new.sem("loaded"), new.sem("made")
        block = ctx.enter_context(nc.Block())

        @block.sync
        def _(sp):
            for b in range(B):
                sp.dma_start(X[:, 5 * b + 1:5 * b + 5, :],
                             x[b].rearrange("(j p) d -> p j d", p=P)).then_inc(loaded, 16)
            sp.wait_ge(loaded, 16 * B)

        @block.gpsimd
        def _(pool):
            pool.memset(ident[:, :], 0.0).then_inc(made, 1)
            pool.wait_ge(made, 1)
            pool.affine_select(out=ident[:, :], in_=ident[:, :], compare_op=ALU.not_equal, fill=1.0, base=0,
                               pattern=[[-1, P]], channel_multiplier=1).then_inc(made, 1)
            pool.wait_ge(made, 2)
            pool.tensor_copy(identb[:, :], ident[:, :])

        @block.vector
        def _(dve):
            for b in range(B):
                dve.memset(X[:, 5 * b, :], 0.0)


def store_stream(nc, X, out):
    with ExitStack() as ctx:
        stored = Pool_(nc, ctx, "store").sem("stored")
        block = ctx.enter_context(nc.Block())

        @block.sync
        def _(sp):
            for b in range(B):
                sp.dma_start(out[b].rearrange("(j p) d -> p j d", p=P),
                             X[:, 5 * b + 1:5 * b + 5, :]).then_inc(stored, 16)
            sp.wait_ge(stored, 16 * B)


STAGES = ["attn_a", "ffn0", "attn_b", "ffn1", "window", "moe0", "attn_t", "moe1"]


def lay_out_others(a, np):
    laid = {}
    q, k, v = (np.transpose(a[f"L0_attn_a_{n}"], (1, 2, 0)).reshape(D, PAIRS, 1, P) for n in "QKV")
    laid["a_qkv"] = np.transpose(np.concatenate([q, k, v], 2), (1, 0, 2, 3))
    laid["a_out"] = np.transpose(a["L0_attn_a_W"], (2, 1, 0)).reshape(PAIRS, P, D)
    laid["b_w"] = np.stack([a[f"L0_attn_b_w_{n}"] for n in "qkvo"], 0)
    laid["b_gain"] = a["L0_attn_b_gain"].reshape(1)
    laid["w_qkv"] = a["L1_attn_a_w_qkv"]
    laid["w_out"] = a["L1_attn_a_w_out"]
    laid["w_bias"] = a["L1_attn_a_b_out"]
    laid["m_gate"] = a["L1_ffn_w_gate"].T
    for n, name in (("g", "w1"), ("u", "w3")):
        routed = a[f"L1_ffn_{name}_e"].reshape(EXPERTS * EXPERT_FF, D)
        laid[f"m_{n}"] = np.concatenate([routed, a[f"L1_ffn_{name}_s"]], 0).T
    routed = np.transpose(a["L1_ffn_w2_e"], (0, 2, 1)).reshape(EXPERTS * EXPERT_FF, D)
    laid["m_d"] = np.concatenate([routed, a["L1_ffn_w2_s"].T], 0)
    laid["t_w"] = a["L1_attn_b_W"]
    laid["t_proj"] = a["L1_attn_b_proj"]
    laid["t_cat"] = a["L1_attn_b_concat_w"].T
    laid["t_bias"] = a["L1_attn_b_concat_b"]
    return laid


def build(nc, dram, out):
    with ExitStack() as ctx:
        new = Pool_(nc, ctx, "all")
        X = new.sb("X", [P, B * (TPB + 1), D])
        Y = new.sb("Y", [P, B * (TPB + 1), D])
        ident = new.sb("ident", [P, P])
        identb = new.sb("identb", [P, P], BF16)
        load_stream(nc, dram["x"], X, ident, identb)
        with ExitStack() as zero_ctx:
            block = zero_ctx.enter_context(nc.Block())

            @block.gpsimd
            def _(pool):
                for b in range(B):
                    pool.memset(Y[:, 5 * b, :], 0.0)
        for stage in STAGES:
            clear_semaphores(nc)
            layernorm(nc, stage + "_norm", X, Y)
            if stage == "attn_a":
                causal_attention(nc, stage, X, Y, ident, identb, dram)
            elif stage.startswith("ffn"):
                with ExitStack() as stack_ctx:
                    X1 = Pool_(nc, stack_ctx, stage).sb("X1", [P, B * (TPB + 1), D])
                    zero_tiles(nc, X1)
                    ffn_stack(nc, stage, X1, Y, ident, identb, dram)
                add_stream(nc, stage + "_add", X, Y)
            elif stage == "attn_b":
                channel_attention(nc, stage, X, Y, ident, dram)
            elif stage == "window":
                window_attention(nc, stage, X, Y, ident, identb, dram)
            elif stage.startswith("moe"):
                experts(nc, stage, X, Y, ident, dram)
            elif stage == "attn_t":
                time_attention(nc, stage, X, Y, ident, dram)
        store_stream(nc, X, out)


def clear_semaphores(nc):
    ids = sorted(nc.free_semaphores)
    assert ids == list(range(ids[0], ids[-1] + 1))
    with ExitStack() as ctx:
        block = ctx.enter_context(nc.Block())

        @block.gpsimd
        def _(pool):
            pool.sem_clear(range(ids[0], ids[-1] + 1))


def zero_tiles(nc, T):
    with ExitStack() as ctx:
        block = ctx.enter_context(nc.Block())

        @block.vector
        def _(dve):
            for b in range(B):
                dve.memset(T[:, 5 * b, :], 0.0)


def kernel(**inputs):
    import numpy as _np
    import concourse.bacc as _bacc
    from concourse import mybir as _mybir
    from concourse.bass_utils import run_bass_kernel_spmd as _run

    a = {n: _np.asarray(v) for n, v in inputs.items()}
    half = 32

    def swapped(s):
        return _np.concatenate([s[:, half:], s[:, :half]], 1)

    qs, ks = a["L0_ffn_q_scale"], a["L0_ffn_k_scale"]
    laid = {
        "x": a["L0_attn_a_x"],
        "rotary": rotary_base(),
        "qk_scales": _np.stack([qs, swapped(qs), ks, swapped(ks)], 1).reshape(-1),
        "Wqkv": a["L0_ffn_Wqkv"], "Wo": a["L0_ffn_Wo"], "W1": a["L0_ffn_W1"], "W2": a["L0_ffn_W2"],
        "b1": a["L0_ffn_b1"], "b2": a["L0_ffn_b2"],
        "ln_gb": _np.stack([a["L0_ffn_ln_g"].T, a["L0_ffn_ln_b"].T], -1),
    }
    laid.update(lay_out_others(a, _np))
    nc = _bacc.Bacc("TRN2", target_bir_lowering=False, num_devices=1)
    arrays, dram = {}, {}
    for name, v in laid.items():
        v = _np.ascontiguousarray(v)
        arrays[f"in_{name}"] = v
        dram[name] = nc.dram_tensor(f"in_{name}", v.shape, _mybir.dt.from_np(v.dtype), kind="ExternalInput").ap()
    out = nc.dram_tensor("out", (B, S, D), _mybir.dt.float32, kind="ExternalOutput").ap()
    build(nc, dram, out)
    r = _run(nc, [arrays], core_ids=[0])
    return r.results[0]["out"]
```

```python
from contextlib import ExitStack

import numpy as np
import concourse.bass as bass
from concourse import mybir

F32 = mybir.dt.float32
BF16 = mybir.dt.bfloat16
ALU = mybir.AluOpType
ACT = mybir.ActivationFunctionType
AX = mybir.AxisListType

P = 128
D = 128
B, S = 4, 512
TPB = S // P
NT = B * TPB
NEG = -1.0e30
LN_EPS = 1e-5


def wait(eng, sem, value):
    if isinstance(value, int) and value <= 0:
        return
    eng.wait_ge(sem, value)


def slot(t):
    return (t // TPB) * (TPB + 1) + t % TPB + 1


class Pool_:

    def __init__(self, nc, ctx, tag):
        self.nc, self.ctx, self.tag = nc, ctx, tag

    def sb(self, name, shape, dt=F32):
        return self.ctx.enter_context(self.nc.sbuf_tensor(f"{self.tag}_{name}", shape, dt))

    def ps(self, name, shape, dt=F32):
        return self.ctx.enter_context(self.nc.psum_tensor(f"{self.tag}_{name}", shape, dt))

    def sem(self, name):
        return self.ctx.enter_context(self.nc.semaphore(f"{self.tag}_{name}"))


def layernorm(nc, tag, src, dst):
    with ExitStack() as ctx:
        new = Pool_(nc, ctx, tag)
        stats = new.sb("stats", [P, NT, 6])
        mean_var = new.sb("mean_var", [P, NT, 2])
        log_var = new.sb("log_var", [P, NT])
        rstd = new.sb("rstd", [P, NT])
        stats_ready, moments_ready, eps_added, rstd_ready, centred, dve_chain = (
            new.sem(n) for n in ("stats", "moments", "eps_added", "rstd_ready", "centred", "chain"))
        block = ctx.enter_context(nc.Block())

        @block.vector
        def _(dve):
            for t in range(NT):
                dve.bn_stats(stats[:, t, :], src[:, slot(t), :]).then_inc(stats_ready, 1)
            for t in range(NT):
                dve.wait_ge(stats_ready, t + 1)
                dve.bn_aggr(mean_var[:, t, :], stats[:, t, :]).then_inc(moments_ready, 1)
            dve.wait_ge(moments_ready, NT)
            dve.tensor_scalar(log_var[:, :], mean_var[:, :, 1], LN_EPS, None, ALU.add).then_inc(eps_added, 1)
            dve.wait_ge(rstd_ready, 2)
            for t in range(NT):
                dve.tensor_scalar(dst[:, slot(t), :], src[:, slot(t), :], mean_var[:, t, 0:1],
                                  rstd[:, t:t + 1], ALU.subtract, ALU.mult).then_inc(centred, 1)

        @block.scalar
        def _(act):
            act.wait_ge(eps_added, 1)
            act.activation(rstd[:, :], log_var[:, :], ACT.Ln).then_inc(rstd_ready, 1)
            act.wait_ge(rstd_ready, 1)
            act.activation(rstd[:, :], rstd[:, :], ACT.Exp, scale=-0.5).then_inc(rstd_ready, 1)


def add_stream(nc, tag, X, Y):
    with ExitStack() as ctx:
        new = Pool_(nc, ctx, tag)
        added = new.sem("added")
        block = ctx.enter_context(nc.Block())

        @block.vector
        def _(dve):
            dve.tensor_tensor(X[:, :, :], X[:, :, :], Y[:, :, :], ALU.add).then_inc(added, 1)


DEPTH, HEADS, DH, WINDOW = 6, 16, 64, 32
INNER = HEADS * DH
FF = int(D * 4 * 2 / 3)
KEYS = WINDOW + P
WINDOWS = P // WINDOW
SEEN = 2 * WINDOW
PAIRS = HEADS // 2
FF_CHUNKS = [(0, 128), (128, 128), (256, FF - 256)]


def rotary_base():
    half = np.arange(0, DH, 2, dtype=np.float32)
    inv_freq = (1.0 / np.float32(10000.0) ** (half / np.float32(DH))).astype(np.float32)
    t = np.arange(S, dtype=np.float32)
    freqs = t[:, None] * inv_freq[None, :]
    freqs = np.concatenate([freqs, freqs], -1).astype(np.float32)
    base = ((half + np.float32(0.4 * DH)) / np.float32(1.4 * DH)).astype(np.float32)
    scale = (base[None, :] ** ((t - S // 2) / (WINDOW // 2))[:, None]).astype(np.float32)
    scale = np.concatenate([scale, scale], -1)
    cos, sin = np.cos(freqs), np.sin(freqs)
    sin = np.concatenate([-sin[:, :DH // 2], sin[:, DH // 2:]], -1)
    tab = np.stack([cos * scale * 8.0, sin * scale * 8.0, cos / scale, sin / scale], 1)
    return np.ascontiguousarray(tab.reshape(TPB, P, 4, DH).transpose(1, 0, 2, 3)).astype(np.float32)


def rotary_tables(nc, tag, table, dram):
    with ExitStack() as ctx:
        new = Pool_(nc, ctx, tag + "_rot")
        base = new.sb("base", [P, TPB, 4, DH])
        scales = new.sb("scales", [P, DEPTH, 4, DH])
        loaded, built = new.sem("loaded"), new.sem("built")
        block = ctx.enter_context(nc.Block())

        @block.sync
        def _(sp):
            sp.dma_start(base[:, :, :, :], dram["rotary"]).then_inc(loaded, 16)
            sp.dma_start(scales[:, :, :, :].rearrange("p l a e -> p (l a e)"),
                         dram["qk_scales"].partition_broadcast(P)).then_inc(loaded, 16)

        @block.vector
        def _(dve):
            dve.wait_ge(loaded, 32)
            for l in range(DEPTH):
                for j in range(TPB):
                    dve.tensor_tensor(table[:, l, j, :, :], base[:, j, :, :], scales[:, l, :, :],
                                      ALU.mult).then_inc(built, 1)


def ffn_stack(nc, tag, X1, Y, ident, identb, dram):
    STEPS = DEPTH * NT
    with ExitStack() as ctx:
        new = Pool_(nc, ctx, tag)
        w_qk = new.sb("w_qk", [P, 2, 2 * INNER])
        w_v = new.sb("w_v", [P, INNER])
        w_o = new.sb("w_o", [P, 2, PAIRS, D])
        w_1 = new.sb("w_1", [P, 2, 2 * FF])
        w_2 = new.sb("w_2", [P, 2, 3, D])
        b_1 = new.sb("b_1", [P, 2, 2 * FF])
        b_2 = new.sb("b_2", [P, 2, D])
        ln_gb = new.sb("ln_gb", [P, DEPTH, 2])
        table = new.sb("table", [P, DEPTH, TPB, 4, DH])
        mask = new.sb("mask", [P, 2, SEEN], BF16)
        shift = new.sb("shift", [P, P])
        carry = new.sb("carry", [P, P])

        xs = new.sb("xs", [P, 2, D])
        xsT = new.sb("xsT", [P, 2, KEYS])
        squares = new.sb("squares", [P, 2, 512])
        cos_part = new.sb("cos_part", [P, 2, 512])
        sin_part = new.sb("sin_part", [P, 2, 512])
        qk = new.sb("qk", [P, 4, 512])
        sum_sq = new.sb("sum_sq", [P, 2 * HEADS])
        norms = new.sb("norms", [P, 2 * HEADS])
        qT = new.sb("qT", [P, 2, PAIRS, P])
        kT = new.sb("kT", [P, 2, PAIRS, KEYS])
        values = new.sb("values", [P, 2, WINDOWS, 512])

        row_max = new.sb("row_max", [P, 2, PAIRS])
        row_sum = new.sb("row_sum", [P, 2, PAIRS])
        inv_sum = new.sb("inv_sum", [P, 2, 2, PAIRS])
        probs = new.sb("probs", [P, 2, PAIRS, SEEN])
        probsT = new.sb("probsT", [P, 2, 4, P])
        o_sb = new.sb("o_sb", [P, 2, 512])
        oT = new.sb("oT", [P, PAIRS, P])

        xm = new.sb("xm", [P, D])
        ln_stats = new.sb("ln_stats", [P, 6])
        ln_mv = new.sb("ln_mv", [P, 2])
        ln_var = new.sb("ln_var", [P, 1])
        ln_rstd = new.sb("ln_rstd", [P, 1])
        zeros = new.sb("zeros", [P, 1])
        held = new.sb("held", [1, 1])
        xhat = new.sb("xhat", [P, D])
        xnT = new.sb("xnT", [P, P])
        up = new.sb("up", [P, 2, FF])
        gate = new.sb("gate", [P, FF])
        hT = new.sb("hT", [P, 3, P])
        x1b = new.sb("x1b", [P, D])

        rotary_tables(nc, tag, table, dram)

        ps_front = [new.ps(f"ps_front{n}", [P, 512]) for n in range(2)]
        ps_s = [new.ps(f"ps_s{n}", [P, 512]) for n in range(2)]
        ps_o = [new.ps(f"ps_o{n}", [P, 512]) for n in range(2)]
        ps_up = new.ps("ps_up", [P, 512])
        ps_gate = new.ps("ps_gate", [P, 512])
        ps_small = ps_up[:, 384:512]
        ps_y = ps_gate[:, 384:512]

        base_loaded, weights0, weights1, wv_loaded = (
            new.sem(n) for n in ("base_loaded", "weights0", "weights1", "wv_loaded"))
        const_ready = new.sem("const_ready")
        (shifted_f, xs_ready, xsT_full, xsT_ready, xs_before_ready, proj_full, squared, sumsq_ready, rotated,
         summed, clamped, logged, rn_ready, qk_ready, qT_full, qT_ready, kT_full, kT_ready, k_before_ready,
         v_full, v_ready) = (new.sem(n) for n in (
             "shifted_f", "xs_ready", "xsT_full", "xsT_ready", "xs_before_ready", "proj_full", "squared",
             "sumsq_ready", "rotated", "summed", "clamped", "logged", "rn_ready", "qk_ready", "qT_full",
             "qT_ready", "kT_full", "kT_ready", "k_before_ready", "v_full", "v_ready"))
        (s_full, max_ready, diff_ready, exp_ready, sum_ready, inv_ready, pT_full, pT_ready, pv_done, o_scaled,
         oT_full, o_ready) = (new.sem(n) for n in (
             "s_full", "max_ready", "diff_ready", "exp_ready", "sum_ready", "inv_ready", "pT_full", "pT_ready",
             "pv_done", "o_scaled", "oT_full", "o_ready"))
        (y_full, x1_ready, shifted_m, xm_ready, stats_ready, mv_ready, var_ready, mlog_ready, mrstd_ready,
         xhat_ready, xhT_full, xnT_ready, up_full, biased, gelu_ready, hid_ready, hT_full, hT_ready, down_full,
         x1b_ready, y_ready) = (new.sem(n) for n in (
             "y_full", "x1_ready", "shifted_m", "xm_ready", "stats_ready", "mv_ready", "var_ready",
             "mlog_ready", "mrstd_ready", "xhat_ready", "xhT_full", "xnT_ready", "up_full", "biased",
             "gelu_ready", "hid_ready", "hT_full", "hT_ready", "down_full", "x1b_ready", "y_ready"))
        block = ctx.enter_context(nc.Block())

        def par(i):
            return (i // NT) % 2

        def u(i):
            t = i % NT
            return (t // TPB) * (TPB + 1) + t % TPB + 1

        PEEL = 6
        LAG = 4

        class Parts:

            def __init__(self, i):
                self.i, self.a, self.o, self.m, self.d = i, i - 1, i - 2, i - 3, i - 4
                peeled = isinstance(i, int)
                self.pre, self.front, self.attend, self.out, self.mlp, self.down = (
                    not peeled or 0 <= i - lag < STEPS for lag in range(-1, 5))

        def run(step, eng):
            for i in range(-1, PEEL):
                step(Parts(i), i % 2)
            with eng.Fori(PEEL // 2, STEPS // 2 - 1) as two_steps:
                i = 2 * two_steps
                step(Parts(i), 0)
                step(Parts(i + 1), 1)
            for i in range(STEPS - 2, STEPS + LAG):
                step(Parts(i), i % 2)

        WEIGHT_DMAS = 7
        V_BANKS = (0, 0, 1, 0)
        CONSTS = 9 + 2 * WINDOWS

        def wait_weights(eng, i):
            l = i // NT
            wait(eng, weights0, 16 * WEIGHT_DMAS * ((l + 2) // 2))
            wait(eng, weights1, 16 * WEIGHT_DMAS * ((l + 1) // 2))

        def pool_copy(dst, src):
            shape, zero = list(src.shape), zeros[:, :]
            while len(zero.shape) < len(shape):
                zero = zero.unsqueeze(1)
            return nc.gpsimd.tensor_tensor(dst, src, zero.to_broadcast(shape), ALU.add)

        @block.sync
        def _(sp):
            def load(l, q):
                done = (weights0, weights1)[q]
                sp.dma_start(w_qk[:, q, :], dram["Wqkv"][l, :, 0:2 * INNER]).then_inc(done, 16)
                sp.dma_start(w_o[:, q, :, :], dram["Wo"][l].rearrange("(c p) d -> p c d", p=P)).then_inc(done, 16)
                sp.dma_start(w_1[:, q, :], dram["W1"][l]).then_inc(done, 16)
                sp.dma_start(w_2[:, q, 0:2, :],
                             dram["W2"][l, 0:256, :].rearrange("(c p) d -> p c d", p=P)).then_inc(done, 16)
                sp.dma_start(w_2[0:FF - 256, q, 2, :], dram["W2"][l, 256:FF, :]).then_inc(done, 16)
                sp.dma_start(b_1[:, q, :], dram["b1"][l].partition_broadcast(P)).then_inc(done, 16)
                sp.dma_start(b_2[:, q, :], dram["b2"][l].partition_broadcast(P)).then_inc(done, 16)

            def load_v(l):
                wait(sp, v_full, WINDOWS * NT * l)
                sp.dma_start(w_v[:, :], dram["Wqkv"][l, :, 2 * INNER:3 * INNER]).then_inc(wv_loaded, 16)

            load(0, 0)
            load_v(0)
            sp.dma_start(ln_gb[:, :, :], dram["ln_gb"]).then_inc(base_loaded, 16)
            load(1, 1)
            load_v(1)
            with sp.Fori(1, DEPTH // 2) as two_layers:
                l = 2 * two_layers
                sp.wait_ge(y_ready, NT * l)
                load(l, 0)
                load_v(l)
                sp.wait_ge(y_ready, NT * (l + 1))
                load(l + 1, 1)
                load_v(l + 1)

        @block.gpsimd
        def _(pool):
            pool.memset(shift[:, :], 0.0).then_inc(const_ready, 1)
            pool.memset(carry[:, :], 0.0).then_inc(const_ready, 1)
            pool.memset(mask[:, :, :], 0.0).then_inc(const_ready, 1)
            pool.memset(kT[:, 1, :, :], 0.0).then_inc(const_ready, 1)
            pool.memset(xsT[:, 1, :], 0.0).then_inc(const_ready, 1)
            pool.memset(zeros[:, :], 0.0).then_inc(const_ready, 1)
            pool.wait_ge(const_ready, 6)
            pool.affine_select(out=shift[:, :], in_=shift[:, :], compare_op=ALU.not_equal, fill=1.0, base=1,
                               pattern=[[-1, P]], channel_multiplier=1).then_inc(const_ready, 1)
            pool.affine_select(out=carry[:, :], in_=carry[:, :], compare_op=ALU.not_equal, fill=1.0,
                               base=-(P - 1), pattern=[[P, P]], channel_multiplier=1).then_inc(const_ready, 1)
            for w in range(WINDOWS):
                part = mask[WINDOW * w:WINDOW * w + WINDOW, :, :]
                pool.wait_ge(const_ready, 8 + w)
                pool.affine_select(out=part, in_=part, compare_op=ALU.is_ge, fill=NEG, base=0,
                                   pattern=[[0, 2], [1, SEEN]], channel_multiplier=-1).then_inc(const_ready, 1)
            for w in range(WINDOWS):
                part = mask[WINDOW * w:WINDOW * w + WINDOW, :, :]
                pool.wait_ge(const_ready, 8 + WINDOWS + w)
                pool.affine_select(out=part, in_=part, compare_op=ALU.is_ge, fill=NEG, base=WINDOW,
                                   pattern=[[0, 2], [-1, SEEN]], channel_multiplier=1).then_inc(const_ready, 1)
            pool.wait_ge(const_ready, 8 + 2 * WINDOWS)
            pool.memset(mask[0:WINDOW, 0, 0:WINDOW], NEG).then_inc(const_ready, 1)

            def add_parts(i, c):
                wait(pool, rotated, 4 * i + c + 1)
                if c < 2:
                    wait(pool, qT_full, 2 * (i - 1) + c + 1)
                else:
                    wait(pool, kT_full, 2 * (i - 1) + c - 1)
                pool.tensor_tensor(qk[:, c, :], cos_part[:, c % 2, :], sin_part[:, c % 2, :],
                                   ALU.add).then_inc(summed, 1)

            def norm_qk(i, c):
                wait(pool, summed, 4 * i + c + 1)
                view = qk[:, c, :].rearrange("p (h e) -> p h e", e=DH)
                rn = norms[:, 8 * c:8 * c + 8].unsqueeze(2).to_broadcast([P, 8, DH])
                pool.tensor_tensor(view, view, rn, ALU.mult).then_inc(qk_ready, 1)

            def step(s, p):
                i, m = s.i, s.m
                if s.mlp:
                    wait(pool, x1_ready, m + 1)
                    wait(pool, xhat_ready, m)
                    pool_copy(xm[:, 0:DH], X1[:, u(m), 0:DH]).then_inc(xm_ready, 1)
                    wait_weights(pool, m)
                    wait(pool, y_ready, NT + m)
                    pool.tensor_tensor(x1b[:, :], X1[:, u(m), :], b_2[:, par(m), :], ALU.add).then_inc(x1b_ready, 1)
                if s.front:
                    add_parts(i, 0)
                    add_parts(i, 1)
                    wait(pool, kT_ready, 2 * i)
                    wait(pool, s_full, 2 * (i - 1))
                    pool_copy(kT[:, p, :, 0:WINDOW], kT[:, 1 - p, :, P:KEYS]).then_inc(k_before_ready, 1)
                    wait(pool, rn_ready, 2 * i + 1)
                    norm_qk(i, 0)
                    norm_qk(i, 1)
                    add_parts(i, 2)
                    add_parts(i, 3)
                if s.pre:
                    n = i + 1
                    wait(pool, y_ready, n + 1)
                    wait(pool, xsT_full, n - 1)
                    pool_copy(xs[:, 1 - p, 0:DH], Y[:, u(n), 0:DH]).then_inc(xs_ready, 1)
                    wait(pool, xsT_ready, n)
                    wait(pool, v_full, 4 * (n - 1))
                    pool_copy(xsT[:, 1 - p, 0:WINDOW], xsT[:, p, P:KEYS]).then_inc(xs_before_ready, 1)
                if s.front:
                    wait(pool, rn_ready, 2 * i + 2)
                    norm_qk(i, 2)
                    norm_qk(i, 3)
                if s.mlp:
                    wait(pool, gelu_ready, m + 1)
                    pool.tensor_tensor(gate[:, :], up[:, 0, :], gate[:, :], ALU.mult).then_inc(hid_ready, 1)

            run(step, pool)

        @block.vector
        def _(dve):
            dve.memset(ln_var[:, :], 0.0).then_inc(y_ready, NT)

            def shifted_logits(a, h):
                n = 2 * a + h
                bank = ps_s[h][:, :].rearrange("p (c k) -> p c k", k=SEEN)
                wait(dve, s_full, n + 1)
                dve.tensor_reduce(row_max[:, h, :], bank, AX.X, ALU.max).then_inc(max_ready, 1)
                wait(dve, max_ready, n + 1)
                wait(dve, pT_full, n - 1)
                dve.tensor_tensor(probs[:, h, :, :], bank, row_max[:, h, :].unsqueeze(2).to_broadcast(
                    [P, PAIRS, SEEN]), ALU.subtract).then_inc(diff_ready, 1)

            def inverse(a, h, pa):
                n = 2 * a + h
                wait(dve, exp_ready, n + 1)
                dve.tensor_reduce(row_sum[:, h, :], probs[:, h, :, :], AX.X, ALU.add).then_inc(sum_ready, 1)
                wait(dve, sum_ready, n + 1)
                dve.reciprocal(inv_sum[:, pa, h, :], row_sum[:, h, :]).then_inc(inv_ready, 1)

            def scale_o(a, half, pa):
                n = 2 * a + half
                wait(dve, pv_done, n + 1)
                wait(dve, inv_ready, 2 * a + 2)
                wait(dve, oT_full, n - 1)
                inv = inv_sum[:, pa, :, :].rearrange("p h (j u) -> p u j h", u=2)[:, half].unsqueeze(3)
                split = "p (j h e) -> p j h e"
                dve.tensor_tensor(o_sb[:, half, :].rearrange(split, h=2, e=DH),
                                  ps_o[half][:, :].rearrange(split, h=2, e=DH),
                                  inv.to_broadcast([P, 4, 2, DH]), ALU.mult).then_inc(o_scaled, 1)

            def rotate(i, c):
                n = 4 * i + c
                src = ps_front[c % 2][:, :].rearrange("p (h a e) -> p h a e", a=2, e=DH // 2)
                j, l, which = i % TPB, i // NT, 2 * (c // 2)
                cos = table[:, l, j, which, :].unsqueeze(1).to_broadcast([P, 8, DH])
                wait(dve, squared, n + 1)
                wait(dve, summed, n - 1)
                dve.tensor_tensor(cos_part[:, c % 2, :].rearrange("p (h e) -> p h e", e=DH),
                                  ps_front[c % 2][:, :].rearrange("p (h e) -> p h e", e=DH), cos, ALU.mult)
                out = sin_part[:, c % 2, :].rearrange("p (h a e) -> p h a e", a=2, e=DH // 2)
                for half in range(2):
                    sin = table[:, l, j, which + 1, half * 32:half * 32 + 32].unsqueeze(1).to_broadcast([P, 8, 32])
                    last = dve.tensor_tensor(out[:, :, half, :], src[:, :, 1 - half, :], sin, ALU.mult)
                last.then_inc(rotated, 1)
                wait(dve, clamped, 2 * i + c // 2 - 1)
                dve.tensor_reduce(sum_sq[:, 8 * c:8 * c + 8], squares[:, c % 2, :].rearrange(
                    "p (h e) -> p h e", e=DH), AX.X, ALU.add).then_inc(sumsq_ready, 1)

            def clamp(i, q):
                wait(dve, sumsq_ready, 4 * i + 2 * q + 2)
                wait(dve, qk_ready, 4 * i + 2 * q - 2)
                dve.tensor_scalar(norms[:, 16 * q:16 * q + 16], sum_sq[:, 16 * q:16 * q + 16], 1e-19, None,
                                  ALU.max).then_inc(clamped, 1)

            def step(s, p):
                i, a, o, m, d = s.i, s.a, s.o, s.m, s.d
                if s.down:
                    wait(dve, hT_full, d + 1)
                    wait(dve, down_full, d)
                    dve.tensor_copy(hT[:, 0:2, :].rearrange("p c t -> p (c t)"), ps_up[:, 0:256])
                    dve.tensor_copy(hT[0:FF - 256, 2, :], ps_up[0:FF - 256, 256:384]).then_inc(hT_ready, 1)
                if s.front:
                    rotate(i, 0)
                if s.down:
                    wait(dve, down_full, d + 1)
                    wait(dve, x1b_ready, d + 1)
                    dve.tensor_tensor(Y[:, u(d), :], ps_small[:, :], x1b[:, :], ALU.add).then_inc(y_ready, 1)
                if s.attend:
                    shifted_logits(a, 0)
                if s.front:
                    rotate(i, 1)
                if s.out:
                    scale_o(o, 0, p)
                if s.mlp:
                    wait(dve, shifted_m, m + 1)
                    wait(dve, xhat_ready, m)
                    dve.tensor_copy(xm[:, DH:D], ps_small[:, 0:DH]).then_inc(xm_ready, 1)
                    wait(dve, xm_ready, 2 * m + 2)
                    dve.bn_stats(ln_stats[:, :], xm[:, :]).then_inc(stats_ready, 1)
                    wait(dve, stats_ready, m + 1)
                    dve.memset(held[:, :], 0.0)
                    dve.bn_aggr(ln_mv[:, :], ln_stats[:, :]).then_inc(mv_ready, 1)
                    wait(dve, mv_ready, m + 1)
                    dve.tensor_scalar(ln_var[:, :], ln_mv[:, 1:2], LN_EPS, None, ALU.add).then_inc(var_ready, 1)
                if s.out:
                    scale_o(o, 1, p)
                if s.attend:
                    inverse(a, 0, 1 - p)
                if s.mlp:
                    wait(dve, mrstd_ready, m + 1)
                    wait(dve, xhT_full, m)
                    dve.tensor_scalar(xhat[:, :], xm[:, :], ln_mv[:, 0:1], ln_rstd[:, 0:1], ALU.subtract,
                                      ALU.mult).then_inc(xhat_ready, 1)
                if s.front:
                    rotate(i, 2)
                    clamp(i, 0)
                    rotate(i, 3)
                    clamp(i, 1)
                if s.mlp:
                    wait_weights(dve, m)
                    wait(dve, up_full, m + 1)
                    wait(dve, hid_ready, m)
                    dve.tensor_tensor(up[:, 0, :], ps_up[:, 0:FF], b_1[:, par(m), 0:FF], ALU.add)
                    dve.tensor_tensor(up[:, 1, :], ps_gate[:, 0:FF], b_1[:, par(m), FF:2 * FF], ALU.add).then_inc(biased, 1)
                if s.attend:
                    shifted_logits(a, 1)
                if s.pre:
                    wait(dve, shifted_f, i + 2)
                    wait(dve, xsT_full, i)
                    dve.tensor_copy(xs[:, 1 - p, DH:D], ps_small[:, 0:DH]).then_inc(xs_ready, 1)
                if s.attend:
                    inverse(a, 1, 1 - p)
                if s.out:
                    wait(dve, y_full, o + 1)
                    dve.tensor_tensor(X1[:, u(o), :], ps_y[:, :], Y[:, u(o), :], ALU.add).then_inc(x1_ready, 1)

            run(step, dve)

        @block.scalar
        def _(act):
            def exponentials(a, h):
                wait(act, diff_ready, 2 * a + h + 1)
                act.activation(probs[:, h, :, :], probs[:, h, :, :], ACT.Exp).then_inc(exp_ready, 1)

            def copy_pT(a, h):
                wait(act, pT_full, 2 * a + h + 1)
                wait(act, pv_done, 2 * a)
                act.activation(probsT[:, h, :, :].rearrange("p j t -> p (j t)"), ps_s[h][:, :],
                               ACT.Copy).then_inc(pT_ready, 1)

            def square(i, c):
                wait(act, proj_full, 4 * i + c + 1)
                wait(act, sumsq_ready, 4 * i + c - 1)
                act.activation(squares[:, c % 2, :], ps_front[c % 2][:, :], ACT.Square).then_inc(squared, 1)

            def rnorm(i, q):
                wait(act, clamped, 2 * i + q + 1)
                act.activation(norms[:, 16 * q:16 * q + 16], norms[:, 16 * q:16 * q + 16], ACT.Ln).then_inc(logged, 1)
                wait(act, logged, 2 * i + q + 1)
                act.activation(norms[:, 16 * q:16 * q + 16], norms[:, 16 * q:16 * q + 16], ACT.Exp,
                               scale=-0.5).then_inc(rn_ready, 1)

            def copy_v(i, p, w):
                wait(act, v_full, 4 * i + w + 1)
                wait(act, pv_done, 2 * (i - 1))
                act.activation(values[:, p, w, :], ps_o[V_BANKS[w]][:, :], ACT.Copy).then_inc(v_ready, 1)

            def copy_qT(i, p, c):
                wait(act, qT_full, 2 * i + c + 1)
                wait(act, s_full, 2 * (i - 1))
                act.activation(qT[:, p, 4 * c:4 * c + 4, :].rearrange("p c t -> p (c t)"), ps_front[c][:, :],
                               ACT.Copy).then_inc(qT_ready, 1)

            def copy_kT(a, pa, c):
                wait(act, kT_full, 2 * a + c + 1)
                wait(act, s_full, 2 * (a - 1))
                wait(act, k_before_ready, a)
                act.activation(kT[:, pa, 4 * c:4 * c + 4, WINDOW:KEYS],
                               ps_s[c][:, :].rearrange("p (c t) -> p c t", t=P), ACT.Copy).then_inc(kT_ready, 1)

            def copy_o(a, half):
                wait(act, oT_full, 2 * a + half + 1)
                wait(act, y_full, a)
                act.activation(oT[:, :, :].rearrange("p (j u) t -> p u j t", u=2)[:, half],
                               ps_o[half][:, :].rearrange("p (j t) -> p j t", t=P), ACT.Copy).then_inc(o_ready, 1)

            def step(s, p):
                i, a, o, m = s.i, s.a, s.o, s.m
                if s.attend:
                    copy_kT(a, 1 - p, 0)
                    copy_kT(a, 1 - p, 1)
                if s.front:
                    square(i, 0)
                if s.attend:
                    exponentials(a, 0)
                if s.front:
                    square(i, 1)
                    square(i, 2)
                if s.mlp:
                    wait(act, var_ready, m + 1)
                    wait(act, xhat_ready, m)
                    act.activation(ln_rstd[:, :], ln_var[:, :], ACT.Ln).then_inc(mlog_ready, 1)
                    wait(act, mlog_ready, m + 1)
                    act.activation(ln_rstd[:, :], ln_rstd[:, :], ACT.Exp, scale=-0.5).then_inc(mrstd_ready, 1)
                if s.attend:
                    copy_pT(a, 0)
                if s.out:
                    copy_o(o, 0)
                if s.front:
                    square(i, 3)
                    copy_v(i, p, 0)
                if s.mlp:
                    wait(act, xhT_full, m + 1)
                    wait(act, up_full, m)
                    act.activation(xnT[:, :], ps_small[:, :], ACT.Identity, bias=ln_gb[:, m // NT, 1:2],
                                   scale=ln_gb[:, m // NT, 0:1]).then_inc(xnT_ready, 1)
                if s.out:
                    copy_o(o, 1)
                if s.front:
                    rnorm(i, 0)
                    copy_v(i, p, 1)
                    rnorm(i, 1)
                    copy_v(i, p, 2)
                if s.mlp:
                    wait(act, biased, m + 1)
                    wait(act, hT_full, m)
                    act.activation(gate[:, :], up[:, 1, :], ACT.Gelu).then_inc(gelu_ready, 1)
                    act.preload_act_table_set("natural_log_exp_and_others")
                if s.pre:
                    n = i + 1
                    wait(act, xsT_full, n + 1)
                    wait(act, proj_full, 4 * (n - 1))
                    wait(act, v_full, 4 * (n - 1))
                    wait(act, xs_before_ready, n)
                    act.activation(xsT[:, 1 - p, WINDOW:KEYS], ps_small[:, :], ACT.Copy).then_inc(xsT_ready, 1)
                if s.attend:
                    exponentials(a, 1)
                if s.front:
                    copy_v(i, p, 3)
                if s.attend:
                    copy_pT(a, 1)
                if s.front:
                    copy_qT(i, p, 0)
                    copy_qT(i, p, 1)

            act.preload_act_table_set("natural_log_exp_and_others")
            act.wait_ge(base_loaded, 16)
            run(step, act)

        @block.tensor
        def _(pe):
            def scores(a, pa, h):
                first = 1 if pa == 1 else ((a % TPB) + 1) // 2
                pe.matmul(ps_s[h][:, :], identb[:, :], mask[:, first, :].unsqueeze(1).to_broadcast(
                    [P, PAIRS, SEEN]), start=True, stop=False)
                rows = slice(DH * h, DH * h + DH)
                for c in range(PAIRS):
                    for w in range(WINDOWS):
                        last = pe.matmul(ps_s[h][WINDOW * w:WINDOW * w + WINDOW, SEEN * c:SEEN * c + SEEN],
                                         qT[rows, pa, c, WINDOW * w:WINDOW * w + WINDOW],
                                         kT[rows, pa, c, WINDOW * w:WINDOW * w + SEEN],
                                         start=False, stop=(c == PAIRS - 1), tile_position=(DH * h, WINDOW * w))
                last.then_inc(s_full, 1)

            def turn_probs(a, h):
                wait(pe, exp_ready, 2 * a + h + 1)
                for j in range(4):
                    last = pe.transpose(ps_s[h][:, j * P:(j + 1) * P], probs[:, h, 2 * j:2 * j + 2, :].rearrange(
                        "p c k -> p (c k)"), ident[:, :])
                last.then_inc(pT_full, 1)

            def weigh_values(a, pa, half):
                rows = slice(DH * half, DH * half + DH)
                for j in range(4):
                    for h in range(2):
                        for w in range(WINDOWS):
                            q = slice(WINDOW * w, WINDOW * w + WINDOW)
                            cols = slice(P * j + DH * h, P * j + DH * h + DH)
                            last = pe.matmul(ps_o[half][q, cols], probsT[rows, h, j, q], values[rows, pa, w, cols],
                                             start=True, stop=True, tile_position=(DH * half, WINDOW * w))
                last.then_inc(pv_done, 1)

            def turn_o(a, half):
                wait(pe, o_scaled, 2 * a + half + 1)
                for j in range(4):
                    last = pe.transpose(ps_o[half][:, P * j:P * j + P], o_sb[:, half, P * j:P * j + P], ident[:, :])
                last.then_inc(oT_full, 1)

            def project(i, p, c):
                if c >= 2:
                    wait(pe, rotated, 4 * i + c - 1)
                pe.matmul(ps_front[c % 2][:, :], xsT[:, p, WINDOW:KEYS], w_qk[:, par(i), 512 * c:512 * c + 512],
                          start=True, stop=True).then_inc(proj_full, 1)

            def project_v(i, p, w):
                for half in range(2):
                    cols = w_v[:, :].rearrange("p (j u x) -> p u j x", u=2, x=P)[:, half]
                    last = pe.matmul(ps_o[V_BANKS[w]][DH * half:DH * half + DH, :],
                                     xsT[:, p, WINDOW * w:WINDOW * w + SEEN], cols, start=True, stop=True)
                last.then_inc(v_full, 1)

            def turn_q(i, c):
                wait(pe, qk_ready, 4 * i + c + 1)
                wait(pe, rotated, 4 * i + c + 3)
                for n in range(4):
                    last = pe.transpose(ps_front[c][:, n * P:(n + 1) * P], qk[:, c, n * P:(n + 1) * P], ident[:, :])
                last.then_inc(qT_full, 1)

            def turn_k(a, c):
                wait(pe, qk_ready, 4 * a + c + 3)
                wait(pe, pT_ready, 2 * a - 1 + c)
                for n in range(4):
                    last = pe.transpose(ps_s[c][:, n * P:(n + 1) * P], qk[:, 2 + c, n * P:(n + 1) * P],
                                        ident[:, :])
                last.then_inc(kT_full, 1)

            def step(s, p):
                i, a, o, m, d = s.i, s.a, s.o, s.m, s.d
                pa = 1 - p
                if s.attend:
                    turn_k(a, 0)
                    turn_k(a, 1)
                if s.front:
                    wait_weights(pe, i)
                    wait(pe, xsT_ready, i + 1)
                    wait(pe, qT_ready, 2 * a + 1)
                    project(i, p, 0)
                if s.out:
                    wait(pe, pT_ready, 2 * o + 2)
                    wait(pe, v_ready, 4 * a + 4 if s.attend else 4 * o + 4)
                if s.down:
                    wait(pe, hid_ready, d + 1)
                    for c, (lo, n) in enumerate(FF_CHUNKS):
                        last = pe.transpose(ps_up[0:n, c * P:(c + 1) * P], gate[:, lo:lo + n], ident[:, :])
                    last.then_inc(hT_full, 1)
                if s.attend:
                    wait(pe, kT_ready, 2 * a + 2)
                    wait(pe, qT_ready, 2 * a + 2)
                    wait(pe, k_before_ready, a + 1)
                    scores(a, pa, 0)
                if s.down:
                    wait(pe, hT_ready, d + 1)
                    for c, (lo, n) in enumerate(FF_CHUNKS):
                        last = pe.matmul(ps_small[:, :], hT[0:n, c, :], w_2[0:n, par(d), c, :], start=(c == 0),
                                         stop=(c == 2))
                    last.then_inc(down_full, 1)
                if s.front:
                    wait(pe, qT_ready, 2 * a + 2)
                    project(i, p, 1)
                if s.out:
                    weigh_values(o, p, 0)
                if s.mlp:
                    wait(pe, x1_ready, m + 1)
                    wait(pe, y_ready, NT + m)
                    pe.matmul(ps_small[:, 0:DH], shift[:, :], X1[:, u(m), DH:D], start=True, stop=False)
                    pe.matmul(ps_small[:, 0:DH], carry[:, :], X1[:, u(m) - 1, DH:D], start=False,
                              stop=True).then_inc(shifted_m, 1)
                if s.front:
                    project(i, p, 2)
                if s.out:
                    weigh_values(o, p, 1)
                if s.attend:
                    turn_probs(a, 0)
                if s.front:
                    project(i, p, 3)
                if s.out:
                    turn_o(o, 0)
                if s.attend:
                    scores(a, pa, 1)
                if s.front:
                    wait(pe, xs_before_ready, i + 1)
                    wait(pe, wv_loaded, 16 * (i // NT + 1))
                    wait(pe, o_ready, 2 * a - 1)
                    project_v(i, p, 0)
                if s.mlp:
                    wait(pe, xhat_ready, m + 1)
                    pe.transpose(ps_small[:, :], xhat[:, :], ident[:, :]).then_inc(xhT_full, 1)
                if s.out:
                    turn_o(o, 1)
                if s.front:
                    wait(pe, v_ready, 4 * i + 1)
                    project_v(i, p, 1)
                if s.mlp:
                    wait(pe, xnT_ready, m + 1)
                    wait_weights(pe, m)
                    wait(pe, x1_ready, m + 1)
                    pe.matmul(ps_up[:, 0:FF], xnT[:, :], w_1[:, par(m), 0:FF], start=True, stop=True)
                    pe.matmul(ps_gate[:, 0:FF], xnT[:, :], w_1[:, par(m), FF:2 * FF], start=True,
                              stop=True).then_inc(up_full, 1)
                if s.front:
                    wait(pe, o_ready, 2 * a)
                    project_v(i, p, 2)
                    wait(pe, v_ready, 4 * i + 2)
                    project_v(i, p, 3)
                if s.pre:
                    wait(pe, y_ready, i + 2)
                    if s.mlp:
                        wait(pe, biased, m + 1)
                    else:
                        wait(pe, xsT_ready, i + 1)
                    pe.matmul(ps_small[:, 0:DH], shift[:, :], Y[:, u(i + 1), DH:D], start=True, stop=False)
                    pe.matmul(ps_small[:, 0:DH], carry[:, :], Y[:, u(i + 1) - 1, DH:D], start=False,
                              stop=True).then_inc(shifted_f, 1)
                if s.out:
                    wait_weights(pe, o)
                    wait(pe, o_ready, 2 * o + 2)
                    wait(pe, biased, m + 1)
                    for c in range(PAIRS):
                        last = pe.matmul(ps_y[:, :], oT[:, c, :], w_o[:, par(o), c, :], start=(c == 0), stop=(c == PAIRS - 1))
                    last.then_inc(y_full, 1)
                if s.pre:
                    wait(pe, xs_ready, 2 * i + 4)
                    pe.transpose(ps_small[:, :], xs[:, 1 - p, :], ident[:, :]).then_inc(xsT_full, 1)
                if s.front:
                    turn_q(i, 0)
                    turn_q(i, 1)
                if s.attend:
                    turn_probs(a, 1)

            pe.wait_ge(const_ready, CONSTS)
            run(step, pe)


def transpose_stream(nc, tag, Y, YT, ident):
    with ExitStack() as ctx:
        new = Pool_(nc, ctx, tag)
        banks = [new.ps(f"bank{b}", [P, TPB, P]) for b in range(B)]
        turned, copied = new.sem("turned"), new.sem("copied")
        block = ctx.enter_context(nc.Block())

        @block.tensor
        def _(pe):
            for b in range(B):
                for j in range(TPB):
                    last = pe.transpose(banks[b][:, j, :], Y[:, slot(TPB * b + j), :], ident[:, :])
                last.then_inc(turned, 1)

        @block.vector
        def _(dve):
            for b in range(B):
                dve.wait_ge(turned, b + 1)
                dve.tensor_copy(YT[:, TPB * b:TPB * b + TPB, :], banks[b][:, :, :]).then_inc(copied, 1)


def causal_attention(nc, tag, X, Y, ident, identb, dram):
    STEPS = B * PAIRS
    UNITS = 2 * TPB
    with ExitStack() as ctx:
        new = Pool_(nc, ctx, tag)
        YT = new.sb("YT", [P, NT, P])
        transpose_stream(nc, tag + "_turn", Y, YT, ident)
        w_pair = new.sb("w_pair", [P, 2, 3, P])
        w_out = new.sb("w_out", [P, 2, P])
        causal = new.sb("causal", [P, P], BF16)
        qT = new.sb("qT", [P, 2, 2, S])
        kT = new.sb("kT", [P, 2, S])
        vT = new.sb("vT", [P, S])
        v = new.sb("v", [P, 2, TPB, P])
        neg_max = new.sb("neg_max", [P, 2])
        row_sum = new.sb("row_sum", [P, 2])
        inv_sum = new.sb("inv_sum", [P, 2])
        probs = new.sb("probs", [P, 2, S])
        probsT = new.sb("probsT", [P, 2, S])
        oT = new.sb("oT", [P, S])
        ps_proj = [new.ps(f"ps_proj{n}", [P, 512]) for n in range(2)]
        ps_s = [new.ps(f"ps_s{n}", [P, 512]) for n in range(2)]
        ps_pT = [new.ps(f"ps_pT{n}", [P, 512]) for n in range(2)]
        ps_o = new.ps("ps_o", [P, 512])
        ps_z = new.ps("ps_z", [P, TPB, D])
        w_loaded0, w_loaded1, out_loaded0, out_loaded1, made, q_zeroed = (
            new.sem(n) for n in ("w_loaded0", "w_loaded1", "out_loaded0", "out_loaded1", "made", "q_zeroed"))
        (q_full, k_full, vT_full, v_full, q_ready, k_ready, vT_ready, v_ready) = (new.sem(n) for n in (
            "q_full", "k_full", "vT_full", "v_full", "q_ready", "k_ready", "vT_ready", "v_ready"))
        (s_full, max_ready, exp_ready, inv_ready, p_ready, pT_full, pT_ready, pv_done, o_ready, z_full,
         x_added) = (new.sem(n) for n in ("s_full", "max_ready", "exp_ready", "inv_ready", "p_ready", "pT_full",
                                          "pT_ready", "pv_done", "o_ready", "z_full", "x_added"))
        block = ctx.enter_context(nc.Block())

        def run(step, eng):
            step(0, 0, True, False, False)
            step(1, 1, True, True, False)
            step(2, 0, True, True, True)
            step(3, 1, True, True, True)
            with eng.Fori(2, STEPS // 2) as two_steps:
                i = 2 * two_steps
                step(i, 0, True, True, True)
                step(i + 1, 1, True, True, True)
            step(STEPS, 0, False, True, True)
            step(STEPS + 1, 1, False, False, True)

        def unit(n):
            return n // 2, n % 2

        @block.sync
        def _(sp):
            def load(i, p):
                done = (w_loaded0, w_loaded1)[p]
                sp.dma_start(w_pair[:, p, :, :], dram["a_qkv"][i % PAIRS]).then_inc(done, 16)

            def load_out(i, p):
                done = (out_loaded0, out_loaded1)[p]
                sp.dma_start(w_out[:, p, :], dram["a_out"][i % PAIRS]).then_inc(done, 16)

            load(0, 0)
            load(1, 1)
            load_out(0, 0)
            load_out(1, 1)
            with sp.Fori(1, STEPS // 2) as two_steps:
                i = 2 * two_steps
                sp.wait_ge(vT_full, i - 1)
                load(i, 0)
                sp.wait_ge(vT_full, i)
                load(i + 1, 1)
                sp.wait_ge(z_full, i - 1)
                load_out(i, 0)
                sp.wait_ge(z_full, i)
                load_out(i + 1, 1)

        @block.gpsimd
        def _(pool):
            pool.memset(causal[:, :], 0.0).then_inc(made, 1)
            pool.wait_ge(made, 1)
            pool.affine_select(out=causal[:, :], in_=causal[:, :], compare_op=ALU.is_ge, fill=NEG, base=0,
                               pattern=[[-1, P]], channel_multiplier=1).then_inc(made, 1)

        @block.vector
        def _(dve):
            dve.memset(qT[DH:P, :, 0, :], 0.0).then_inc(q_zeroed, 1)
            dve.memset(qT[0:DH, :, 1, :], 0.0).then_inc(q_zeroed, 1)

            def row_max(a, n):
                g, keys = UNITS * a + n, P * (unit(n)[0] + 1)
                wait(dve, s_full, g + 1)
                wait(dve, exp_ready, g - 1)
                dve.tensor_reduce(neg_max[:, n % 2:n % 2 + 1], ps_s[n % 2][:, 0:keys], AX.X, ALU.max,
                                  negate=True).then_inc(max_ready, 1)

            def normalize(a, n):
                g, keys = UNITS * a + n, P * (unit(n)[0] + 1)
                wait(dve, exp_ready, g + 1)
                dve.reciprocal(inv_sum[:, n % 2:n % 2 + 1], row_sum[:, n % 2:n % 2 + 1]).then_inc(inv_ready, 1)
                wait(dve, inv_ready, g + 1)
                dve.tensor_scalar(probs[:, n % 2, 0:keys], probs[:, n % 2, 0:keys], inv_sum[:, n % 2:n % 2 + 1],
                                  None, ALU.mult).then_inc(p_ready, 1)

            def step(i, p, front, attend, out):
                a, o = i - 1, i - 2
                for n in range(UNITS + 1):
                    if out and n == 6:
                        wait(dve, z_full, o + 1)
                        tiles = X[:, 5 * (o // PAIRS) + 1:5 * (o // PAIRS) + 5, :] if isinstance(o, int) else \
                            X[:, bass.ds(5 * (o // PAIRS) + 1, TPB), :]
                        dve.scalar_tensor_tensor(out=tiles, in0=ps_z[:, :, :], scalar=1.0 / HEADS, in1=tiles,
                                                 op0=ALU.mult, op1=ALU.add).then_inc(x_added, 1)
                    if attend and n >= 1:
                        normalize(a, n - 1)
                    if attend and n < UNITS:
                        row_max(a, n)
                    if front and n == 2:
                        wait(dve, k_full, i + 1)
                        wait(dve, s_full, UNITS * (i - 1))
                        dve.tensor_copy(kT[:, p, :], ps_proj[1][:, :]).then_inc(k_ready, 1)
                    if front and n == 4:
                        wait(dve, vT_full, i + 1)
                        wait(dve, v_full, i)
                        dve.tensor_copy(vT[:, :], ps_proj[0][:, :]).then_inc(vT_ready, 1)

            run(step, dve)

        @block.scalar
        def _(act):
            def exp(a, n):
                g, keys = UNITS * a + n, P * (unit(n)[0] + 1)
                wait(act, max_ready, g + 1)
                wait(act, pT_full, g - 1)
                wait(act, inv_ready, g - 1)
                act.activation(probs[:, n % 2, 0:keys], ps_s[n % 2][:, 0:keys], ACT.Exp,
                               bias=neg_max[:, n % 2:n % 2 + 1],
                               accum_out=row_sum[:, n % 2:n % 2 + 1]).then_inc(exp_ready, 1)

            def copy_pT(a, n):
                g, keys = UNITS * a + n, P * (unit(n)[0] + 1)
                wait(act, pT_full, g + 1)
                wait(act, pv_done, g - 1)
                act.activation(probsT[:, n % 2, 0:keys], ps_pT[n % 2][:, 0:keys], ACT.Copy).then_inc(pT_ready, 1)

            def step(i, p, front, attend, out):
                a, o = i - 1, i - 2
                for n in range(UNITS + 1):
                    if attend and n < UNITS:
                        exp(a, n)
                    if out and n == 0:
                        wait(act, pv_done, UNITS * o + UNITS)
                        wait(act, z_full, o)
                        act.activation(oT[:, :], ps_o[:, :], ACT.Copy).then_inc(o_ready, 1)
                    if front and n == 1:
                        wait(act, q_full, i + 1)
                        wait(act, s_full, UNITS * (i - 1))
                        act.activation(qT[0:DH, p, 0, :], ps_proj[0][0:DH, :], ACT.Copy, scale=1.0 / P)
                        act.activation(qT[DH:P, p, 1, :], ps_proj[0][DH:P, :], ACT.Copy,
                                       scale=1.0 / P).then_inc(q_ready, 1)
                    if front and n == 6:
                        wait(act, v_full, i + 1)
                        wait(act, pv_done, UNITS * (i - 1))
                        act.activation(v[:, p, :, :], ps_proj[1][:, :].rearrange("p (j e) -> p j e", e=P),
                                       ACT.Copy).then_inc(v_ready, 1)
                    if attend and n >= 1:
                        copy_pT(a, n - 1)

            act.wait_ge(q_zeroed, 2)
            run(step, act)

        @block.tensor
        def _(pe):
            def scores(a, p, n):
                g = UNITS * a + n
                t, h = unit(n)
                wait(pe, exp_ready, g - 1)
                pe.matmul(ps_s[n % 2][:, 0:P * (t + 1)], qT[:, p, h, P * t:P * t + P], kT[:, p, 0:P * (t + 1)],
                          start=True, stop=False)
                pe.matmul(ps_s[n % 2][:, P * t:P * t + P], identb[:, :], causal[:, :], start=False,
                          stop=True).then_inc(s_full, 1)

            def turn(a, n):
                g = UNITS * a + n
                wait(pe, p_ready, g + 1)
                wait(pe, pT_ready, g - 1)
                for c in range(unit(n)[0] + 1):
                    last = pe.transpose(ps_pT[n % 2][:, P * c:P * c + P], probs[:, n % 2, P * c:P * c + P],
                                        ident[:, :])
                last.then_inc(pT_full, 1)

            def weigh_values(a, p, n):
                t, h = unit(n)
                wait(pe, pT_ready, UNITS * a + n + 1)
                if n == 0:
                    wait(pe, o_ready, a)
                for c in range(t + 1):
                    last = pe.matmul(ps_o[DH * h:DH * h + DH, P * t:P * t + P], v[:, p, c, DH * h:DH * h + DH],
                                     probsT[:, n % 2, P * c:P * c + P], start=(c == 0), stop=(c == t))
                last.then_inc(pv_done, 1)

            def wait_w(i, p):
                wait(pe, (w_loaded0, w_loaded1)[p], 16 * (i // 2 + 1))

            def step(i, p, front, attend, out):
                a, o = i - 1, i - 2
                tokens = YT[:, TPB * (i // PAIRS):TPB * (i // PAIRS) + TPB, :] if isinstance(i, int) and front \
                    else YT[:, bass.ds(TPB * (i // PAIRS), TPB), :] if front else None
                for n in range(UNITS + 2):
                    if attend and n < UNITS:
                        if n == 0:
                            wait(pe, q_ready, a + 1)
                            wait(pe, k_ready, a + 1)
                            wait(pe, v_ready, a + 1)
                        scores(a, 1 - p, n)
                    if front and n == 0:
                        wait_w(i, p)
                        wait(pe, vT_ready, i)
                        pe.matmul(ps_proj[0][:, :], w_pair[:, p, 0, :], tokens, start=True,
                                  stop=True).then_inc(q_full, 1)
                    if front and n == 1:
                        wait(pe, v_ready, i)
                        pe.matmul(ps_proj[1][:, :], w_pair[:, p, 1, :], tokens, start=True,
                                  stop=True).then_inc(k_full, 1)
                    if out and n == 2:
                        wait(pe, (out_loaded0, out_loaded1)[p], 16 * (o // 2 + 1))
                        wait(pe, o_ready, o + 1)
                        wait(pe, x_added, o)
                        for t in range(TPB):
                            last = pe.matmul(ps_z[:, t, :], oT[:, P * t:P * t + P], w_out[:, p, :],
                                             start=True, stop=True)
                        last.then_inc(z_full, 1)
                    if front and n == 3:
                        wait(pe, q_ready, i + 1)
                        pe.matmul(ps_proj[0][:, :], w_pair[:, p, 2, :], tokens, start=True,
                                  stop=True).then_inc(vT_full, 1)
                    if front and n == 5:
                        wait(pe, vT_ready, i + 1)
                        wait(pe, k_ready, i + 1)
                        for j in range(TPB):
                            last = pe.transpose(ps_proj[1][:, P * j:P * j + P], vT[:, P * j:P * j + P], ident[:, :])
                        last.then_inc(v_full, 1)
                    if attend and 1 <= n <= UNITS:
                        turn(a, n - 1)
                    if attend and n >= 2:
                        weigh_values(a, 1 - p, n - 2)

            pe.wait_ge(made, 2)
            pe.wait_ge(q_zeroed, 2)
            run(step, pe)


HD_B = D // HEADS
MP_EPS = 1e-4


def block_diagonal(pool, tile_, size, done, inside, outside):
    n, k = tile_.shape[1], tile_.shape[2]
    pool.memset(tile_, inside).then_inc(done, 1)
    pool.wait_ge(done, 1)
    pool.affine_select(out=tile_, in_=tile_, compare_op=ALU.is_ge, fill=outside, base=0,
                       pattern=[[-size, n], [0, k]], channel_multiplier=1).then_inc(done, 1)
    pool.wait_ge(done, 2)
    pool.affine_select(out=tile_, in_=tile_, compare_op=ALU.is_ge, fill=outside, base=size - 1,
                       pattern=[[size, n], [0, k]], channel_multiplier=-1).then_inc(done, 1)


def channel_attention(nc, tag, X, Y, ident, dram):
    GROUPS = TPB * 2 * HEADS
    MIX = 0.5 / np.sqrt(0.5)
    with ExitStack() as ctx:
        new = Pool_(nc, ctx, tag)
        YT = new.sb("YT", [P, NT, P])
        wT = new.sb("wT", [P, 4, D])
        transpose_stream(nc, tag + "_turn", Y, YT, ident)
        normalized_weights(nc, tag + "_w", wT, ident, dram)
        block_mask = new.sb("block_mask", [P, HEADS, HD_B])
        yT = new.sb("yT", [P, S])
        sq = new.sb("sq", [P, GROUPS * HD_B])
        ss = new.sb("ss", [P, GROUPS])
        qk = new.sb("qk", [P, TPB, 2, D])
        vT = new.sb("vT", [P, S])
        logits = new.sb("logits", [P, D])
        neg_max = new.sb("neg_max", [P, 1])
        row_sum = new.sb("row_sum", [P, 1])
        probs = new.sb("probs", [P, D])
        probsT = new.sb("probsT", [P, D])
        oT = new.sb("oT", [P, S])
        ps_qk = new.ps("ps_qk", [P, TPB, 2, D])
        ps_v = new.ps("ps_v", [P, S])
        ps_g = new.ps("ps_g", [P, 512])
        ps_o = new.ps("ps_o", [P, S])
        ps_out = new.ps("ps_out", [P, TPB, D])
        made = new.sem("made")
        (y_copied, qkv_full, squared, summed, rooted, offset, inverted, qk_ready, v_ready, g_full, masked,
         max_ready, exp_ready, sum_inverted, p_ready, pT_full, pT_ready, o_full, o_ready, out_full, kept,
         x_added) = (new.sem(n) for n in (
             "y_copied", "qkv_full", "squared", "summed", "rooted", "offset", "inverted", "qk_ready", "v_ready",
             "g_full", "masked", "max_ready", "exp_ready", "sum_inverted", "p_ready", "pT_full", "pT_ready",
             "o_full", "o_ready", "out_full", "kept", "x_added"))
        block = ctx.enter_context(nc.Block())
        SCALE = float(1.0 / np.sqrt(np.float32(S)))

        @block.gpsimd
        def _(pool):
            block_diagonal(pool, block_mask[:, :, :], HD_B, made, 0.0, NEG)

        @block.vector
        def _(dve):
            dve.wait_ge(made, 3)
            with dve.Fori(0, B) as b:
                dve.tensor_copy(yT[:, :].rearrange("p (j t) -> p j t", t=P),
                                YT[:, bass.ds(TPB * b, TPB), :]).then_inc(y_copied, 1)
                dve.wait_ge(squared, b + 1)
                dve.tensor_reduce(ss[:, :], sq[:, :].rearrange("p (g e) -> p g e", e=HD_B), AX.X,
                                  ALU.add).then_inc(summed, 1)
                dve.wait_ge(rooted, b + 1)
                dve.tensor_scalar(ss[:, :], ss[:, :], float(1.0 / np.sqrt(HD_B)), MP_EPS, ALU.mult,
                                  ALU.add).then_inc(offset, 1)
                dve.wait_ge(offset, b + 1)
                dve.reciprocal(ss[:, :], ss[:, :]).then_inc(inverted, 1)
                dve.wait_ge(inverted, b + 1)
                for bank in range(2):
                    g = GROUPS // 2
                    dve.tensor_tensor(qk[:, 2 * bank:2 * bank + 2, :, :].rearrange("p j w (h e) -> p (j w h) e", e=HD_B),
                                      ps_qk[:, 2 * bank:2 * bank + 2, :, :].rearrange("p j w (h e) -> p (j w h) e", e=HD_B),
                                      ss[:, g * bank:g * bank + g].unsqueeze(2).to_broadcast([P, g, HD_B]),
                                      ALU.mult).then_inc(qk_ready, 1)
                dve.wait_ge(g_full, b + 1)
                dve.scalar_tensor_tensor(out=logits[:, :], in0=ps_g[:, 0:D], scalar=SCALE,
                                         in1=block_mask[:, :, :].rearrange("p n k -> p (n k)"), op0=ALU.mult,
                                         op1=ALU.add).then_inc(masked, 1)
                dve.wait_ge(masked, b + 1)
                dve.tensor_reduce(neg_max[:, :], logits[:, :], AX.X, ALU.max, negate=True).then_inc(max_ready, 1)
                dve.wait_ge(exp_ready, b + 1)
                dve.reciprocal(row_sum[:, :], row_sum[:, :]).then_inc(sum_inverted, 1)
                dve.wait_ge(sum_inverted, b + 1)
                dve.tensor_scalar(probs[:, :], probs[:, :], row_sum[:, 0:1], None, ALU.mult).then_inc(p_ready, 1)
                dve.wait_ge(pT_full, b + 1)
                dve.tensor_copy(probsT[:, :], ps_g[:, 0:D]).then_inc(pT_ready, 1)
                xs, ys = X[:, bass.ds(5 * b + 1, TPB), :], Y[:, bass.ds(5 * b + 1, TPB), :]
                dve.scalar_tensor_tensor(out=xs, in0=ys, scalar=MIX, in1=xs, op0=ALU.mult,
                                         op1=ALU.add).then_inc(kept, 1)
                dve.wait_ge(out_full, b + 1)
                dve.wait_ge(kept, b + 1)
                dve.scalar_tensor_tensor(out=xs, in0=ps_out[:, :, :], scalar=MIX, in1=xs, op0=ALU.mult,
                                         op1=ALU.add).then_inc(x_added, 1)

        @block.scalar
        def _(act):
            with act.Fori(0, B) as b:
                act.wait_ge(qkv_full, b + 1)
                for bank in range(2):
                    last = act.activation(sq[:, 512 * bank:512 * bank + 512],
                                          ps_qk[:, 2 * bank:2 * bank + 2, :, :].rearrange("p j w d -> p (j w d)"),
                                          ACT.Square)
                last.then_inc(squared, 1)
                act.wait_ge(summed, b + 1)
                act.activation(ss[:, :], ss[:, :], ACT.Sqrt).then_inc(rooted, 1)
                act.activation(vT[:, :], ps_v[:, :], ACT.Copy).then_inc(v_ready, 1)
                act.wait_ge(max_ready, b + 1)
                act.activation(probs[:, :], logits[:, :], ACT.Exp, bias=neg_max[:, 0:1],
                               accum_out=row_sum[:, 0:1]).then_inc(exp_ready, 1)
                act.wait_ge(o_full, b + 1)
                act.activation(oT[:, :], ps_o[:, :], ACT.Copy).then_inc(o_ready, 1)

        @block.tensor
        def _(pe):
            with pe.Fori(0, B) as b:
                pe.wait_ge(y_copied, b + 1)
                for j in range(TPB):
                    pe.matmul(ps_qk[:, j, :, :].rearrange("p w d -> p (w d)"), yT[:, P * j:P * j + P],
                              wT[:, 0:2, :].rearrange("p w d -> p (w d)"), start=True, stop=True)
                pe.matmul(ps_v[:, :], wT[:, 2, :], yT[:, :], start=True, stop=True).then_inc(qkv_full, 1)
                pe.wait_ge(qk_ready, 2 * b + 2)
                for j in range(TPB):
                    last = pe.matmul(ps_g[:, 0:D], qk[:, j, 0, :], qk[:, j, 1, :], start=(j == 0),
                                     stop=(j == TPB - 1))
                last.then_inc(g_full, 1)
                pe.wait_ge(p_ready, b + 1)
                pe.transpose(ps_g[:, 0:D], probs[:, :], ident[:, :]).then_inc(pT_full, 1)
                pe.wait_ge(pT_ready, b + 1)
                pe.wait_ge(v_ready, b + 1)
                pe.matmul(ps_o[:, :], probsT[:, :], vT[:, :], start=True, stop=True).then_inc(o_full, 1)
                pe.wait_ge(o_ready, b + 1)
                for j in range(TPB):
                    last = pe.matmul(ps_out[:, j, :], oT[:, P * j:P * j + P], wT[:, 3, :], start=True, stop=True)
                last.then_inc(out_full, 1)
                pe.wait_ge(x_added, b + 1)


def normalized_weights(nc, tag, wT, ident, dram):
    with ExitStack() as ctx:
        new = Pool_(nc, ctx, tag)
        w = new.sb("w", [P, 4, D])
        gain = new.sb("gain", [P, 1])
        sq = new.sb("sq", [P, 4, D])
        norm = new.sb("norm", [P, 4])
        ps_w = new.ps("ps_w", [P, 4, P])
        (loaded, squared, summed, rooted, chain, scaled, turned) = (new.sem(n) for n in (
            "loaded", "squared", "summed", "rooted", "chain", "scaled", "turned"))
        block = ctx.enter_context(nc.Block())

        @block.sync
        def _(sp):
            sp.dma_start(w[:, :, :], dram["b_w"].rearrange("n o e -> o n e")).then_inc(loaded, 16)
            sp.dma_start(gain[:, :], dram["b_gain"].partition_broadcast(P)).then_inc(loaded, 16)

        @block.scalar
        def _(act):
            act.wait_ge(summed, 1)
            act.activation(norm[:, :], norm[:, :], ACT.Sqrt).then_inc(rooted, 1)

        @block.vector
        def _(dve):
            dve.wait_ge(loaded, 32)
            dve.tensor_tensor(sq[:, :, :], w[:, :, :], w[:, :, :], ALU.mult).then_inc(squared, 1)
            dve.wait_ge(squared, 1)
            dve.tensor_reduce(norm[:, :], sq[:, :, :], AX.X, ALU.add).then_inc(summed, 1)
            dve.wait_ge(rooted, 1)
            dve.tensor_scalar(norm[:, :], norm[:, :], float(1.0 / np.sqrt(D)), MP_EPS, ALU.mult,
                              ALU.add).then_inc(chain, 1)
            dve.wait_ge(chain, 1)
            dve.reciprocal(norm[:, :], norm[:, :]).then_inc(chain, 1)
            dve.wait_ge(chain, 2)
            dve.tensor_scalar(norm[:, :], norm[:, :], gain[:, 0:1], float(1.0 / np.sqrt(D)), ALU.mult,
                              ALU.mult).then_inc(chain, 1)
            dve.wait_ge(chain, 3)
            for n in range(4):
                dve.tensor_scalar(w[:, n, :], w[:, n, :], norm[:, n:n + 1], None, ALU.mult).then_inc(scaled, 1)
            dve.wait_ge(turned, 1)
            dve.tensor_copy(wT[:, :, :], ps_w[:, :, :])

        @block.tensor
        def _(pe):
            pe.wait_ge(scaled, 4)
            for n in range(4):
                last = pe.transpose(ps_w[:, n, :], w[:, n, :], ident[:, :])
            last.then_inc(turned, 1)


HALF_WIN, WIN = 32, 64
BAND = P + 2 * HALF_WIN
GLOBALS = S // WIN
DH_W = D // HEADS


def window_attention(nc, tag, X, Y, ident, identb, dram):
    SPAN = S + 2 * HALF_WIN
    SCALE = float(DH_W) ** -0.5
    with ExitStack() as ctx:
        new = Pool_(nc, ctx, tag)
        YT = new.sb("YT", [P, NT, P])
        transpose_stream(nc, tag + "_turn", Y, YT, ident)
        padded = new.sb("padded", [P, B, SPAN])
        w_qkv = new.sb("w_qkv", [P, 3, D])
        w_out = new.sb("w_out", [P, D])
        bias = new.sb("bias", [P, D])
        head_mask = new.sb("head_mask", [P, HEADS, GLOBALS])
        mask = new.sb("mask", [P, 3, BAND], BF16)
        band = new.sb("band", [P, BAND])
        global_rep = new.sb("global_rep", [P, HEADS, GLOBALS])
        qT = new.sb("qT", [P, P])
        q_heads = new.sb("q_heads", [P, HEADS, P])
        kT = new.sb("kT", [P, BAND])
        vA = new.sb("vA", [P, D])
        vB = new.sb("vB", [WIN, D])
        kg = new.sb("kg", [P, HEADS, GLOBALS])
        vg = new.sb("vg", [P, HEADS, DH_W])
        neg_max = new.sb("neg_max", [P, 2, 2])
        row_sum = new.sb("row_sum", [P, HEADS])
        probs = new.sb("probs", [P, 2, 2, BAND])
        probsT = new.sb("probsT", [P, 2, 512])
        g_max = new.sb("g_max", [P, HEADS])
        g_sum = new.sb("g_sum", [P, HEADS])
        g_probs = new.sb("g_probs", [P, HEADS, GLOBALS])
        g_probsT = new.sb("g_probsT", [P, P])
        o_local = new.sb("o_local", [P, HEADS, DH_W])
        o_global = new.sb("o_global", [P, HEADS, DH_W])
        oT = new.sb("oT", [P, P])
        ps_s = [new.ps(f"ps_s{n}", [P, 512]) for n in range(2)]
        ps_pT = [new.ps(f"ps_pT{n}", [P, 512]) for n in range(2)]
        ps_o = new.ps("ps_o", [P, 512])
        ps_a = new.ps("ps_a", [P, 512])
        ps_b = new.ps("ps_b", [P, 512])
        ps_c = new.ps("ps_c", [P, 512])
        (loaded, made, padding, filled, zeroed) = (new.sem(n) for n in (
            "loaded", "made", "padding", "filled", "zeroed"))
        (band_ready, q_full, kv_full, vg_full, kv_ready, q_ready, heads_ready, vg_ready, kg_ready, lg_full, g_chain, g_max_ready,
         g_shifted, g_exp_ready, gT_full, gT_ready, og_full) = (new.sem(n) for n in (
             "band_ready", "q_full", "kv_full", "vg_full", "kv_ready", "q_ready", "heads_ready", "vg_ready", "kg_ready",
             "lg_full", "g_chain", "g_max_ready", "g_shifted", "g_exp_ready", "gT_full", "gT_ready", "og_full"))
        (s_full, max_ready, exp_ready, pT_full, pT_ready, pv_done, inverted, local_ready, global_ready, summed, oT_full,
         oT_ready, out_full, x_added) = (new.sem(n) for n in (
             "s_full", "max_ready", "exp_ready", "pT_full", "pT_ready", "pv_done", "inverted", "local_ready",
             "global_ready", "summed", "oT_full", "oT_ready", "out_full", "x_added"))
        block = ctx.enter_context(nc.Block())

        @block.sync
        def _(sp):
            sp.dma_start(w_qkv[:, :, :].rearrange("p a d -> p (a d)"), dram["w_qkv"]).then_inc(loaded, 16)
            sp.dma_start(w_out[:, :], dram["w_out"]).then_inc(loaded, 16)
            sp.dma_start(bias[:, :], dram["w_bias"].partition_broadcast(P)).then_inc(loaded, 16)

        @block.gpsimd
        def _(pool):
            block_diagonal(pool, head_mask[:, :, :], DH_W, made, 1.0, 0.0)
            pool.memset(mask[:, :, :], 0.0).then_inc(filled, 1)
            pool.wait_ge(filled, 1)
            pool.affine_select(out=mask[:, :, :], in_=mask[:, :, :], compare_op=ALU.is_ge, fill=NEG, base=0,
                               pattern=[[0, 3], [1, BAND]], channel_multiplier=-1).then_inc(filled, 1)
            pool.wait_ge(filled, 2)
            pool.affine_select(out=mask[:, :, :], in_=mask[:, :, :], compare_op=ALU.is_ge, fill=NEG, base=WIN - 1,
                               pattern=[[0, 3], [-1, BAND]], channel_multiplier=1).then_inc(filled, 1)
            pool.wait_ge(filled, 3)
            pool.memset(mask[:, 0, 0:HALF_WIN], NEG).then_inc(filled, 1)
            pool.memset(mask[:, 2, BAND - HALF_WIN:BAND], NEG).then_inc(filled, 1)
            pool.wait_ge(made, 3)
            with pool.Fori(0, NT) as i:
                pool.wait_ge(q_ready, i + 1)
                pool.tensor_tensor(q_heads[:, :, :], qT[:, :].unsqueeze(1).to_broadcast([P, HEADS, P]),
                                   head_mask[:, :, 0:1].to_broadcast([P, HEADS, P]), ALU.mult).then_inc(heads_ready, 1)

        @block.vector
        def _(dve):
            dve.memset(padded[:, :, 0:HALF_WIN], 0.0).then_inc(padding, 1)
            dve.memset(padded[:, :, S + HALF_WIN:SPAN], 0.0).then_inc(padding, 1)
            for n in range(2):
                dve.memset(ps_pT[n][:, :], 0.0).then_inc(zeroed, 1)
            dve.tensor_copy(padded[:, :, HALF_WIN:S + HALF_WIN].rearrange("p b (j t) -> p b j t", t=P),
                            YT[:, :, :].rearrange("p (b j) t -> p b j t", b=B)).then_inc(padding, 1)
            dve.wait_ge(loaded, 48)
            dve.wait_ge(made, 3)
            dve.wait_ge(padding, 3)

            def pair(i, c):
                n = PAIRS * i + c
                dve.wait_ge(s_full, n + 1)
                dve.tensor_reduce(neg_max[:, c % 2, :], ps_s[c % 2][:, 0:2 * BAND].rearrange(
                    "p (h k) -> p h k", k=BAND), AX.X, ALU.max, negate=True).then_inc(max_ready, 1)

            def copy_pT(i, c):
                n = PAIRS * i + c
                dve.wait_ge(pT_full, n + 1)
                dve.tensor_copy(probsT[:, c % 2, :], ps_pT[c % 2][:, :]).then_inc(pT_ready, 1)

            with dve.Fori(0, NT) as i:
                b, j = i // TPB, i % TPB
                tile_ = (i // TPB) * (TPB + 1) + i % TPB + 1
                dve.tensor_copy(band[:, :], padded[:, b, bass.ds(P * j, BAND)])
                dve.tensor_copy(global_rep[:, :, :], padded[:, b, bass.ds(HALF_WIN, GLOBALS, WIN)].unsqueeze(1)
                                .to_broadcast([P, HEADS, GLOBALS])).then_inc(band_ready, 1)
                dve.wait_ge(kv_full, i + 1)
                dve.tensor_copy(kT[:, :], ps_b[:, 0:BAND])
                dve.tensor_copy(vA[:, :], ps_b[:, 192:320])
                dve.tensor_copy(vB[:, :], ps_b[0:WIN, 320:448]).then_inc(kv_ready, 1)
                dve.wait_ge(vg_full, i + 1)
                dve.tensor_tensor(vg[:, :, :], ps_c[:, 0:D].rearrange("p (n e) -> p n e", e=DH_W),
                                  head_mask[:, :, :], ALU.mult)
                dve.tensor_tensor(kg[:, :, :], ps_c[:, 128:136].unsqueeze(1).to_broadcast([P, HEADS, GLOBALS]),
                                  head_mask[:, :, :], ALU.mult).then_inc(kg_ready, 1)
                pair(i, 0)
                pair(i, 1)
                dve.wait_ge(lg_full, i + 1)
                lg = ps_a[:, 0:P].rearrange("p (n g) -> p n g", g=GLOBALS)
                dve.tensor_reduce(g_max[:, :], lg, AX.X, ALU.max, negate=True).then_inc(g_max_ready, 1)
                dve.wait_ge(g_max_ready, i + 1)
                dve.tensor_tensor(g_probs[:, :, :], lg, g_max[:, :].unsqueeze(2).to_broadcast(
                    [P, HEADS, GLOBALS]), ALU.add).then_inc(g_shifted, 1)
                copy_pT(i, 0)
                pair(i, 2)
                dve.wait_ge(g_exp_ready, i + 1)
                dve.tensor_reduce(g_sum[:, :], g_probs[:, :, :], AX.X, ALU.add).then_inc(g_chain, 1)
                for c in range(3, PAIRS):
                    copy_pT(i, c - 2)
                    pair(i, c)
                copy_pT(i, PAIRS - 2)
                copy_pT(i, PAIRS - 1)
                dve.wait_ge(gT_full, i + 1)
                dve.tensor_copy(g_probsT[:, :], ps_a[:, 128:256]).then_inc(gT_ready, 1)
                dve.reciprocal(row_sum[:, :], row_sum[:, :])
                dve.wait_ge(g_chain, 2 * i + 1)
                dve.reciprocal(g_sum[:, :], g_sum[:, :]).then_inc(g_chain, 1)
                dve.wait_ge(g_chain, 2 * i + 2)
                dve.wait_ge(pv_done, PAIRS * i + PAIRS)
                dve.tensor_tensor(o_local[:, :, :], ps_o[:, 0:D].rearrange("p (n e) -> p n e", e=DH_W),
                                  row_sum[:, :].unsqueeze(2).to_broadcast([P, HEADS, DH_W]),
                                  ALU.mult).then_inc(local_ready, 1)
                dve.wait_ge(og_full, i + 1)
                dve.tensor_tensor(o_global[:, :, :], ps_a[:, 256:384].rearrange("p (n e) -> p n e", e=DH_W),
                                  g_sum[:, :].unsqueeze(2).to_broadcast([P, HEADS, DH_W]),
                                  ALU.mult).then_inc(global_ready, 1)
                dve.wait_ge(global_ready, i + 1)
                dve.tensor_tensor(o_local[:, :, :], o_local[:, :, :], o_global[:, :, :],
                                  ALU.add).then_inc(summed, 1)
                dve.wait_ge(oT_full, i + 1)
                dve.tensor_copy(oT[:, :], ps_a[:, 384:512]).then_inc(oT_ready, 1)
                dve.tensor_tensor(X[:, tile_, :], X[:, tile_, :], bias[:, :], ALU.add).then_inc(inverted, 1)
                dve.wait_ge(out_full, i + 1)
                dve.wait_ge(inverted, i + 1)
                dve.tensor_tensor(X[:, tile_, :], X[:, tile_, :], ps_c[:, 256:384], ALU.add).then_inc(x_added, 1)

        @block.scalar
        def _(act):
            def exps(i, c):
                n = PAIRS * i + c
                act.wait_ge(max_ready, n + 1)
                if c >= 2:
                    act.wait_ge(pT_full, n - 1)
                for h in range(2):
                    act.activation(probs[:, c % 2, h, :], ps_s[c % 2][:, h * BAND:(h + 1) * BAND], ACT.Exp,
                                   bias=neg_max[:, c % 2, h:h + 1],
                                   accum_out=row_sum[:, 2 * c + h:2 * c + h + 1]).then_inc(exp_ready, 1)

            with act.Fori(0, NT) as i:
                act.wait_ge(q_full, i + 1)
                act.activation(qT[:, :], ps_a[:, 0:P], ACT.Copy, scale=SCALE).then_inc(q_ready, 1)
                exps(i, 0)
                exps(i, 1)
                act.wait_ge(g_shifted, i + 1)
                act.activation(g_probs[:, :, :], g_probs[:, :, :], ACT.Exp).then_inc(g_exp_ready, 1)
                for c in range(2, PAIRS):
                    exps(i, c)

        @block.tensor
        def _(pe):
            pe.wait_ge(loaded, 48)
            pe.wait_ge(filled, 5)
            pe.wait_ge(zeroed, 2)

            def scores(i, c):
                n = PAIRS * i + c
                if c >= 2:
                    pe.wait_ge(exp_ready, 2 * n - 2)
                dst = ps_s[c % 2][:, 0:2 * BAND]
                variant = (i % TPB + 1) // 2
                pe.matmul(dst, identb[:, :], mask[:, variant, :].unsqueeze(1).to_broadcast([P, 2, BAND]),
                          start=True, stop=False)
                for h in range(2):
                    last = pe.matmul(dst[:, h * BAND:(h + 1) * BAND], q_heads[:, 2 * c + h, :], kT[:, :],
                                     start=False, stop=(h == 1))
                last.then_inc(s_full, 1)

            def turn(i, c):
                n = PAIRS * i + c
                pe.wait_ge(exp_ready, 2 * n + 2)
                if c >= 2:
                    pe.wait_ge(pT_ready, n - 1)
                for h in range(2):
                    pe.transpose(ps_pT[c % 2][:, h * P:(h + 1) * P], probs[:, c % 2, h, 0:P], ident[:, :])
                for h in range(2):
                    last = pe.transpose(ps_pT[c % 2][0:WIN, (2 + h) * P:(3 + h) * P], probs[:, c % 2, h, P:BAND],
                                        ident[:, :])
                last.then_inc(pT_full, 1)

            def weigh_values(i, c):
                pe.wait_ge(pT_ready, PAIRS * i + c + 1)
                for h in range(2):
                    o = DH_W * (2 * c + h)
                    pe.matmul(ps_o[:, o:o + DH_W], probsT[:, c % 2, h * P:(h + 1) * P], vA[:, o:o + DH_W],
                              start=True, stop=False)
                    last = pe.matmul(ps_o[:, o:o + DH_W], probsT[0:WIN, c % 2, (2 + h) * P:(3 + h) * P],
                                     vB[:, o:o + DH_W], start=False, stop=True)
                last.then_inc(pv_done, 1)

            with pe.Fori(0, NT) as i:
                pe.wait_ge(band_ready, i + 1)
                pe.matmul(ps_a[:, 0:P], w_qkv[:, 0, :], band[:, HALF_WIN:HALF_WIN + P], start=True,
                          stop=True).then_inc(q_full, 1)
                pe.matmul(ps_b[:, 0:BAND], w_qkv[:, 1, :], band[:, :], start=True, stop=True)
                pe.matmul(ps_b[:, 192:320], band[:, 0:P], w_qkv[:, 2, :], start=True, stop=True)
                pe.matmul(ps_b[0:WIN, 320:448], band[:, P:BAND], w_qkv[:, 2, :], start=True,
                          stop=True).then_inc(kv_full, 1)
                pe.matmul(ps_c[:, 0:D], global_rep[:, :, :].rearrange("p n g -> p (n g)"), w_qkv[:, 2, :],
                          start=True, stop=True)
                pe.matmul(ps_c[:, 128:136], w_qkv[:, 1, :], global_rep[:, 0, :], start=True,
                          stop=True).then_inc(vg_full, 1)
                pe.wait_ge(heads_ready, i + 1)
                pe.wait_ge(kv_ready, i + 1)
                scores(i, 0)
                scores(i, 1)
                pe.wait_ge(q_ready, i + 1)
                pe.wait_ge(kg_ready, i + 1)
                pe.matmul(ps_a[:, 0:P], qT[:, :], kg[:, :, :].rearrange("p n g -> p (n g)"), start=True,
                          stop=True).then_inc(lg_full, 1)
                turn(i, 0)
                scores(i, 2)
                for c in range(3, PAIRS):
                    turn(i, c - 2)
                    scores(i, c)
                    weigh_values(i, c - 3)
                turn(i, PAIRS - 2)
                weigh_values(i, PAIRS - 3)
                turn(i, PAIRS - 1)
                weigh_values(i, PAIRS - 2)
                pe.wait_ge(g_exp_ready, i + 1)
                pe.transpose(ps_a[:, 128:256], g_probs[:, :, :].rearrange("p n g -> p (n g)"),
                             ident[:, :]).then_inc(gT_full, 1)
                weigh_values(i, PAIRS - 1)
                pe.wait_ge(gT_ready, i + 1)
                pe.matmul(ps_a[:, 256:384], g_probsT[:, :], vg[:, :, :].rearrange("p n e -> p (n e)"),
                          start=True, stop=True).then_inc(og_full, 1)
                pe.wait_ge(summed, i + 1)
                pe.transpose(ps_a[:, 384:512], o_local[:, :, :].rearrange("p n e -> p (n e)"),
                             ident[:, :]).then_inc(oT_full, 1)
                pe.wait_ge(oT_ready, i + 1)
                pe.matmul(ps_c[:, 256:384], oT[:, :], w_out[:, :], start=True, stop=True).then_inc(out_full, 1)
                pe.wait_ge(x_added, i + 1)


EXPERTS, EXPERT_FF, GROUPS, TOP_GROUPS, TOP_K = 16, 64, 4, 2, 4
PER_GROUP = EXPERTS // GROUPS
BLOCKS = EXPERTS + 2
WIDE = BLOCKS * EXPERT_FF
CHUNKS = 3
CHUNK = WIDE // CHUNKS
TURNS = CHUNK // P


def experts(nc, tag, X, Y, ident, dram):
    LAST = NT * CHUNKS
    with ExitStack() as ctx:
        new = Pool_(nc, ctx, tag)
        YT = new.sb("YT", [P, NT, P])
        transpose_stream(nc, tag + "_turn", Y, YT, ident)
        w_gate = new.sb("w_gate", [P, EXPERTS])
        w_g = new.sb("w_g", [P, WIDE])
        w_u = new.sb("w_u", [P, WIDE])
        w_d = new.sb("w_d", [P, CHUNKS * TURNS, D])
        scores = new.sb("scores", [P, NT, EXPERTS])
        pairs4 = new.sb("pairs4", [P, 6, NT * GROUPS])
        lower = new.sb("lower", [P, EXPERTS, EXPERTS])
        beats = new.sb("beats", [P, NT, EXPERTS, EXPERTS])
        ties = new.sb("ties", [P, NT, EXPERTS, EXPERTS])
        rank = new.sb("rank", [P, NT, EXPERTS])
        open_ = new.sb("open", [P, NT * GROUPS])
        allowed = new.sb("allowed", [P, NT, EXPERTS])
        total = new.sb("total", [P, NT])
        combine = new.sb("combine", [P, NT, BLOCKS])
        yT = new.sb("yT", [P, 2, P])
        silu = new.sb("silu", [P, 2, CHUNK])
        act_ = new.sb("act", [P, 2, CHUNK])
        actT = new.sb("actT", [P, 2, CHUNK])
        ps_g = [new.ps(f"ps_g{n}", [P, 512]) for n in range(2)]
        ps_u = [new.ps(f"ps_u{n}", [P, 512]) for n in range(2)]
        ps_t = [new.ps(f"ps_t{n}", [P, 512]) for n in range(2)]
        ps_out = new.ps("ps_out", [P, 512])
        ps_gate = new.ps("ps_gate", [P, NT * EXPERTS])
        (loaded, made, gate_full, scored, chain, combined, ones) = (new.sem(n) for n in (
            "loaded", "made", "gate_full", "scored", "chain", "combined", "ones"))
        (yT_ready, g_full, u_full, silu_ready, act_ready, weighted, t_full, t_ready, down_done,
         x_added) = (new.sem(n) for n in ("yT_ready", "g_full", "u_full", "silu_ready", "act_ready", "weighted",
                                          "t_full", "t_ready", "down_done", "x_added"))
        block = ctx.enter_context(nc.Block())

        def run(step, eng):
            step(0, True)
            with eng.Fori(1, NT // 2) as s:
                step(s, False)

        @block.sync
        def _(sp):
            sp.dma_start(w_gate[:, :], dram["m_gate"]).then_inc(loaded, 16)
            sp.dma_start(w_g[:, :], dram["m_g"]).then_inc(loaded, 16)
            sp.dma_start(w_u[:, :], dram["m_u"]).then_inc(loaded, 16)
            sp.dma_start(w_d[:, :, :], dram["m_d"].rearrange("(c p) d -> p c d", p=P)).then_inc(loaded, 16)

        @block.gpsimd
        def _(pool):
            pool.memset(lower[:, :, :], 1.0).then_inc(made, 1)
            pool.wait_ge(made, 1)
            pool.affine_select(out=lower[:, :, :], in_=lower[:, :, :], compare_op=ALU.is_gt, fill=0.0, base=0,
                               pattern=[[1, EXPERTS], [-1, EXPERTS]], channel_multiplier=0).then_inc(made, 1)
            pool.memset(combine[:, :, EXPERTS:BLOCKS], 1.0).then_inc(made, 1)
            pool.wait_ge(made, 3)
            pool.wait_ge(combined, 1)

            def step(s, first):
                for k in range(2 * CHUNKS):
                    n = 2 * CHUNKS * s + k
                    i, c, b = 2 * s + k // CHUNKS, k % CHUNKS, k % 2
                    wait(pool, act_ready, n + 1)
                    view = act_[:, b, :].rearrange("p (e f) -> p e f", f=EXPERT_FF)
                    e = CHUNK // EXPERT_FF
                    pool.tensor_tensor(view, view, combine[:, i, e * c:e * c + e].unsqueeze(2).to_broadcast(
                        [P, e, EXPERT_FF]), ALU.mult).then_inc(weighted, 1)

            run(step, pool)

        @block.vector
        def _(dve):
            links = [0]

            def link(ins):
                links[0] += 1
                ins.then_inc(chain, 1)
                dve.wait_ge(chain, links[0])

            dve.wait_ge(scored, 1)
            dve.wait_ge(made, 3)
            a, b_, c_, d_ = (scores[:, :, :].rearrange("p t (g k) -> p (t g) k", k=PER_GROUP)[:, :, k]
                             for k in range(PER_GROUP))
            dve.tensor_tensor(pairs4[:, 0, :], a, b_, ALU.max)
            dve.tensor_tensor(pairs4[:, 1, :], a, b_, ALU.min)
            dve.tensor_tensor(pairs4[:, 2, :], c_, d_, ALU.max)
            link(dve.tensor_tensor(pairs4[:, 3, :], c_, d_, ALU.min))
            dve.tensor_tensor(pairs4[:, 4, :], pairs4[:, 0, :], pairs4[:, 2, :], ALU.max)
            link(dve.tensor_tensor(pairs4[:, 5, :], pairs4[:, 0, :], pairs4[:, 2, :], ALU.min))
            link(dve.tensor_tensor(pairs4[:, 1, :], pairs4[:, 1, :], pairs4[:, 3, :], ALU.max))
            link(dve.tensor_tensor(pairs4[:, 5, :], pairs4[:, 5, :], pairs4[:, 1, :], ALU.max))
            link(dve.tensor_tensor(pairs4[:, 4, :], pairs4[:, 4, :], pairs4[:, 5, :], ALU.add))

            def ranks(values, n, out):
                own = values.unsqueeze(3).to_broadcast([P, NT, n, n])
                rival = values.unsqueeze(2).to_broadcast([P, NT, n, n])
                dve.tensor_tensor(beats[:, :, 0:n, 0:n], rival, own, ALU.is_gt)
                link(dve.tensor_tensor(ties[:, :, 0:n, 0:n], rival, own, ALU.is_equal))
                link(dve.tensor_tensor(ties[:, :, 0:n, 0:n], ties[:, :, 0:n, 0:n],
                                       lower[:, 0:n, 0:n].unsqueeze(1).to_broadcast([P, NT, n, n]), ALU.mult))
                link(dve.tensor_tensor(beats[:, :, 0:n, 0:n], beats[:, :, 0:n, 0:n], ties[:, :, 0:n, 0:n], ALU.add))
                link(dve.tensor_reduce(out, beats[:, :, 0:n, 0:n], AX.X, ALU.add))

            ranks(pairs4[:, 4, :].rearrange("p (t g) -> p t g", g=GROUPS), GROUPS,
                  open_[:, :].rearrange("p (t g) -> p t g", g=GROUPS))
            link(dve.tensor_scalar(open_[:, :], open_[:, :], float(TOP_GROUPS), None, ALU.is_lt))
            flat = "p t (g k) -> p (t g) k"
            wide = open_[:, :].unsqueeze(2).to_broadcast([P, NT * GROUPS, PER_GROUP])
            link(dve.tensor_tensor(allowed[:, :, :].rearrange(flat, k=PER_GROUP),
                                   scores[:, :, :].rearrange(flat, k=PER_GROUP), wide, ALU.mult))
            link(dve.tensor_tensor(allowed[:, :, :].rearrange(flat, k=PER_GROUP),
                                   allowed[:, :, :].rearrange(flat, k=PER_GROUP), wide, ALU.add))
            ranks(allowed[:, :, :], EXPERTS, rank[:, :, :])
            link(dve.tensor_scalar(rank[:, :, :], rank[:, :, :], float(TOP_K), None, ALU.is_lt))
            link(dve.tensor_tensor(rank[:, :, :], rank[:, :, :], scores[:, :, :], ALU.mult))
            link(dve.tensor_reduce(total[:, :], rank[:, :, :], AX.X, ALU.add))
            link(dve.tensor_scalar(total[:, :], total[:, :], 1e-6, None, ALU.add))
            link(dve.reciprocal(total[:, :], total[:, :]))
            dve.tensor_tensor(combine[:, :, 0:EXPERTS], rank[:, :, :],
                              total[:, :].unsqueeze(2).to_broadcast([P, NT, EXPERTS]), ALU.mult).then_inc(combined, 1)

            def turned(n, b):
                wait(dve, t_full, n + 1)
                wait(dve, down_done, n - 1)
                dve.tensor_copy(actT[:, b, :], ps_t[b][:, 0:CHUNK]).then_inc(t_ready, 1)

            def add(i, tile_):
                wait(dve, down_done, CHUNKS * i + CHUNKS)
                dve.tensor_tensor(X[:, tile_, :], X[:, tile_, :], ps_out[:, 0:D], ALU.add).then_inc(x_added, 1)

            def tile_of(i):
                return (i // TPB) * (TPB + 1) + i % TPB + 1

            def step(s, first):
                for k in range(2 * CHUNKS):
                    n, b = 2 * CHUNKS * s + k, k % 2
                    wait(dve, u_full, n + 1)
                    wait(dve, silu_ready, n + 1)
                    wait(dve, t_full, n - 1)
                    dve.tensor_tensor(act_[:, b, :], silu[:, b, :], ps_u[b][:, 0:CHUNK], ALU.mult).then_inc(act_ready, 1)
                    if not (first and k == 0):
                        turned(n - 1, 1 - b)
                    if k == 2 and not first:
                        add(2 * s - 1, tile_of(2 * s - 1))
                    if k == 5:
                        add(2 * s, tile_of(2 * s))

            run(step, dve)
            turned(LAST - 1, 1)
            add(NT - 1, tile_of(NT - 1))

        @block.scalar
        def _(act):
            act.wait_ge(gate_full, 1)
            act.activation(scores[:, :, :].rearrange("p t e -> p (t e)"), ps_gate[:, :], ACT.Sigmoid).then_inc(scored, 1)

            def step(s, first):
                for k in range(2 * CHUNKS):
                    n, b = 2 * CHUNKS * s + k, k % 2
                    if k % CHUNKS == 0:
                        i, p = 2 * s + k // CHUNKS, k // CHUNKS
                        wait(act, u_full, CHUNKS * (i - 1))
                        act.activation(yT[:, p, :], YT[:, i, :], ACT.Copy).then_inc(yT_ready, 1)
                    wait(act, g_full, n + 1)
                    wait(act, act_ready, n - 1)
                    act.activation(silu[:, b, :], ps_g[b][:, 0:CHUNK], ACT.Silu).then_inc(silu_ready, 1)

            run(step, act)

        @block.tensor
        def _(pe):
            pe.wait_ge(loaded, 64)
            for i in range(NT):
                last = pe.matmul(ps_gate[:, EXPERTS * i:EXPERTS * i + EXPERTS], YT[:, i, :], w_gate[:, :],
                                 start=True, stop=True)
            last.then_inc(gate_full, 1)

            def turn(n, b):
                wait(pe, weighted, n + 1)
                wait(pe, t_ready, n - 1)
                for k in range(TURNS):
                    last = pe.transpose(ps_t[b][:, P * k:P * k + P], act_[:, b, P * k:P * k + P], ident[:, :])
                last.then_inc(t_full, 1)

            def down(n, c, i, b):
                wait(pe, t_ready, n + 1)
                if c == 0:
                    wait(pe, x_added, i)
                for k in range(TURNS):
                    last = pe.matmul(ps_out[:, 0:D], actT[:, b, P * k:P * k + P], w_d[:, TURNS * c + k, :],
                                     start=(c == 0 and k == 0), stop=(c == CHUNKS - 1 and k == TURNS - 1))
                last.then_inc(down_done, 1)

            def step(s, first):
                for k in range(2 * CHUNKS):
                    n, b = 2 * CHUNKS * s + k, k % 2
                    i, p, c = 2 * s + k // CHUNKS, k // CHUNKS, k % CHUNKS
                    wait(pe, yT_ready, i + 1)
                    wait(pe, silu_ready, n - 1)
                    pe.matmul(ps_g[b][:, 0:CHUNK], yT[:, p, :], w_g[:, CHUNK * c:CHUNK * c + CHUNK],
                              start=True, stop=True).then_inc(g_full, 1)
                    wait(pe, act_ready, n - 1)
                    pe.matmul(ps_u[b][:, 0:CHUNK], yT[:, p, :], w_u[:, CHUNK * c:CHUNK * c + CHUNK],
                              start=True, stop=True).then_inc(u_full, 1)
                    if not (first and k == 0):
                        turn(n - 1, 1 - b)
                    if not (first and k <= 1):
                        m = k - 2
                        down(n - 2, m % CHUNKS, 2 * s + m // CHUNKS, b)

            run(step, pe)
            turn(LAST - 1, 1)
            down(LAST - 2, 1, NT - 1, 0)
            down(LAST - 1, 2, NT - 1, 1)


def time_attention(nc, tag, X, Y, ident, dram):
    T = B
    with ExitStack() as ctx:
        new = Pool_(nc, ctx, tag)
        YT = new.sb("YT", [P, NT, P])
        transpose_stream(nc, tag + "_turn", Y, YT, ident)
        w = new.sb("w", [P, D])
        proj = new.sb("proj", [P, D])
        w_cat = new.sb("w_cat", [P, 2, D])
        bias = new.sb("bias", [P, D])
        yT = new.sb("yT", [P, T, P])
        hp = new.sb("hp", [P, T - 1, D])
        score = new.sb("score", [P, T - 1])
        neg_max = new.sb("neg_max", [P, 2])
        prob = new.sb("prob", [P, 2, T - 1])
        total = new.sb("total", [P, 2])
        context = new.sb("context", [P, 2, D])
        contextT = new.sb("contextT", [P, 2, P])
        res = new.sb("res", [P, 2, D])
        ps_h = new.ps("ps_h", [P, T - 1, D])
        ps_c = new.ps("ps_c", [P, 2, P])
        ps_out = new.ps("ps_out", [P, 2, D])
        (loaded, y_copied, h_full, tanh_ready, chain, max_ready, exp_ready, c_ready, cT_full, cT_ready, out_full,
         biased, out_ready, done) = (new.sem(n) for n in (
             "loaded", "y_copied", "h_full", "tanh_ready", "chain", "max_ready", "exp_ready", "c_ready", "cT_full",
             "cT_ready", "out_full", "biased", "out_ready", "done"))
        block = ctx.enter_context(nc.Block())
        CHAIN = 11

        @block.sync
        def _(sp):
            sp.dma_start(w[:, :], dram["t_w"]).then_inc(loaded, 16)
            sp.dma_start(proj[:, :], dram["t_proj"].partition_broadcast(P)).then_inc(loaded, 16)
            sp.dma_start(w_cat[:, :, :], dram["t_cat"].rearrange("(a p) h -> p a h", p=P)).then_inc(loaded, 16)
            sp.dma_start(bias[:, :], dram["t_bias"].partition_broadcast(P)).then_inc(loaded, 16)

        @block.vector
        def _(dve):
            dve.wait_ge(loaded, 64)
            with dve.Fori(0, TPB) as j:
                links = [0]

                def link(ins):
                    links[0] += 1
                    ins.then_inc(chain, 1)
                    dve.wait_ge(chain, CHAIN * j + links[0])

                dve.tensor_copy(yT[:, :, :], YT[:, bass.ds(j, T, TPB), :]).then_inc(y_copied, 1)
                dve.wait_ge(tanh_ready, j + 1)
                link(dve.tensor_tensor(hp[:, :, :], hp[:, :, :],
                                       proj[:, :].unsqueeze(1).to_broadcast([P, T - 1, D]), ALU.mult))
                link(dve.tensor_reduce(score[:, :], hp[:, :, :], AX.X, ALU.add))
                dve.tensor_reduce(neg_max[:, 0:1], score[:, 0:2], AX.X, ALU.max, negate=True)
                dve.tensor_reduce(neg_max[:, 1:2], score[:, 0:3], AX.X, ALU.max, negate=True).then_inc(max_ready, 1)
                dve.wait_ge(exp_ready, j + 1)
                link(dve.reciprocal(total[:, :], total[:, :]))
                link(dve.tensor_tensor(prob[:, :, :], prob[:, :, :],
                                       total[:, :].unsqueeze(2).to_broadcast([P, 2, T - 1]), ALU.mult))
                link(dve.tensor_scalar(context[:, 0, :], Y[:, 1 + j, :], prob[:, 0, 0:1], None, ALU.mult))
                link(dve.tensor_scalar(context[:, 1, :], Y[:, 1 + j, :], prob[:, 1, 0:1], None, ALU.mult))
                link(dve.scalar_tensor_tensor(out=context[:, 0, :], in0=Y[:, 6 + j, :], scalar=prob[:, 0, 1:2],
                                              in1=context[:, 0, :], op0=ALU.mult, op1=ALU.add))
                link(dve.scalar_tensor_tensor(out=context[:, 1, :], in0=Y[:, 6 + j, :], scalar=prob[:, 1, 1:2],
                                              in1=context[:, 1, :], op0=ALU.mult, op1=ALU.add))
                link(dve.scalar_tensor_tensor(out=context[:, 1, :], in0=Y[:, 11 + j, :], scalar=prob[:, 1, 2:3],
                                              in1=context[:, 1, :], op0=ALU.mult, op1=ALU.add))
                dve.tensor_tensor(X[:, 1 + j, :], X[:, 1 + j, :], Y[:, 1 + j, :], ALU.add)
                link(dve.tensor_tensor(X[:, 6 + j, :], X[:, 6 + j, :], Y[:, 6 + j, :], ALU.add))
                dve.wait_ge(cT_full, j + 1)
                dve.tensor_copy(contextT[:, :, :], ps_c[:, :, :]).then_inc(cT_ready, 1)
                dve.wait_ge(out_full, j + 1)
                dve.tensor_tensor(res[:, :, :], ps_out[:, :, :], bias[:, :].unsqueeze(1).to_broadcast([P, 2, D]),
                                  ALU.add).then_inc(biased, 1)
                dve.wait_ge(out_ready, j + 1)
                dve.tensor_tensor(X[:, 11 + j, :], X[:, 11 + j, :], res[:, 0, :], ALU.add)
                link(dve.tensor_tensor(X[:, 16 + j, :], X[:, 16 + j, :], res[:, 1, :], ALU.add))
                assert links[0] == CHAIN

        @block.scalar
        def _(act):
            with act.Fori(0, TPB) as j:
                act.wait_ge(h_full, j + 1)
                act.activation(hp[:, :, :], ps_h[:, :, :], ACT.Tanh).then_inc(tanh_ready, 1)
                act.wait_ge(max_ready, j + 1)
                act.activation(prob[:, 0, 0:2], score[:, 0:2], ACT.Exp, bias=neg_max[:, 0:1],
                               accum_out=total[:, 0:1])
                act.activation(prob[:, 0, 2:3], score[:, 2:3], ACT.Copy, scale=0.0)
                act.activation(prob[:, 1, :], score[:, :], ACT.Exp, bias=neg_max[:, 1:2],
                               accum_out=total[:, 1:2]).then_inc(exp_ready, 1)
                act.wait_ge(biased, j + 1)
                act.activation(res[:, :, :], res[:, :, :], ACT.Tanh).then_inc(out_ready, 1)

        @block.tensor
        def _(pe):
            pe.wait_ge(loaded, 64)
            with pe.Fori(0, TPB) as j:
                pe.wait_ge(y_copied, j + 1)
                for t in range(T - 1):
                    last = pe.matmul(ps_h[:, t, :], yT[:, t, :], w[:, :], start=True, stop=True)
                last.then_inc(h_full, 1)
                pe.wait_ge(chain, CHAIN * j + 9)
                for n in range(2):
                    last = pe.transpose(ps_c[:, n, :], context[:, n, :], ident[:, :])
                last.then_inc(cT_full, 1)
                pe.wait_ge(cT_ready, j + 1)
                for n in range(2):
                    pe.matmul(ps_out[:, n, :], yT[:, 2 + n, :], w_cat[:, 0, :], start=True, stop=False)
                    last = pe.matmul(ps_out[:, n, :], contextT[:, n, :], w_cat[:, 1, :], start=False, stop=True)
                last.then_inc(out_full, 1)


def load_stream(nc, x, X, ident, identb):
    with ExitStack() as ctx:
        new = Pool_(nc, ctx, "load")
        loaded, made = new.sem("loaded"), new.sem("made")
        block = ctx.enter_context(nc.Block())

        @block.sync
        def _(sp):
            for b in range(B):
                sp.dma_start(X[:, 5 * b + 1:5 * b + 5, :],
                             x[b].rearrange("(j p) d -> p j d", p=P)).then_inc(loaded, 16)
            sp.wait_ge(loaded, 16 * B)

        @block.gpsimd
        def _(pool):
            pool.memset(ident[:, :], 0.0).then_inc(made, 1)
            pool.wait_ge(made, 1)
            pool.affine_select(out=ident[:, :], in_=ident[:, :], compare_op=ALU.not_equal, fill=1.0, base=0,
                               pattern=[[-1, P]], channel_multiplier=1).then_inc(made, 1)
            pool.wait_ge(made, 2)
            pool.tensor_copy(identb[:, :], ident[:, :])

        @block.vector
        def _(dve):
            for b in range(B):
                dve.memset(X[:, 5 * b, :], 0.0)


def store_stream(nc, X, out):
    with ExitStack() as ctx:
        stored = Pool_(nc, ctx, "store").sem("stored")
        block = ctx.enter_context(nc.Block())

        @block.sync
        def _(sp):
            for b in range(B):
                sp.dma_start(out[b].rearrange("(j p) d -> p j d", p=P),
                             X[:, 5 * b + 1:5 * b + 5, :]).then_inc(stored, 16)
            sp.wait_ge(stored, 16 * B)


STAGES = ["attn_a", "ffn0", "attn_b", "ffn1", "window", "moe0", "attn_t", "moe1"]


def lay_out_others(a, np):
    laid = {}
    q, k, v = (np.transpose(a[f"L0_attn_a_{n}"], (1, 2, 0)).reshape(D, PAIRS, 1, P) for n in "QKV")
    laid["a_qkv"] = np.transpose(np.concatenate([q, k, v], 2), (1, 0, 2, 3))
    laid["a_out"] = np.transpose(a["L0_attn_a_W"], (2, 1, 0)).reshape(PAIRS, P, D)
    laid["b_w"] = np.stack([a[f"L0_attn_b_w_{n}"] for n in "qkvo"], 0)
    laid["b_gain"] = a["L0_attn_b_gain"].reshape(1)
    laid["w_qkv"] = a["L1_attn_a_w_qkv"]
    laid["w_out"] = a["L1_attn_a_w_out"]
    laid["w_bias"] = a["L1_attn_a_b_out"]
    laid["m_gate"] = a["L1_ffn_w_gate"].T
    for n, name in (("g", "w1"), ("u", "w3")):
        routed = a[f"L1_ffn_{name}_e"].reshape(EXPERTS * EXPERT_FF, D)
        laid[f"m_{n}"] = np.concatenate([routed, a[f"L1_ffn_{name}_s"]], 0).T
    routed = np.transpose(a["L1_ffn_w2_e"], (0, 2, 1)).reshape(EXPERTS * EXPERT_FF, D)
    laid["m_d"] = np.concatenate([routed, a["L1_ffn_w2_s"].T], 0)
    laid["t_w"] = a["L1_attn_b_W"]
    laid["t_proj"] = a["L1_attn_b_proj"]
    laid["t_cat"] = a["L1_attn_b_concat_w"].T
    laid["t_bias"] = a["L1_attn_b_concat_b"]
    return laid


def build(nc, dram, out):
    with ExitStack() as ctx:
        new = Pool_(nc, ctx, "all")
        X = new.sb("X", [P, B * (TPB + 1), D])
        Y = new.sb("Y", [P, B * (TPB + 1), D])
        ident = new.sb("ident", [P, P])
        identb = new.sb("identb", [P, P], BF16)
        load_stream(nc, dram["x"], X, ident, identb)
        with ExitStack() as zero_ctx:
            block = zero_ctx.enter_context(nc.Block())

            @block.gpsimd
            def _(pool):
                for b in range(B):
                    pool.memset(Y[:, 5 * b, :], 0.0)
        for stage in STAGES:
            clear_semaphores(nc)
            layernorm(nc, stage + "_norm", X, Y)
            if stage == "attn_a":
                causal_attention(nc, stage, X, Y, ident, identb, dram)
            elif stage.startswith("ffn"):
                with ExitStack() as stack_ctx:
                    X1 = Pool_(nc, stack_ctx, stage).sb("X1", [P, B * (TPB + 1), D])
                    zero_tiles(nc, X1)
                    ffn_stack(nc, stage, X1, Y, ident, identb, dram)
                add_stream(nc, stage + "_add", X, Y)
            elif stage == "attn_b":
                channel_attention(nc, stage, X, Y, ident, dram)
            elif stage == "window":
                window_attention(nc, stage, X, Y, ident, identb, dram)
            elif stage.startswith("moe"):
                experts(nc, stage, X, Y, ident, dram)
            elif stage == "attn_t":
                time_attention(nc, stage, X, Y, ident, dram)
        store_stream(nc, X, out)


def clear_semaphores(nc):
    ids = sorted(nc.free_semaphores)
    assert ids == list(range(ids[0], ids[-1] + 1))
    with ExitStack() as ctx:
        block = ctx.enter_context(nc.Block())

        @block.gpsimd
        def _(pool):
            pool.sem_clear(range(ids[0], ids[-1] + 1))


def zero_tiles(nc, T):
    with ExitStack() as ctx:
        block = ctx.enter_context(nc.Block())

        @block.vector
        def _(dve):
            for b in range(B):
                dve.memset(T[:, 5 * b, :], 0.0)


def kernel(**inputs):
    import numpy as _np
    import concourse.bacc as _bacc
    from concourse import mybir as _mybir
    from concourse.bass_utils import run_bass_kernel_spmd as _run

    a = {n: _np.asarray(v) for n, v in inputs.items()}
    half = 32

    def swapped(s):
        return _np.concatenate([s[:, half:], s[:, :half]], 1)

    qs, ks = a["L0_ffn_q_scale"], a["L0_ffn_k_scale"]
    laid = {
        "x": a["L0_attn_a_x"],
        "rotary": rotary_base(),
        "qk_scales": _np.stack([qs, swapped(qs), ks, swapped(ks)], 1).reshape(-1),
        "Wqkv": a["L0_ffn_Wqkv"], "Wo": a["L0_ffn_Wo"], "W1": a["L0_ffn_W1"], "W2": a["L0_ffn_W2"],
        "b1": a["L0_ffn_b1"], "b2": a["L0_ffn_b2"],
        "ln_gb": _np.stack([a["L0_ffn_ln_g"].T, a["L0_ffn_ln_b"].T], -1),
    }
    laid.update(lay_out_others(a, _np))
    nc = _bacc.Bacc("TRN2", target_bir_lowering=False, num_devices=1)
    arrays, dram = {}, {}
    for name, v in laid.items():
        v = _np.ascontiguousarray(v)
        arrays[f"in_{name}"] = v
        dram[name] = nc.dram_tensor(f"in_{name}", v.shape, _mybir.dt.from_np(v.dtype), kind="ExternalInput").ap()
    out = nc.dram_tensor("out", (B, S, D), _mybir.dt.float32, kind="ExternalOutput").ap()
    build(nc, dram, out)
    r = _run(nc, [arrays], core_ids=[0])
    return r.results[0]["out"]
```
